# Optimizing a Trainium2 kernel written in Bass

```python
import numpy as np
import jax
import jax.numpy as jnp

def _softmax(x, axis=-1):
    return jax.nn.softmax(x, axis=axis)

def _gelu(x):
    return jax.nn.gelu(x, approximate=True)

def _silu(x):
    return jax.nn.silu(x)

def _sigmoid(x):
    return jax.nn.sigmoid(x)

def _layernorm(x, axis=-1, eps=1e-05):
    m = jnp.mean(x, axis=axis, keepdims=True)
    v = jnp.var(x, axis=axis, keepdims=True)
    return (x - m) / jnp.sqrt(v + eps)

def _scatter_add(tgt, idx, src, axis=0):
    return tgt.at[idx].add(src)

def _segment_sum(src, seg, n):
    return jax.ops.segment_sum(src, seg, n)
kernel_name = 'mk_gnn_resnorm_d2_gnn_r8_a703b8'

def setup_inputs(seed: int=0):
    np.random.seed(seed)
    _w = jnp.asarray

    def _rec_inputs():
        import jax
        import jax.numpy as jnp
        _gk = jax.random.key(seed)
        x = -1.686e-05 + 1 * jax.random.normal(jax.random.fold_in(_gk, 1), (6250, 160), jnp.float32)
        src = jax.random.randint(jax.random.fold_in(_gk, 2), (200000,), 0, 6250, jnp.int32)
        dst = jax.random.randint(jax.random.fold_in(_gk, 3), (200000,), 0, 6250, jnp.int32)
        _o = jnp.argsort(dst, stable=True)
        src = src[_o]
        dst = dst[_o]
        edge_attr_16 = -0.000191324 + 0.999809 * jax.random.normal(jax.random.fold_in(_gk, 12), (200000, 16), jnp.float32)
        edge_attr_32 = 0.000196303 + 1.00016 * jax.random.normal(jax.random.fold_in(_gk, 13), (200000, 32), jnp.float32)
        edge_attr_4 = 0.000126197 + 0.999763 * jax.random.normal(jax.random.fold_in(_gk, 14), (200000, 4), jnp.float32)
        node_vec1 = -0.00915711 + 0.999674 * jax.random.normal(jax.random.fold_in(_gk, 16), (6250, 1), jnp.float32)
        return (x, src, dst, edge_attr_16, edge_attr_32, edge_attr_4, node_vec1)
    x, src, dst, edge_attr_16, edge_attr_32, edge_attr_4, node_vec1 = _rec_inputs()

    def _L0_gnn_setup():
        import jax, jax.numpy as jnp
        import numpy as np
        MUL0_N, MUL1_N = (64, 32)
        MUL0_E, MUL1_E = (8, 8)
        MUL0_H, MUL1_H = (64, 32)
        N_NODES, N_EDGES = (6250, 100000)
        D_NODE = MUL0_N + 3 * MUL1_N
        D_EDGE = MUL0_E + 3 * MUL1_E
        D_HID = MUL0_H + 3 * MUL1_H

        def _split(x, mul0, mul1):
            s = x[..., :mul0]
            v = x[..., mul0:].reshape(x.shape[0], mul1, 3)
            return (s, v)

        def fctp_messages(x, e, W1, W2, W3, W4):
            xs, xv = _split(x, MUL0_N, MUL1_N)
            es, ev = _split(e, MUL0_E, MUL1_E)
            inv_sqrt2 = 1.0 / np.sqrt(2.0)
            s1 = jnp.einsum('ea,eb,abc->ec', xs, es, W1) * (1.0 / np.sqrt(MUL0_N * MUL0_E))
            s2 = jnp.einsum('eai,ebi,abc->ec', xv, ev, W2) * (1.0 / (np.sqrt(3.0) * np.sqrt(MUL1_N * MUL1_E)))
            out_s = (s1 + s2) * inv_sqrt2
            v1 = jnp.einsum('ea,ebi,abc->eci', xs, ev, W3) * (1.0 / np.sqrt(MUL0_N * MUL1_E))
            v2 = jnp.einsum('eai,eb,abc->eci', xv, es, W4) * (1.0 / np.sqrt(MUL1_N * MUL0_E))
            out_v = (v1 + v2) * inv_sqrt2
            return jnp.concatenate([out_s, out_v.reshape(out_v.shape[0], -1)], axis=-1)
        key = jax.random.key(seed)
        ks = jax.random.split(key, 12)
        node_features = jax.random.normal(ks[0], (N_NODES, D_NODE), dtype=jnp.float32)
        edge_index = jax.random.randint(ks[1], (2, N_EDGES), 0, N_NODES, dtype=jnp.int64)
        edge_attr_tensor = jax.random.normal(ks[2], (N_EDGES, D_EDGE), dtype=jnp.float32)
        node_attr_scalar_raw = jax.random.normal(ks[3], (N_NODES, 1), dtype=jnp.float32)
        W1 = jax.random.normal(ks[4], (MUL0_N, MUL0_E, MUL0_H), dtype=jnp.float32)
        W2 = jax.random.normal(ks[5], (MUL1_N, MUL1_E, MUL0_H), dtype=jnp.float32)
        W3 = jax.random.normal(ks[6], (MUL0_N, MUL1_E, MUL1_H), dtype=jnp.float32)
        W4 = jax.random.normal(ks[7], (MUL1_N, MUL0_E, MUL1_H), dtype=jnp.float32)
        Wm = jax.random.normal(ks[8], (D_HID, D_HID), dtype=jnp.float32) / np.sqrt(D_HID)
        bm = jnp.zeros((D_HID,), dtype=jnp.float32)
        Wu = jax.random.normal(ks[9], (D_NODE + D_HID, D_NODE), dtype=jnp.float32) / np.sqrt(D_NODE + D_HID)
        bu = jnp.zeros((D_NODE,), dtype=jnp.float32)
        return {'node_features': node_features, 'edge_index': edge_index, 'edge_attr_tensor': edge_attr_tensor, 'node_attr_scalar_raw': node_attr_scalar_raw, 'W1': W1, 'W2': W2, 'W3': W3, 'W4': W4, 'Wm': Wm, 'bm': bm, 'Wu': Wu, 'bu': bu}
    _L0_gnn_all = _L0_gnn_setup()
    _L0_gnn_in = {k: v for k, v in _L0_gnn_all.items() if k in ('W1', 'W2', 'W3', 'W4', 'Wm', 'bm', 'Wu', 'bu')}
    del _L0_gnn_all

    def _L1_gnn_setup():
        import jax, jax.numpy as jnp
        import numpy as np
        N = 2500
        E = 40000
        MUL0 = 64
        MUL1 = 32
        FC_IN = 16
        FC_H = 64
        WNUM = 192
        key = jax.random.key(seed)
        ks = jax.random.split(key, 16)
        return {'x': jax.random.normal(ks[0], (N, MUL0 + 3 * MUL1), jnp.float32), 'node_attr': jnp.ones((N, 1), jnp.float32), 'edge_scalars': jax.random.normal(ks[1], (E, FC_IN), jnp.float32), 'edge_attr_sh': jax.random.normal(ks[2], (E, 4), jnp.float32), 'edge_src': jax.random.randint(ks[3], (E,), 0, N), 'edge_dst': jax.random.randint(ks[4], (E,), 0, N), 'Wfc1': jax.random.normal(ks[5], (FC_IN, FC_H), jnp.float32), 'Wfc2': jax.random.normal(ks[6], (FC_H, WNUM), jnp.float32), 'Wsc0': jax.random.normal(ks[7], (MUL0, MUL0), jnp.float32), 'Wsc1': jax.random.normal(ks[8], (MUL1, MUL1), jnp.float32), 'Wl1_0': jax.random.normal(ks[9], (MUL0, MUL0), jnp.float32), 'Wl1_1': jax.random.normal(ks[10], (MUL1, MUL1), jnp.float32), 'Wl2_s': jax.random.normal(ks[11], (MUL0 + MUL1, MUL0), jnp.float32), 'Wl2_v': jax.random.normal(ks[12], (MUL0 + MUL1, MUL1), jnp.float32), 'Wa': 0.1 * jax.random.normal(ks[13], (MUL0 + MUL1, 1), jnp.float32)}
    _L1_gnn_all = _L1_gnn_setup()
    _L1_gnn_in = {k: v for k, v in _L1_gnn_all.items() if k in ('Wfc1', 'Wfc2', 'Wsc0', 'Wsc1', 'Wl1_0', 'Wl1_1', 'Wl2_s', 'Wl2_v', 'Wa')}
    del _L1_gnn_all
    return {'x': x, 'src': src, 'dst': dst, 'edge_attr_16': edge_attr_16, 'edge_attr_32': edge_attr_32, 'edge_attr_4': edge_attr_4, 'node_vec1': node_vec1, 'L0_gnn_W1': _L0_gnn_in['W1'], 'L0_gnn_W2': _L0_gnn_in['W2'], 'L0_gnn_W3': _L0_gnn_in['W3'], 'L0_gnn_W4': _L0_gnn_in['W4'], 'L0_gnn_Wm': _L0_gnn_in['Wm'], 'L0_gnn_bm': _L0_gnn_in['bm'], 'L0_gnn_Wu': _L0_gnn_in['Wu'], 'L0_gnn_bu': _L0_gnn_in['bu'], 'L1_gnn_Wfc1': _L1_gnn_in['Wfc1'], 'L1_gnn_Wfc2': _L1_gnn_in['Wfc2'], 'L1_gnn_Wsc0': _L1_gnn_in['Wsc0'], 'L1_gnn_Wsc1': _L1_gnn_in['Wsc1'], 'L1_gnn_Wl1_0': _L1_gnn_in['Wl1_0'], 'L1_gnn_Wl1_1': _L1_gnn_in['Wl1_1'], 'L1_gnn_Wl2_s': _L1_gnn_in['Wl2_s'], 'L1_gnn_Wl2_v': _L1_gnn_in['Wl2_v'], 'L1_gnn_Wa': _L1_gnn_in['Wa']}

def reference(x, src, dst, edge_attr_16, edge_attr_32, edge_attr_4, node_vec1, L0_gnn_W1, L0_gnn_W2, L0_gnn_W3, L0_gnn_W4, L0_gnn_Wm, L0_gnn_bm, L0_gnn_Wu, L0_gnn_bu, L1_gnn_Wfc1, L1_gnn_Wfc2, L1_gnn_Wsc0, L1_gnn_Wsc1, L1_gnn_Wl1_0, L1_gnn_Wl1_1, L1_gnn_Wl2_s, L1_gnn_Wl2_v, L1_gnn_Wa):
    import jax
    import jax.numpy as jnp

    def _L0_gnn_ref(node_features, edge_index, edge_attr_tensor, node_attr_scalar_raw, W1, W2, W3, W4, Wm, bm, Wu, bu):
        import jax, jax.numpy as jnp
        import numpy as np
        MUL0_N, MUL1_N = (64, 32)
        MUL0_E, MUL1_E = (8, 8)
        MUL0_H, MUL1_H = (64, 32)
        N_NODES, N_EDGES = (6250, 100000)
        D_NODE = MUL0_N + 3 * MUL1_N
        D_EDGE = MUL0_E + 3 * MUL1_E
        D_HID = MUL0_H + 3 * MUL1_H

        def _split(x, mul0, mul1):
            s = x[..., :mul0]
            v = x[..., mul0:].reshape(x.shape[0], mul1, 3)
            return (s, v)

        def fctp_messages(x, e, W1, W2, W3, W4):
            xs, xv = _split(x, MUL0_N, MUL1_N)
            es, ev = _split(e, MUL0_E, MUL1_E)
            inv_sqrt2 = 1.0 / np.sqrt(2.0)
            s1 = jnp.einsum('ea,eb,abc->ec', xs, es, W1) * (1.0 / np.sqrt(MUL0_N * MUL0_E))
            s2 = jnp.einsum('eai,ebi,abc->ec', xv, ev, W2) * (1.0 / (np.sqrt(3.0) * np.sqrt(MUL1_N * MUL1_E)))
            out_s = (s1 + s2) * inv_sqrt2
            v1 = jnp.einsum('ea,ebi,abc->eci', xs, ev, W3) * (1.0 / np.sqrt(MUL0_N * MUL1_E))
            v2 = jnp.einsum('eai,eb,abc->eci', xv, es, W4) * (1.0 / np.sqrt(MUL1_N * MUL0_E))
            out_v = (v1 + v2) * inv_sqrt2
            return jnp.concatenate([out_s, out_v.reshape(out_v.shape[0], -1)], axis=-1)
        row, col = (edge_index[0], edge_index[1])
        tp = fctp_messages(node_features[col], edge_attr_tensor, W1, W2, W3, W4)
        messages = tp @ Wm + bm
        agg = jax.ops.segment_sum(messages, row, num_segments=N_NODES)
        upd = jnp.concatenate([node_features, agg], axis=-1) @ Wu + bu
        return node_features + upd

    def _L1_gnn_ref(x, node_attr, edge_scalars, edge_attr_sh, edge_src, edge_dst, Wfc1, Wfc2, Wsc0, Wsc1, Wl1_0, Wl1_1, Wl2_s, Wl2_v, Wa):
        import jax, jax.numpy as jnp
        import numpy as np
        N = 2500
        E = 40000
        MUL0 = 64
        MUL1 = 32
        FC_IN = 16
        FC_H = 64
        WNUM = 192
        n = x.shape[0]
        x0 = x[:, :MUL0]
        x1 = x[:, MUL0:].reshape(n, MUL1, 3)
        a = node_attr
        h = jax.nn.silu(edge_scalars @ (Wfc1 / jnp.sqrt(jnp.float32(FC_IN))))
        w = h @ (Wfc2 / jnp.sqrt(jnp.float32(FC_H)))
        w0 = w[:, :64]
        w1 = w[:, 64:128]
        w2 = w[:, 128:160]
        w3 = w[:, 160:192]
        inv8 = 1.0 / jnp.sqrt(jnp.float32(MUL0))
        inv32 = 1.0 / jnp.sqrt(jnp.float32(MUL1))
        sc = jnp.concatenate([x0 @ Wsc0 * a * inv8, (jnp.einsum('num,uv->nvm', x1, Wsc1) * a[..., None] * inv32).reshape(n, 3 * MUL1)], axis=1)
        f0 = x0 @ Wl1_0 * a * inv8
        f1 = jnp.einsum('num,uv->nvm', x1, Wl1_1) * a[..., None] * inv32
        e0 = f0[edge_src]
        e1 = f1[edge_src]
        sh0 = edge_attr_sh[:, :1]
        sh1 = edge_attr_sh[:, 1:4]
        mid0 = w0 * e0 * sh0
        mid1 = w3 * jnp.einsum('eum,em->eu', e1, sh1) / jnp.sqrt(3.0)
        mid2 = w1[:, :, None] * e0[:, :, None] * sh1[:, None, :]
        mid3 = w2[:, :, None] * e1 * sh0[:, :, None]
        cnt = jnp.clip(jax.ops.segment_sum(jnp.ones(edge_dst.shape, x.dtype), edge_dst, num_segments=n), 1.0)

        def smean(v):
            s = jax.ops.segment_sum(v, edge_dst, num_segments=n)
            return s / cnt.reshape((n,) + (1,) * (v.ndim - 1))
        n0, n1 = (smean(mid0), smean(mid1))
        n2, n3 = (smean(mid2), smean(mid3))
        scal = jnp.concatenate([n0, n1], axis=1)
        vec = jnp.concatenate([n2, n3], axis=1)
        inv96 = 1.0 / jnp.sqrt(jnp.float32(MUL0 + MUL1))
        alpha = scal @ Wa * a * inv96
        out_s = scal @ Wl2_s * a * inv96
        out_v = jnp.einsum('num,uv->nvm', vec, Wl2_v) * a[..., None] * inv96
        conv = jnp.concatenate([out_s, out_v.reshape(n, 3 * MUL1)], axis=1)
        return sc + alpha * conv
    edge_index = jnp.stack([src, dst])
    x = _layernorm(x + _L0_gnn_ref(x, edge_index, edge_attr_32, node_vec1, L0_gnn_W1, L0_gnn_W2, L0_gnn_W3, L0_gnn_W4, L0_gnn_Wm, L0_gnn_bm, L0_gnn_Wu, L0_gnn_bu), axis=-1)
    x = _layernorm(x + _L1_gnn_ref(x, node_vec1, edge_attr_16, edge_attr_4, src, dst, L1_gnn_Wfc1, L1_gnn_Wfc2, L1_gnn_Wsc0, L1_gnn_Wsc1, L1_gnn_Wl1_0, L1_gnn_Wl1_1, L1_gnn_Wl2_s, L1_gnn_Wl2_v, L1_gnn_Wa), axis=-1)
    return x

_drawn_inputs = setup_inputs


def setup_inputs(seed=0):
    import zlib

    import numpy as np

    out = dict(_drawn_inputs(seed))
    spreads = {'L0_gnn_bm': (0.0, 0.1), 'L0_gnn_bu': (0.0, 0.38)}
    factors = {'edge_attr_16': 8.0,
     'edge_attr_4': 8.0,
     'L1_gnn_Wfc1': 8.0,
     'L1_gnn_Wfc2': 8.0,
     'L1_gnn_Wl1_0': 8.0,
     'L1_gnn_Wl1_1': 8.0,
     'L1_gnn_Wl2_s': 8.0,
     'L1_gnn_Wl2_v': 8.0,
     'L1_gnn_Wa': 8.0}
    for name, (base, spread) in spreads.items():
        noise = np.random.default_rng([zlib.crc32(name.encode()), seed]).standard_normal(out[name].shape)
        drawn = base * np.exp(spread * noise) if base else spread * noise
        out[name] = jnp.asarray(drawn.astype(out[name].dtype))
    for name, factor in factors.items():
        out[name] = (out[name] * factor).astype(out[name].dtype)
    return out
```

```python
import concourse.bass as bass
from concourse import mybir
from contextlib import ExitStack
import numpy as np

fp32 = mybir.dt.float32
bf16 = mybir.dt.bfloat16
i32 = mybir.dt.int32
ALU = mybir.AluOpType
ACT = mybir.ActivationFunctionType
AX = mybir.AxisListType

P = 128
N_NODES = 6250
N_EDGES = 200000
GROUPS = 16
TILES = 1568
STEPS = TILES // GROUPS
SLOTS = P * TILES
NODE_TILES = 50
NODE_ROWS = NODE_TILES * P
PAD_NODE = NODE_ROWS - 1
DIGIT = 32


class Grouping:

    def __init__(self, name, shift, per_step):
        self.name, self.shift = name, shift
        self.width = 1 << shift
        self.buckets = -(-N_NODES // self.width)
        most = self.buckets + N_EDGES // P
        self.visits = -(-most // per_step) * per_step
        self.cols = -(-self.visits // P)


class Rank:
    pass


def alloc_rank(ctx, nc, g):
    R = Rank()

    def sb(n, s, d=fp32):
        return ctx.enter_context(nc.sbuf_tensor(f"{g.name}_{n}", s, d))

    def ps(n, s, d=fp32):
        return ctx.enter_context(nc.psum_tensor(f"{g.name}_{n}", s, d))

    def sem(n):
        return ctx.enter_context(nc.semaphore(f"{g.name}_{n}"))

    R.digit_i = sb("digit_i", [P, TILES], i32)
    R.digits = sb("digits", [P, 2, TILES], bf16)
    R.onehot = sb("onehot", [P, 2, 2, GROUPS, DIGIT], bf16)
    R.hi_t = sb("hi_t", [P, 4, P], bf16)
    R.hi_t32 = sb("hi_t32", [P, 4, P])
    R.earlier = sb("earlier", [P, GROUPS, P], bf16)
    R.count = sb("count", [P, 4, 4, DIGIT])
    R.fresh = sb("fresh", [P, 4, 4, DIGIT])
    R.by_group = sb("by_group", [P, 4, DIGIT])
    R.picked = sb("picked", [P, GROUPS, DIGIT])
    R.pos_f = sb("pos_f", [P, TILES])
    R.small = sb("small", [P, 16, DIGIT])
    R.small_i = sb("small_i", [P, 2, DIGIT], i32)
    R.vb_row = sb("vb_row", [P, g.buckets])
    R.s_row = sb("s_row", [P, g.buckets])
    R.ds_row = sb("ds_row", [P, g.buckets])
    R.mask = sb("mask", [P, g.buckets])
    R.junk = sb("junk", [P, g.buckets])
    R.ones = sb("ones", [P, max(g.buckets, DIGIT)])
    R.vtab = sb("vtab", [P, 4, g.cols])
    R.vtab_i = sb("vtab_i", [P, g.cols], i32)
    R.ps_t = ps("ps_t", [P, 4, P], bf16)
    R.ps_eq = ps("ps_eq", [P, GROUPS, P])
    R.ps_g = ps("ps_g", [P, GROUPS, DIGIT])
    R.ps_h = ps("ps_h", [P, 4, 4, DIGIT])
    R.ps_s = ps("ps_s", [P, 3 * DIGIT])
    R.s_loaded = sem("loaded")
    R.s_onehot_ready = sem("onehot_ready")
    R.s_onehot_counted = sem("onehot_counted")
    R.s_counted = sem("counted")
    R.s_sums_ready = sem("sums_ready")
    R.s_sums_done = sem("sums_done")
    R.s_hi_t_ps = sem("hi_t_ps")
    R.s_hi_t_ready = sem("hi_t_ready")
    R.s_eq_ps = sem("eq_ps")
    R.s_earlier_ready = sem("earlier_ready")
    R.s_hist_ps = sem("hist_ps")
    R.s_count_ready = sem("count_ready")
    R.s_rank_ps = sem("rank_ps")
    R.s_rank_read = sem("rank_read")
    R.s_dve = sem("dve")
    R.s_act = sem("act")
    R.s_tables_ready = sem("tables_ready")
    R.s_tables_out = sem("tables_out")
    R.s_rows_in = sem("rows_in")
    R.s_visits_ready = sem("visits_ready")
    R.s_visits_out = sem("visits_out")
    R.s_pos_ready = sem("pos_ready")
    return R


def rank_vector(nc, dve, g, R, C, node, pos):
    done = [0]

    def link(ins):
        done[0] += 1
        ins.then_inc(R.s_dve, 1)
        dve.wait_ge(R.s_dve, done[0])

    link(nc.vector.memset(R.ones[:, :], 1.0))
    dve.wait_ge(R.s_loaded, 16)
    link(nc.vector.tensor_scalar(R.digit_i[:, :], node[:, :], g.shift + 5, None, ALU.logical_shift_right))
    link(nc.vector.tensor_copy(R.digits[:, 0, :], R.digit_i[:, :]))
    link(nc.vector.tensor_scalar(R.digit_i[:, :], node[:, :], g.shift, DIGIT - 1, ALU.logical_shift_right, ALU.bitwise_and))
    link(nc.vector.tensor_copy(R.digits[:, 1, :], R.digit_i[:, :]))

    def onehots(step, par):
        return nc.vector.tensor_tensor(
            R.onehot[:, par, :, :, :],
            R.digits[:, :, bass.ds(step * GROUPS, GROUPS)].unsqueeze(3).broadcast_to([P, 2, GROUPS, DIGIT]),
            C["iota"][:, 0:DIGIT].unsqueeze(1).unsqueeze(1).broadcast_to([P, 2, GROUPS, DIGIT]),
            ALU.is_equal)

    for par in range(2):
        onehots(par, par).then_inc(R.s_onehot_ready, 1)
    with dve.Fori(1, STEPS // 2) as t:
        for par in range(2):
            dve.wait_ge(R.s_onehot_counted, t * 2 + par - 1)
            onehots(t * 2 + par, par).then_inc(R.s_onehot_ready, 1)

    small = R.small
    dve.wait_ge(R.s_counted, 1)
    own = C["own_group"].unsqueeze(1).broadcast_to([P, 4, 4, DIGIT])
    link(nc.vector.tensor_tensor(R.fresh[:, :, :, :], R.ps_h[:, :, :, :], own, ALU.mult))
    link(nc.vector.tensor_reduce(R.by_group[:, :, :], R.fresh[:, :, :, :].rearrange("p q g l -> p q l g"), AX.X, ALU.add))
    nc.vector.tensor_reduce(small[:, 0, :], R.by_group[:, :, :].rearrange("p q l -> p l q"), AX.X, ALU.add).then_inc(R.s_sums_ready, 1)
    dve.wait_ge(R.s_sums_done, 1)
    link(nc.vector.tensor_copy(small[:, 1:3, :], R.ps_s[:, 0:2 * DIGIT].rearrange("p (a l) -> p a l", l=DIGIT)))
    link(nc.vector.tensor_tensor_scan(small[:, 3, :], R.ones[:, 0:DIGIT], small[:, 1, :], 0.0, ALU.mult, ALU.add))
    link(nc.vector.tensor_scalar(small[:, 4, :], small[:, 1, :], float(P - 1), None, ALU.add))
    link(nc.vector.tensor_copy(R.small_i[:, 0, :], small[:, 4, :]))
    link(nc.vector.tensor_scalar(R.small_i[:, 1, :], R.small_i[:, 0, :], 7, None, ALU.logical_shift_right))
    link(nc.vector.tensor_copy(small[:, 5, :], R.small_i[:, 1, :]))
    link(nc.vector.tensor_scalar(small[:, 6, :], small[:, 5, :], 1.0, None, ALU.max))
    link(nc.vector.tensor_tensor_scan(small[:, 7, :], R.ones[:, 0:DIGIT], small[:, 6, :], 0.0, ALU.mult, ALU.add))
    link(nc.vector.tensor_copy(small[:, 8, 0:1], small[:, 3, DIGIT - 1:DIGIT]))
    nc.vector.tensor_copy(small[:, 8, 1:2], small[:, 7, DIGIT - 1:DIGIT]).then_inc(R.s_sums_ready, 1)
    dve.wait_ge(R.s_sums_done, 2)
    link(nc.vector.tensor_copy(small[:, 8, 2:4], R.ps_s[:, 2 * DIGIT:2 * DIGIT + 2]))
    link(nc.vector.tensor_tensor(small[:, 9, :], small[:, 3, :], small[:, 1, :], ALU.subtract))
    link(nc.vector.tensor_scalar(small[:, 9, :], small[:, 9, :], small[:, 8, 2:3], None, ALU.add))
    link(nc.vector.tensor_tensor(small[:, 10, :], small[:, 7, :], small[:, 6, :], ALU.subtract))
    link(nc.vector.tensor_scalar(small[:, 10, :], small[:, 10, :], small[:, 8, 3:4], None, ALU.add))
    nc.vector.scalar_tensor_tensor(small[:, 11, :], small[:, 10, :], -float(P), small[:, 9, :], ALU.mult, ALU.add).then_inc(R.s_tables_ready, 1)
    link(nc.vector.tensor_tensor(small[:, 13, :], small[:, 9, :], small[:, 2, :], ALU.add))
    for q in range(4):
        last = nc.vector.tensor_tensor(R.count[:, q, :, :], C["own_group"], small[:, 13, :].unsqueeze(1).broadcast_to([P, 4, DIGIT]), ALU.mult)
        if q < 3:
            link(last)
            link(nc.vector.tensor_tensor(small[:, 13, :], small[:, 13, :], R.by_group[:, q, :], ALU.add))
    last.then_inc(R.s_count_ready, 1)
    for par in range(2):
        onehots(par, par).then_inc(R.s_onehot_ready, 1)

    first = done[0]
    per_step = 2

    def place(step, par):
        base = step * per_step + first
        dve.wait_ge(R.s_hist_ps, step + 1)
        nc.vector.tensor_tensor(R.fresh[:, :, :, :], R.ps_h[:, :, :, :], own, ALU.mult).then_inc(R.s_dve, 1)
        dve.wait_ge(R.s_rank_ps, step + 1)
        nc.vector.tensor_tensor(R.picked[:, :, :], R.ps_g[:, :, :], R.onehot[:, par, 1, :, :], ALU.mult).then_inc(R.s_dve, 1)
        dve.wait_ge(R.s_dve, base + 1)
        nc.vector.tensor_tensor(R.count[:, :, :, :], R.count[:, :, :, :], R.fresh[:, :, :, :], ALU.add).then_inc(R.s_count_ready, 1)
        dve.wait_ge(R.s_dve, base + 2)
        nc.vector.tensor_reduce(R.pos_f[:, bass.ds(step * GROUPS, GROUPS)], R.picked[:, :, :], AX.X, ALU.add).then_inc(R.s_rank_read, 1)

    with dve.Fori(0, STEPS // 2 - 1) as t:
        for par in range(2):
            place(t * 2 + par, par)
            onehots(t * 2 + par + 2, par).then_inc(R.s_onehot_ready, 1)
    for par in range(2):
        place(STEPS - 2 + par, par)
    done[0] = first + per_step * STEPS
    dve.wait_ge(R.s_rank_read, STEPS)
    nc.vector.tensor_copy(pos[:, :], R.pos_f[:, :]).then_inc(R.s_pos_ready, 1)

    dve.wait_ge(R.s_rows_in, 32)
    nc.vector.tensor_copy(R.ds_row[:, 0:1], R.s_row[:, 0:1]).then_inc(R.s_dve, 1)
    done[0] += 1
    link(nc.vector.tensor_tensor(R.ds_row[:, 1:], R.s_row[:, 1:], R.s_row[:, :g.buckets - 1], ALU.subtract))
    for c in range(g.cols):
        link(nc.vector.tensor_scalar(R.mask[:, :], R.vb_row[:, :], C["visit_" + g.name][:, c:c + 1], None, ALU.is_le))
        link(nc.vector.tensor_tensor_reduce(out=R.junk[:, :], in0=R.mask[:, :], in1=R.ones[:, 0:g.buckets], scale=1.0, scalar=0.0,
                                            op0=ALU.mult, op1=ALU.add, accum_out=R.vtab[:, 0, c:c + 1]))
        link(nc.vector.tensor_tensor_reduce(out=R.junk[:, :], in0=R.mask[:, :], in1=R.ds_row[:, :], scale=1.0, scalar=0.0,
                                            op0=ALU.mult, op1=ALU.add, accum_out=R.vtab[:, 1, c:c + 1]))
    link(nc.vector.tensor_scalar(R.vtab[:, 2, :], R.vtab[:, 0, :], -1.0, None, ALU.add))
    link(nc.vector.scalar_tensor_tensor(R.vtab[:, 3, :], C["visit_" + g.name][:, 0:g.cols], float(P), R.vtab[:, 1, :], ALU.mult, ALU.add))
    link(nc.vector.tensor_scalar(R.vtab[:, 3, :], R.vtab[:, 3, :], float(N_EDGES), None, ALU.min))
    nc.vector.tensor_copy(R.vtab_i[:, :], R.vtab[:, 3, :]).then_inc(R.s_visits_ready, 1)


def rank_tensor(nc, pe, g, R, C):
    def counts(par, start, stop):
        for q in range(4):
            hi, lo = (R.onehot[:, par, d, 4 * q:4 * q + 4, :].rearrange("p g k -> p (g k)") for d in range(2))
            last = nc.tensor.matmul(R.ps_h[:, q, :, :], hi, lo, start=start and q == 0, stop=stop and q == 3)
        return last

    for par in range(2):
        pe.wait_ge(R.s_onehot_ready, par + 1)
        counts(par, par == 0, False).then_inc(R.s_onehot_counted, 1)
    with pe.Fori(1, STEPS // 2 - 1) as t:
        for par in range(2):
            pe.wait_ge(R.s_onehot_ready, t * 2 + par + 1)
            counts(par, False, False).then_inc(R.s_onehot_counted, 1)
    for par in range(2):
        pe.wait_ge(R.s_onehot_ready, STEPS - 1 + par)
        last = counts(par, False, par == 1)
        last.then_inc(R.s_onehot_counted if par == 0 else R.s_counted, 1)

    pe.wait_ge(R.s_sums_ready, 1)
    nc.tensor.matmul(R.ps_s[:, 0:DIGIT], C["all_groups"], R.small[:, 0, :], start=True, stop=True)
    nc.tensor.matmul(R.ps_s[:, DIGIT:2 * DIGIT], C["groups_before"], R.small[:, 0, :], start=True, stop=True).then_inc(R.s_sums_done, 1)
    pe.wait_ge(R.s_sums_ready, 2)
    nc.tensor.matmul(R.ps_s[:, 2 * DIGIT:2 * DIGIT + 2], C["digits_before"], R.small[:, 8, 0:2], start=True, stop=True).then_inc(R.s_sums_done, 1)

    def step(s, par, first):
        pe.wait_ge(R.s_onehot_ready, s + STEPS + 1)
        for q in range(4):
            last = nc.tensor.transpose(R.ps_t[:, q, :], R.onehot[:, par, 0, 4 * q:4 * q + 4, :].rearrange("p g d -> p (g d)"), C["ident16"])
        last.then_inc(R.s_hi_t_ps, 1)
        pe.wait_ge(R.s_count_ready, s + 1)
        counts(par, True, True).then_inc(R.s_hist_ps, 1)
        if not first:
            pe.wait_ge(R.s_earlier_ready, s * 4)
        for b in range(4):
            nc.tensor.matmul(R.ps_eq[:, 4 * b:4 * b + 4, :], C["ident16"], C["not_earlier"], start=True, stop=False)
        pe.wait_ge(R.s_hi_t_ready, s * 2 + 2)
        for b in range(4):
            for q in range(4):
                hi_t = R.hi_t[32 * b:32 * b + 32, q, :]
                last = nc.tensor.matmul(R.ps_eq[:, 4 * b + q, :], hi_t, hi_t, start=False, stop=(q == 3), tile_position=(32 * b, 0))
            last.then_inc(R.s_eq_ps, 1)
        if not first:
            pe.wait_ge(R.s_rank_read, s)
        for q in range(4):
            nc.tensor.matmul(R.ps_g[:, 4 * q:4 * q + 4, :], R.hi_t32[:, q, :], R.count[:, q, :, :], start=(q == 0), stop=False)
        for slot in range(GROUPS):
            b, q = slot // 4, slot % 4
            if q == 0:
                pe.wait_ge(R.s_earlier_ready, s * 4 + b + 1)
            last = nc.tensor.matmul(R.ps_g[:, 4 * q + b, :], R.earlier[:, slot, :], R.onehot[:, par, 1, 4 * q + b, :],
                                    start=False, stop=(slot == GROUPS - 1))
        last.then_inc(R.s_rank_ps, 1)

    for par in range(2):
        step(par, par, par == 0)
    with pe.Fori(1, STEPS // 2) as t:
        for par in range(2):
            step(t * 2 + par, par, False)


def rank_scalar(nc, act, g, R, C, D):
    def step(s, first):
        act.wait_ge(R.s_hi_t_ps, s + 1)
        if not first:
            act.wait_ge(R.s_rank_ps, s)
        nc.scalar.copy(R.hi_t[:, :, :], R.ps_t[:, :, :]).then_inc(R.s_hi_t_ready, 1)
        nc.scalar.copy(R.hi_t32[:, :, :], R.ps_t[:, :, :]).then_inc(R.s_hi_t_ready, 1)
        for b in range(4):
            act.wait_ge(R.s_eq_ps, s * 4 + b + 1)
            nc.scalar.activation(R.earlier[:, 4 * b:4 * b + 4, :], R.ps_eq[:, 4 * b:4 * b + 4, :], ACT.Relu).then_inc(R.s_earlier_ready, 1)

    for s in range(2):
        step(s, s == 0)
    with act.Fori(1, STEPS // 2) as t:
        for par in range(2):
            step(t * 2 + par, False)

    def row(a):
        return a[0:g.buckets].rearrange("(o b) -> o b", o=1).broadcast_to([P, g.buckets])

    act.wait_ge(R.s_tables_ready, 1)
    act.dma_start(D["vb"].rearrange("(h l) -> h l", l=DIGIT), R.small[0:DIGIT, 10, :]).then_inc(R.s_tables_out, 16)
    act.dma_start(D["s"].rearrange("(h l) -> h l", l=DIGIT), R.small[0:DIGIT, 11, :]).then_inc(R.s_tables_out, 16)
    act.wait_ge(R.s_tables_out, 32)
    act.dma_start(R.vb_row[:, :], row(D["vb"])).then_inc(R.s_rows_in, 16)
    act.dma_start(R.s_row[:, :], row(D["s"])).then_inc(R.s_rows_in, 16)
    act.wait_ge(R.s_visits_ready, 1)
    act.dma_start(D["bucket"].rearrange("(p c) -> p c", c=g.cols), R.vtab[:, 2, :]).then_inc(R.s_visits_out, 16)
    act.dma_start(D["start"].rearrange("(p c) -> p c", c=g.cols), R.vtab_i[:, :]).then_inc(R.s_visits_out, 16)
    act.wait_ge(R.s_visits_out, 32)


def rank_constants(groupings):
    k = np.arange(P)
    gp, hi = k // 32, k % 32
    out = {
        "iota": np.tile(np.arange(P, dtype=np.float32), (P, 1)),
        "ident": np.eye(P, dtype=np.float32),
        "not_earlier": np.tile(-(k[:, None] >= k[None, :]).astype(np.float32), (1, 4)),
        "own_group": np.repeat(gp[:, None] == np.arange(4)[None, :], DIGIT, axis=1).astype(np.float32),
        "all_groups": (hi[:, None] == hi[None, :]).astype(np.float32),
        "groups_before": ((hi[:, None] == hi[None, :]) & (gp[:, None] < gp[None, :])).astype(np.float32),
        "digits_before": ((gp[:, None] == gp[None, :]) & (hi[:, None] < hi[None, :])).astype(np.float32),
    }
    for g in groupings:
        out["visit_" + g.name] = np.arange(P * g.cols, dtype=np.float32).reshape(P, g.cols)
    return out



CHUNK = 16
CHUNKS = TILES // CHUNK


class Scatter:

    def __init__(self, ctx, nc, name, width):
        self.name, self.width = name, width
        self.stage = ctx.enter_context(nc.sbuf_tensor(f"{name}_stage", [P, 2, CHUNK, width], fp32))
        self.place = ctx.enter_context(nc.sbuf_tensor(f"{name}_place", [P, 2, CHUNK], i32))
        self.s_in = [ctx.enter_context(nc.semaphore(f"{name}_in{r}")) for r in range(2)]
        self.s_out = [ctx.enter_context(nc.semaphore(f"{name}_out{r}")) for r in range(2)]
        self.s_begun = ctx.enter_context(nc.semaphore(f"{name}_begun"))
        self.s_staged = ctx.enter_context(nc.semaphore(f"{name}_staged"))


def scatter_sync(nc, sp, S, parts):
    def load(c, r):
        for dram, at in parts:
            sp.dma_start(S.stage[:, r, :, at:at + dram.shape[2]], dram[:, bass.ds(c * CHUNK, CHUNK), :]).then_inc(S.s_in[r], 16)

    for r in range(2):
        load(r, r)
    with sp.Fori(1, CHUNKS // 2) as t:
        for r in range(2):
            sp.wait_ge(S.s_out[r], t * (16 * CHUNK))
            load(t * 2 + r, r)


def scatter_pool(nc, pool, S, n_parts, src, dst, pos, known, out):
    w = S.width

    def chunk(t, r, first):
        c = t * 2 + r
        if not first:
            pool.wait_ge(S.s_out[r], t * (16 * CHUNK))
        at = bass.ds(c * CHUNK, CHUNK)
        nc.gpsimd.tensor_copy(S.stage[:, r, :, w - 2].bitcast(i32), src[:, at]).then_inc(S.s_staged, 1)
        nc.gpsimd.tensor_copy(S.stage[:, r, :, w - 1].bitcast(i32), dst[:, at]).then_inc(S.s_staged, 1)
        nc.gpsimd.tensor_copy(S.place[:, r, :], pos[:, at]).then_inc(S.s_staged, 1)
        pool.wait_ge(S.s_in[r], (t + 1) * (16 * n_parts))
        pool.wait_ge(S.s_staged, c * 3 + 3)
        pool.sem_inc(S.s_begun, 1)
        for j in range(CHUNK):
            nc.gpsimd.indirect_dma_start(out=out, out_offset=bass.IndirectOffsetOnAxis(ap=S.place[:, r, j:j + 1], axis=0),
                                         in_=S.stage[:, r, j, :], in_offset=None).then_inc(S.s_out[r], 16)

    pool.wait_ge(*known)
    for r in range(2):
        chunk(0, r, True)
    with pool.Fori(1, CHUNKS // 2) as t:
        for r in range(2):
            chunk(t, r, False)
    for r in range(2):
        pool.wait_ge(S.s_out[r], 16 * CHUNK * (CHUNKS // 2))


def gnn_kernel(nc, A, out, scratch):
    D0 = 160
    NS, NV = 64, 32
    VG = 4
    G0, G1 = A["groupings"]
    REC0, REC1 = 34, 22
    BATCH0, BATCHES0 = 16, G0.visits // 16
    GPB0 = BATCH0 // VG
    BATCH1, BATCHES1 = 8, G1.visits // 8
    GPB1 = BATCH1 // VG
    WIN = P
    rec0, rec1, f_tab, base_tab = scratch["rec0"], scratch["rec1"], scratch["f"], scratch["base"]

    outer = ExitStack()
    with outer:
        def sb_in(ctx, stage=""):
            return lambda n, s, d=fp32: ctx.enter_context(nc.sbuf_tensor(stage + n, s, d))

        def ps_in(ctx, stage=""):
            return lambda n, s, d=fp32: ctx.enter_context(nc.psum_tensor(stage + n, s, d))

        def sem_in(ctx, stage=""):
            return lambda n: ctx.enter_context(nc.semaphore(stage + n))

        sb = sb_in(outer)
        ident = sb("ident", [P, P])
        ident16 = sb("ident16", [P, P], bf16)
        iota = sb("iota", [P, P])

        with ExitStack() as ctx:
            sb, sem = sb_in(ctx), sem_in(ctx)
            src = sb("src", [P, TILES], i32)
            dst = sb("dst", [P, TILES], i32)
            src_pos = sb("src_pos", [P, TILES], i32)
            dst_pos = sb("dst_pos", [P, TILES], i32)
            iota16 = sb("iota16", [P, DIGIT], bf16)
            not_earlier32 = sb("not_earlier32", [P, 4 * P])
            not_earlier = sb("not_earlier", [P, 4 * P], bf16)
            own_group = sb("own_group", [P, 4, DIGIT])
            sums = {n: sb(n, [P, P]) for n in ("all_groups", "groups_before", "digits_before")}
            visit_no = {g.name: sb("visit_" + g.name, [P, g.cols]) for g in (G0, G1)}
            s_const, s_made = sem("s_const"), sem("s_made")
            C = {"iota": iota16, "ident16": ident16[:, :], "not_earlier": not_earlier[:, :], "own_group": own_group[:, :, :],
                 **{n: t[:, :] for n, t in sums.items()}, **{"visit_" + n: t for n, t in visit_no.items()}}
            consts = [(ident, A["ident"]), (iota, A["iota"]), (not_earlier32, A["not_earlier"]), (own_group, A["own_group"].rearrange("p (g l) -> p g l", l=DIGIT))]
            consts += [(sums[n], A[n]) for n in sums] + [(visit_no[n], A["visit_" + n]) for n in visit_no]

            with nc.Block() as block:
                @block.sync
                def _(sp):
                    for tile, dram in consts:
                        sp.dma_start(tile[:], dram).then_inc(s_const, 16)

                @block.vector
                def _(dve):
                    dve.wait_ge(s_const, 16 * len(consts))
                    nc.vector.tensor_copy(ident16[:, :], ident[:, :])
                    nc.vector.tensor_copy(iota16[:, :], iota[:, 0:DIGIT])
                    nc.vector.tensor_copy(not_earlier[:, :], not_earlier32[:, :]).then_inc(s_made, 1)

            with ExitStack() as rank_ctx:
                R0 = alloc_rank(rank_ctx, nc, G0)
                with nc.Block() as block:
                    @block.sync
                    def _(sp):
                        sp.dma_start(src[:, :], A["src"]).then_inc(R0.s_loaded, 16)

                    @block.vector
                    def _(dve):
                        rank_vector(nc, dve, G0, R0, C, src, src_pos)

                    @block.tensor
                    def _(pe):
                        rank_tensor(nc, pe, G0, R0, C)

                    @block.scalar
                    def _(act):
                        rank_scalar(nc, act, G0, R0, C, scratch["tables0"])

            with ExitStack() as rank_ctx:
                S0 = Scatter(rank_ctx, nc, "edges0", REC0)
                S1 = Scatter(rank_ctx, nc, "edges1", REC1)
                R1 = alloc_rank(rank_ctx, nc, G1)
                with nc.Block() as block:
                    @block.sync
                    def _(sp):
                        sp.dma_start(dst[:, :], A["dst"]).then_inc(R1.s_loaded, 16)
                        scatter_sync(nc, sp, S0, [(A["edge_attr_32"], 0)])
                        scatter_sync(nc, sp, S1, [(A["edge_attr_16"], 0), (A["edge_attr_4"], 16)])

                    @block.scalar
                    def _(act):
                        rank_scalar(nc, act, G1, R1, C, scratch["tables1"])

                    @block.vector
                    def _(dve):
                        rank_vector(nc, dve, G1, R1, C, dst, dst_pos)

                    @block.tensor
                    def _(pe):
                        rank_tensor(nc, pe, G1, R1, C)

                    @block.gpsimd
                    def _(pool):
                        scatter_pool(nc, pool, S0, 1, src, dst, src_pos, (R1.s_loaded, 16), rec0)
                        scatter_pool(nc, pool, S1, 2, src, dst, dst_pos, (R1.s_pos_ready, 1), rec1)

        sb = sb_in(outer)
        vec = sb("node_attr", [P, NODE_TILES])
        eps = sb("eps", [P, 1])

        acc_ctx = ExitStack()
        acc_a = sb_in(acc_ctx)("acc_a", [P, NODE_ROWS])
        acc_b = sb_in(acc_ctx)("acc_b", [NV + 1, NODE_ROWS])

        with ExitStack() as ctx:
            sb, ps, sem = sb_in(ctx, "z_"), ps_in(ctx, "z_"), sem_in(ctx, "z_")
            RING = 2 * GPB0
            w_es = sb("w_es", [P, 8, D0])
            w_ex = sb("w_ex", [P, 8, NS + NV])
            w_ey = sb("w_ey", [P, 8, P])
            w_ez = sb("w_ez", [P, 8, NV])
            wb_es = sb("wb_es", [P, 8, NV])
            wb_ez = sb("wb_ez", [P, 8, NS])
            factor = sb("factor", [P, 4])
            vis_start = sb("vis_start", [1, P * G0.cols], i32)
            first_node = sb("first_node", [P, G0.visits])
            win_i = sb("win_i", [1, BATCHES0], i32)
            spread = sb("spread", [P, BATCH0])
            picked = sb("picked", [P, BATCHES0, BATCH0])
            in_bucket = sb("in_bucket", [P, 1])
            rel2 = sb("rel2", [P, BATCHES0])
            rec = sb("rec", [P, RING, VG, REC0])
            xg = sb("xg", [P, RING, VG, D0])
            rel = sb("rel", [P, 2, VG])
            onehot = sb("onehot", [P, 2, BATCH0, 8])
            outer_p = sb("outer_p", [P, 2, VG, 8, 32])
            za = sb("za", [P, 2, 32, P])
            zb = sb("zb", [P, 2, 16, P])
            o_sb = sb("o_sb", [P, 2 * P])
            onehot2 = sb("onehot2", [P, WIN])
            ones = sb("ones", [P, 1])
            begun = sb("begun", [1, 8])
            ps_a = ps("ps_a", [P, 2, VG, 8 * 32])
            ps_b = ps("ps_b", [P, 2, VG, 8 * 16])
            ps_o = ps("ps_o", [P, 512])
            ps_w = ps("ps_w", [P, 4, WIN])
            s_zero, s_w, s_prep, s_dve = (sem(n) for n in ("zero", "w", "prep", "dve"))
            s_rec = [sem(f"rec{i}") for i in range(RING)]
            s_xg = [sem(f"xg{i}") for i in range(RING)]
            s_outer = sem("outer")
            s_z = sem("z")
            s_za, s_zb = sem("za"), sem("zb")
            s_o_ps, s_o = sem("o_ps"), sem("o")
            s_oh2 = sem("oh2")
            s_win = sem("win")
            s_acc = sem("acc")
            s_begun = sem("begun")
            s_tab = sem("tab")
            tab = scratch["tables0"]
            FREE = {"z": RING, "za": 2, "zb": 2, "o_ps": 2, "o": 1, "win": 1, "acc": 2}

            with nc.Block() as block:
                @block.sync
                def _(sp):
                    sp.wait_ge(s_zero, 6)
                    W1, W2, W3, W4 = (A[n] for n in ("W1", "W2", "W3", "W4"))
                    pieces = [(w_es[0:64, :, 0:64], W1), (w_es[64:96, :, 64:96], W4), (w_es[96:128, :, 96:128], W4), (wb_es[96:128, :, :], W4),
                              (w_ex[0:64, :, 64:96], W3), (w_ey[0:64, :, 96:128], W3), (w_ez[0:64, :, :], W3),
                              (w_ex[64:96, :, 0:64], W2), (w_ey[96:128, :, 0:64], W2), (wb_ez[96:128, :, :], W2)]
                    for tile, dram in pieces:
                        sp.dma_start(tile, dram).then_inc(s_w, 16)
                    sp.dma_start(factor[:, :], A["factor0"]).then_inc(s_w, 16)
                    sp.dma_start(vis_start[:, :], tab["start"].rearrange("(o v) -> o v", o=1)).then_inc(s_tab, 16)
                    sp.dma_start(first_node[:, :], tab["bucket"][0:G0.visits].rearrange("(o v) -> o v", o=1).broadcast_to([P, G0.visits])).then_inc(s_tab, 16)
                    sp.dma_start(spread[:, :], A["spread0"]).then_inc(s_tab, 16)
                    sp.dma_start(in_bucket[:, :], A["in_bucket0"]).then_inc(s_tab, 16)
                    sp.wait_ge(s_tab, 64)

                    def group(t, i):
                        n = t * RING + i
                        sp.wait_ge(s_z, n + 1)
                        sp.wait_ge(s_tab, 64)
                        for v in range(VG):
                            row = sp.value_load(vis_start[0:1, bass.ds(n * VG + v, 1)], min_val=0, max_val=N_EDGES)
                            sp.dma_start(rec[:, i, v, :], rec0[bass.ds(row, P), :]).then_inc(s_rec[i], 16)

                    with sp.Fori(0, BATCHES0 // 2) as t:
                        for i in range(RING):
                            group(t, i)

                @block.gpsimd
                def _(pool):
                    for tile in (w_es, w_ex, w_ey, w_ez, wb_es, wb_ez):
                        nc.gpsimd.memset(tile[:], 0.0).then_inc(s_zero, 1)

                    def group(t, i):
                        n = t * RING + i
                        pool.wait_ge(s_z, n + 1)
                        pool.wait_ge(s_rec[i], (t + 1) * (16 * VG))
                        pool.sem_inc(s_begun, 1)
                        for v in range(VG):
                            nc.gpsimd.indirect_dma_start(out=xg[:, i, v, :], out_offset=None, in_=A["x"],
                                                         in_offset=bass.IndirectOffsetOnAxis(ap=rec[:, i, v, REC0 - 1:REC0].bitcast(i32), axis=0)).then_inc(s_xg[i], 16)

                    with pool.Fori(0, BATCHES0 // 2) as t:
                        for i in range(RING):
                            group(t, i)

                @block.vector
                def _(dve):
                    done = [0]

                    def link(ins):
                        done[0] += 1
                        ins.then_inc(s_dve, 1)
                        dve.wait_ge(s_dve, done[0])

                    nc.vector.memset(acc_a[:, :], 0.0).then_inc(s_acc, 1)
                    nc.vector.memset(acc_b[:, :], 0.0).then_inc(s_acc, 1)
                    link(nc.vector.memset(ones[:, :], 1.0))
                    nc.vector.memset(o_sb[:, :], 0.0).then_inc(s_prep, 1)
                    dve.wait_ge(s_w, 16 * 11)
                    for tile, col in ((w_es, 0), (wb_es, 0), (w_ex, 1), (w_ey, 1), (w_ez, 1), (wb_ez, 1)):
                        nc.vector.tensor_scalar(tile[:], tile[:], factor[:, col:col + 1], None, ALU.mult).then_inc(s_prep, 1)
                    dve.wait_ge(s_tab, 64)
                    link(nc.vector.tensor_scalar(first_node[:, :], first_node[:, :], float(G0.width), None, ALU.mult))
                    link(nc.vector.tensor_copy(win_i[:, :], first_node[0:1, ::BATCH0]))
                    link(nc.vector.tensor_tensor(picked[:, :, :], first_node[:, :].rearrange("p (k v) -> p k v", v=BATCH0),
                                                 spread[:, :].unsqueeze(1).broadcast_to([P, BATCHES0, BATCH0]), ALU.mult))
                    link(nc.vector.tensor_reduce(rel2[:, :], picked[:, :, :], AX.X, ALU.add))
                    link(nc.vector.tensor_scalar(rel2[:, :], rel2[:, :], in_bucket[:, 0:1], None, ALU.add))
                    for c, (s, n) in enumerate(((s_z, "z"), (s_za, "za"), (s_zb, "zb"), (s_o_ps, "o_ps"), (s_o, "o"), (s_win, "win"))):
                        nc.vector.memset(begun[:, c:c + 1], 1.0).then_inc(s, FREE[n])
                    first = done[0]

                    def products(t, h, g):
                        i, k = h * GPB0 + g, t * 2 + h
                        n = t * RING + i
                        if g == 0:
                            dve.wait_ge(s_o_ps, k + 1)
                        dve.wait_ge(s_rec[i], (t + 1) * (16 * VG))
                        nc.vector.tensor_tensor(rel[:, g % 2, :], rec[:, i, :, REC0 - 2].bitcast(i32), first_node[:, bass.ds(n * VG, VG)], ALU.subtract).then_inc(s_dve, 1)
                        dve.wait_ge(s_dve, n * 2 + first + 1)
                        oh = onehot[:, h, g * VG:(g + 1) * VG, :]
                        nc.vector.tensor_tensor(oh, iota[:, 0:8].unsqueeze(1).broadcast_to([P, VG, 8]),
                                                rel[:, g % 2, :].unsqueeze(2).broadcast_to([P, VG, 8]), ALU.is_equal).then_inc(s_dve, 1)
                        dve.wait_ge(s_dve, n * 2 + first + 2)
                        dve.wait_ge(s_z, n + (RING - 1))
                        nc.vector.tensor_tensor(outer_p[:, g % 2, :, :, :], oh.unsqueeze(3).broadcast_to([P, VG, 8, 32]),
                                                rec[:, i, :, 0:32].unsqueeze(2).broadcast_to([P, VG, 8, 32]), ALU.mult).then_inc(s_outer, 1)

                    def add_window(k):
                        node = dve.value_load(win_i[0:1, bass.ds(k, 1)], min_val=0, max_val=NODE_ROWS - WIN)
                        dve.wait_ge(s_acc, k * 2 + 2)
                        dve.wait_ge(s_win, k + 2)
                        at = bass.ds(node, WIN)
                        nc.vector.tensor_tensor(acc_a[:, at], acc_a[:, at], ps_w[:, 0, :], ALU.add).then_inc(s_acc, 1)
                        nc.vector.tensor_tensor(acc_b[:, at], acc_b[:, at], ps_w[0:NV + 1, 1, :], ALU.add).then_inc(s_acc, 1)

                    def second_onehot(k):
                        dve.wait_ge(s_win, k + 1)
                        nc.vector.tensor_scalar(onehot2[:, :], iota[:, :], rel2[:, bass.ds(k, 1)], None, ALU.is_equal).then_inc(s_oh2, 1)

                    def batch(t, h, lag1=True, lag2=True):
                        k = t * 2 + h
                        products(t, h, 0)
                        products(t, h, 1)
                        if lag2:
                            add_window(k - 2)
                        if lag1:
                            second_onehot(k - 1)
                        products(t, h, 2)
                        products(t, h, 3)

                    batch(0, 0, False, False)
                    batch(0, 1, True, False)
                    with dve.Fori(1, BATCHES0 // 2) as t:
                        for h in range(2):
                            batch(t, h)
                    add_window(BATCHES0 - 2)
                    second_onehot(BATCHES0 - 1)
                    add_window(BATCHES0 - 1)

                @block.scalar
                def _(act):
                    def evacuate(t, h, g):
                        i, k = h * GPB0 + g, t * 2 + h
                        n = t * RING + i
                        if g == 0:
                            act.wait_ge(s_o_ps, k + 1)
                        act.wait_ge(s_z, n + (RING + 1))
                        rows = slice(g * VG * 8, (g + 1) * VG * 8)
                        nc.scalar.copy(za[:, h, :, rows], ps_a[:, g % 2, :, :].rearrange("p v (m b) -> p b (v m)", b=32)).then_inc(s_za, 1)
                        nc.scalar.copy(zb[:, h, :, rows], ps_b[:, g % 2, :, :].rearrange("p v (m b) -> p b (v m)", b=16)).then_inc(s_zb, 1)

                    def copy_out(k):
                        act.wait_ge(s_win, k + 1)
                        act.wait_ge(s_o_ps, k + 3)
                        nc.scalar.copy(o_sb[:, 0:D0 + 1], ps_o[:, 0:D0 + 1]).then_inc(s_o, 1)

                    def batch(t, h, lag1=True):
                        for g in range(GPB0):
                            evacuate(t, h, g)
                            if g == 1 and lag1:
                                copy_out(t * 2 + h - 1)

                    batch(0, 0, False)
                    batch(0, 1)
                    with act.Fori(1, BATCHES0 // 2) as t:
                        for h in range(2):
                            batch(t, h)
                    copy_out(BATCHES0 - 1)

                @block.tensor
                def _(pe):
                    pe.wait_ge(s_prep, 7)

                    def sums(t, h, g):
                        i = h * GPB0 + g
                        n = t * RING + i
                        pe.wait_ge(s_za, n + 1)
                        pe.wait_ge(s_zb, n + 1)
                        pe.wait_ge(s_xg[i], (t + 1) * (16 * VG))
                        pe.wait_ge(s_outer, n + 1)
                        for v in range(VG):
                            prod = outer_p[:, g % 2, v, :, :]
                            nc.tensor.matmul(ps_a[:, g % 2, v, :], xg[:, i, v, 0:P], prod, start=(v % 2 == 0), stop=(v % 2 == 1))
                            last = nc.tensor.matmul(ps_b[:, g % 2, v, :], xg[:, i, v, NV:NV + P], prod[:, :, 0:16], start=(v == 0), stop=(v == VG - 1))
                        last.then_inc(s_z, 1)

                    def contract(k, h):
                        pe.wait_ge(s_za, k * GPB0 + (GPB0 + FREE["za"]))
                        pe.wait_ge(s_zb, k * GPB0 + (GPB0 + FREE["zb"]))
                        pe.wait_ge(s_o, k + 1)
                        for b in range(8):
                            wide = D0 if b == 0 else P
                            nc.tensor.matmul(ps_o[:, 0:wide], za[:, h, b, :], w_es[:, b, 0:wide], start=(b == 0), stop=False)
                            nc.tensor.matmul(ps_o[:, P:D0], zb[:, h, b, :], wb_es[:, b, :], start=False, stop=False)
                            nc.tensor.matmul(ps_o[:, P:D0], za[:, h, 8 + b, :], w_ez[:, b, :], start=False, stop=False)
                            nc.tensor.matmul(ps_o[:, 0:NS], zb[:, h, 8 + b, :], wb_ez[:, b, :], start=False, stop=False)
                            nc.tensor.matmul(ps_o[:, 0:NS + NV], za[:, h, 16 + b, :], w_ex[:, b, :], start=False, stop=False)
                            nc.tensor.matmul(ps_o[:, 0:P], za[:, h, 24 + b, :], w_ey[:, b, :], start=False, stop=False)
                        nc.tensor.matmul(ps_o[:, D0:D0 + 1], onehot[:, h, :, :].rearrange("p v m -> p (v m)"), ones[:, :], start=False, stop=True).then_inc(s_o_ps, 1)

                    def window(k):
                        pe.wait_ge(s_o, k + 2)
                        pe.wait_ge(s_oh2, k + 1)
                        pe.wait_ge(s_acc, k * 2 + 2)
                        nc.tensor.matmul(ps_w[:, 0, :], o_sb[:, 0:P], onehot2[:, :], start=True, stop=False)
                        nc.tensor.matmul(ps_w[:, 1, :], o_sb[:, P:], onehot2[:, :], start=False, stop=True).then_inc(s_win, 1)

                    def batch(t, h, lag1=True):
                        k = t * 2 + h
                        sums(t, h, 0)
                        sums(t, h, 1)
                        if lag1:
                            contract(k - 1, 1 - h)
                        sums(t, h, 2)
                        sums(t, h, 3)
                        if lag1:
                            window(k - 1)

                    batch(0, 0, False)
                    batch(0, 1)
                    with pe.Fori(1, BATCHES0 // 2) as t:
                        for h in range(2):
                            batch(t, h)
                    contract(BATCHES0 - 1, 1)
                    window(BATCHES0 - 1)

        with ExitStack() as ctx:
            sb, ps, sem = sb_in(ctx, "n_"), ps_in(ctx, "n_"), sem_in(ctx, "n_")
            wm_ta = sb("wm_ta", [P, D0 + 1])
            wm_tb = sb("wm_tb", [NV, D0 + 1])
            wu1_a = sb("wu1_a", [P, D0])
            wu1_b = sb("wu1_b", [NV, D0])
            wu0_a = sb("wu0_a", [P, D0])
            wu0_b = sb("wu0_b", [NV, D0])
            wc_a = sb("wc_a", [P, D0])
            wc_b = sb("wc_b", [NV + 1, D0])
            bu = sb("bu", [P, D0])
            wn_a = sb("wn_a", [P, 2 * D0])
            wn_b = sb("wn_b", [P, 2 * D0])
            factor1 = sb("factor1", [P, 2])
            x = sb("x", [P, 2, D0])
            xt_a = sb("xt_a", [P, 2, P])
            xt_b = sb("xt_b", [NV, 2, P])
            sum_a = sb("sum_a", [P, 2, P])
            sum_b = sb("sum_b", [NV + 1, 2, P])
            y = sb("y", [P, 2, D0])
            stats = sb("stats", [P, 2, 6])
            mean_var = sb("mean_var", [P, 2, 2])
            std = sb("std", [P, 2, 1])
            rstd = sb("rstd", [P, 2, 1])
            x1 = sb("x1", [P, 2, D0])
            x1t = sb("x1t", [P, 2, 2, P])
            f_out = sb("f_out", [P, 2, D0])
            base_out = sb("base_out", [P, 2, D0])
            ps_u = [ps(f"ps_u{r}", [P, 512]) for r in range(2)]
            ps_t = [ps(f"ps_t{r}", [P, 512]) for r in range(2)]
            ps_f = [ps(f"ps_f{r}", [P, 512]) for r in range(2)]
            ps_s = [ps(f"ps_s{r}", [P, 512]) for r in range(2)]
            WEIGHTS = 16 * 17
            s_zero, s_scaled, s_wc_ps, s_wc = (sem(n) for n in ("zero", "scaled", "wc_ps", "wc"))
            s_x = [sem(f"in{r}") for r in range(2)]
            s_sum = sem("sum")
            s_u = sem("u")
            s_y = sem("y")
            s_yb, s_bn, s_var, s_std, s_rstd, s_x1 = (sem(n) for n in ("yb", "bn", "var", "std", "rstd", "x1"))
            s_t, s_x1t = sem("t"), sem("x1t")
            s_f, s_fo, s_bo = sem("f"), sem("fo"), sem("bo")
            s_st = [sem(f"st{r}") for r in range(2)]
            s_w = sem("w")

            with nc.Block() as block:
                @block.sync
                def _(sp):
                    sp.wait_ge(s_zero, 2)
                    WU, WMT = A["Wu"], A["WmT"]
                    pieces = [(wm_ta[:, :], WMT[0:P, :]), (wm_tb[:, :], WMT[P:D0, :]), (wu0_a[:, :], WU[0:P, :]), (wu0_b[:, :], WU[P:D0, :]),
                              (wu1_a[:, :], WU[D0:D0 + P, :]), (wu1_b[:, :], WU[D0 + P:2 * D0, :]),
                              (bu[:, :], A["bu"].rearrange("(o d) -> o d", o=1).broadcast_to([P, D0])),
                              (factor1[:, :], A["factor1"]), (vec[:, :], A["node_vec1"])]
                    for c, (scal, vect) in enumerate((("Wl1_0", "Wl1_1"), ("Wsc0", "Wsc1"))):
                        pieces += [(wn_a[0:64, c * D0:c * D0 + 64], A[scal]), (wn_a[64:96, c * D0 + 64:c * D0 + 96], A[vect]),
                                   (wn_a[96:128, c * D0 + 96:c * D0 + 128], A[vect]), (wn_b[96:128, c * D0 + 128:c * D0 + 160], A[vect])]
                    for tile, dram in pieces:
                        sp.dma_start(tile, dram).then_inc(s_w, 16)

                    def load(i, r):
                        at = bass.ds(i * P, P)
                        sp.dma_start(x[:, r, :], A["x"][at, :]).then_inc(s_x[r], 16)
                        sp.dma_start(xt_a[:, r, :], A["xT"][0:P, at]).then_inc(s_x[r], 16)
                        sp.dma_start(xt_b[:, r, :], A["xT"][P:D0, at]).then_inc(s_x[r], 16)

                    def store(t, r):
                        i = t * 2 + r
                        at = bass.ds(i * P, P)
                        sp.wait_ge(s_fo, i + 1)
                        sp.dma_start(f_tab[at, :], f_out[:, r, :]).then_inc(s_st[r], 16)
                        sp.wait_ge(s_bo, i + 1)
                        sp.dma_start(base_tab[at, :], base_out[:, r, :]).then_inc(s_st[r], 16)

                    for r in range(2):
                        load(r, r)
                    for r in range(2):
                        sp.wait_ge(s_y, 1 + r)
                        load(2 + r, r)
                    with sp.Fori(2, NODE_TILES // 2) as t:
                        for r in range(2):
                            sp.wait_ge(s_y, t * 2 + r - 1)
                            sp.wait_ge(s_u, t * 2 + r - 1)
                            load(t * 2 + r, r)
                            store(t - 2, r)
                    for t in (NODE_TILES // 2 - 2, NODE_TILES // 2 - 1):
                        for r in range(2):
                            store(t, r)
                    for r in range(2):
                        sp.wait_ge(s_st[r], 16 * NODE_TILES)

                @block.gpsimd
                def _(pool):
                    nc.gpsimd.memset(wn_a[:, :], 0.0).then_inc(s_zero, 1)
                    nc.gpsimd.memset(wn_b[:, :], 0.0).then_inc(s_zero, 1)

                    def pick(i, r):
                        at = bass.ds(i * P, P)
                        nc.gpsimd.tensor_copy(sum_a[:, r, :], acc_a[:, at]).then_inc(s_sum, 1)
                        nc.gpsimd.tensor_copy(sum_b[:, r, :], acc_b[:, at]).then_inc(s_sum, 1)

                    for r in range(2):
                        pick(r, r)
                    with pool.Fori(1, NODE_TILES // 2) as t:
                        for r in range(2):
                            pool.wait_ge(s_u, t * 2 + r - 1)
                            pick(t * 2 + r, r)

                @block.vector
                def _(dve):
                    nc.vector.memset(eps[:, :], 1e-5)
                    dve.wait_ge(s_w, WEIGHTS)
                    nc.vector.tensor_scalar(wn_a[:, :], wn_a[:, :], factor1[:, 0:1], None, ALU.mult).then_inc(s_scaled, 1)
                    nc.vector.tensor_scalar(wn_b[:, :], wn_b[:, :], factor1[:, 1:2], None, ALU.mult).then_inc(s_scaled, 1)
                    dve.wait_ge(s_wc_ps, 1)
                    nc.vector.tensor_copy(wc_a[:, :], ps_u[0][:, 0:D0]).then_inc(s_wc, 1)
                    nc.vector.tensor_copy(wc_b[:, :], ps_u[1][0:NV + 1, 0:D0]).then_inc(s_wc, 1)

                    def update(t, r):
                        i = t * 2 + r
                        dve.wait_ge(s_x[r], (t + 1) * 48)
                        dve.wait_ge(s_u, i + 1)
                        nc.vector.scalar_tensor_tensor(y[:, r, :], x[:, r, :], 2.0, ps_u[r][:, 0:D0], ALU.mult, ALU.add).then_inc(s_y, 1)
                        dve.wait_ge(s_y, i + 1)
                        nc.vector.tensor_tensor(y[:, r, :], y[:, r, :], bu[:, :], ALU.add).then_inc(s_yb, 1)
                        dve.wait_ge(s_yb, i + 1)
                        nc.vector.bn_stats(stats[:, r, :], y[:, r, :]).then_inc(s_bn, 1)
                        dve.wait_ge(s_w, WEIGHTS)
                        dve.wait_ge(s_bn, i + 1)
                        nc.vector.bn_aggr(mean_var[:, r, :], stats[:, r, :]).then_inc(s_var, 1)

                    def normalise(j, r):
                        dve.wait_ge(s_std, j + 1)
                        nc.vector.reciprocal(rstd[:, r, :], std[:, r, :]).then_inc(s_rstd, 1)
                        dve.wait_ge(s_rstd, j + 1)
                        nc.vector.tensor_scalar(x1[:, r, :], y[:, r, :], mean_var[:, r, 0:1], rstd[:, r, :], ALU.subtract, ALU.mult).then_inc(s_x1, 1)

                    def residual(t, r, first):
                        j = t * 2 + r
                        dve.wait_ge(s_f, j + 1)
                        if not first:
                            dve.wait_ge(s_st[r], t * 32)
                        nc.vector.scalar_tensor_tensor(base_out[:, r, :], ps_s[r][:, 0:D0], vec[:, bass.ds(j, 1)], x1[:, r, :], ALU.mult, ALU.add).then_inc(s_bo, 1)

                    update(0, 0)
                    update(0, 1)
                    normalise(0, 0)
                    update(1, 0)
                    normalise(1, 1)
                    residual(0, 0, True)
                    update(1, 1)
                    normalise(2, 0)
                    residual(0, 1, True)
                    with dve.Fori(2, NODE_TILES // 2) as t:
                        update(t, 0)
                        normalise(t * 2 - 1, 1)
                        residual(t - 1, 0, False)
                        update(t, 1)
                        normalise(t * 2, 0)
                        residual(t - 1, 1, False)
                    normalise(NODE_TILES - 1, 1)
                    residual(NODE_TILES // 2 - 1, 0, False)
                    residual(NODE_TILES // 2 - 1, 1, False)

                @block.scalar
                def _(act):
                    def deviation(i, r):
                        act.wait_ge(s_var, i + 1)
                        nc.scalar.activation(std[:, r, :], mean_var[:, r, 1:2], ACT.Sqrt, bias=eps[:, :]).then_inc(s_std, 1)

                    def transposed(j, r):
                        act.wait_ge(s_t, j + 1)
                        nc.scalar.copy(x1t[:, r, :, :], ps_t[r][:, 0:2 * P].rearrange("p (a n) -> p a n", a=2)).then_inc(s_x1t, 1)

                    def products(t, r, first):
                        j = t * 2 + r
                        if not first:
                            act.wait_ge(s_st[r], t * 32)
                        act.wait_ge(s_f, j + 1)
                        nc.scalar.activation(f_out[:, r, :], ps_f[r][:, 0:D0], ACT.Copy, scale=vec[:, bass.ds(j, 1)]).then_inc(s_fo, 1)

                    deviation(0, 0)
                    deviation(1, 1)
                    transposed(0, 0)
                    deviation(2, 0)
                    transposed(1, 1)
                    products(0, 0, True)
                    deviation(3, 1)
                    transposed(2, 0)
                    products(0, 1, True)
                    with act.Fori(2, NODE_TILES // 2) as t:
                        deviation(t * 2, 0)
                        transposed(t * 2 - 1, 1)
                        products(t - 1, 0, False)
                        deviation(t * 2 + 1, 1)
                        transposed(t * 2, 0)
                        products(t - 1, 1, False)
                    transposed(NODE_TILES - 1, 1)
                    products(NODE_TILES // 2 - 1, 0, False)
                    products(NODE_TILES // 2 - 1, 1, False)

                @block.tensor
                def _(pe):
                    pe.wait_ge(s_w, WEIGHTS)
                    nc.tensor.matmul(ps_u[0][:, 0:D0], wm_ta[:, 0:P], wu1_a[:, :], start=True, stop=False)
                    nc.tensor.matmul(ps_u[0][:, 0:D0], wm_tb[:, 0:P], wu1_b[:, :], start=False, stop=True)
                    nc.tensor.matmul(ps_u[1][0:NV + 1, 0:D0], wm_ta[:, P:D0 + 1], wu1_a[:, :], start=True, stop=False)
                    nc.tensor.matmul(ps_u[1][0:NV + 1, 0:D0], wm_tb[:, P:D0 + 1], wu1_b[:, :], start=False, stop=True).then_inc(s_wc_ps, 1)
                    pe.wait_ge(s_wc, 2)
                    pe.wait_ge(s_scaled, 2)

                    def update(t, r, first):
                        i = t * 2 + r
                        if not first:
                            pe.wait_ge(s_y, i - 1)
                        pe.wait_ge(s_x[r], (t + 1) * 48)
                        pe.wait_ge(s_sum, i * 2 + 2)
                        nc.tensor.matmul(ps_u[r][:, 0:D0], xt_a[:, r, :], wu0_a[:, :], start=True, stop=False)
                        nc.tensor.matmul(ps_u[r][:, 0:D0], xt_b[:, r, :], wu0_b[:, :], start=False, stop=False)
                        nc.tensor.matmul(ps_u[r][:, 0:D0], sum_a[:, r, :], wc_a[:, :], start=False, stop=False)
                        nc.tensor.matmul(ps_u[r][:, 0:D0], sum_b[:, r, :], wc_b[:, :], start=False, stop=True).then_inc(s_u, 1)

                    def transposes(j, r, first):
                        if not first:
                            pe.wait_ge(s_x1t, j - 1)
                        pe.wait_ge(s_x1, j + 1)
                        nc.tensor.transpose(ps_t[r][:, 0:P], x1[:, r, 0:P], ident[:, :])
                        nc.tensor.transpose(ps_t[r][:, P:2 * P], x1[:, r, NV:D0], ident[:, :]).then_inc(s_t, 1)

                    def products(j, r, first):
                        if not first:
                            pe.wait_ge(s_fo, j - 1)
                            pe.wait_ge(s_bo, j - 1)
                        pe.wait_ge(s_x1t, j + 1)
                        for bank, c in ((ps_f[r], 0), (ps_s[r], D0)):
                            nc.tensor.matmul(bank[:, 0:D0], x1t[:, r, 0, :], wn_a[:, c:c + D0], start=True, stop=False)
                            last = nc.tensor.matmul(bank[:, 0:D0], x1t[:, r, 1, :], wn_b[:, c:c + D0], start=False, stop=True)
                        last.then_inc(s_f, 1)

                    update(0, 0, True)
                    update(0, 1, True)
                    transposes(0, 0, True)
                    update(1, 0, False)
                    transposes(1, 1, True)
                    products(0, 0, True)
                    update(1, 1, False)
                    transposes(2, 0, False)
                    products(1, 1, True)
                    with pe.Fori(2, NODE_TILES // 2) as t:
                        update(t, 0, False)
                        transposes(t * 2 - 1, 1, False)
                        products(t * 2 - 2, 0, False)
                        update(t, 1, False)
                        transposes(t * 2, 0, False)
                        products(t * 2 - 1, 1, False)
                    transposes(NODE_TILES - 1, 1, False)
                    products(NODE_TILES - 2, 0, False)
                    products(NODE_TILES - 1, 1, False)
        acc_ctx.close()

        BUCKETS1 = NODE_TILES * P // G1.width
        W1_ = D0 + 1
        mid_ctx = ExitStack()
        mid = sb_in(mid_ctx)("mid", [P, BUCKETS1, W1_])
        with ExitStack() as ctx:
            sb, ps, sem = sb_in(ctx, "e_"), ps_in(ctx, "e_"), sem_in(ctx, "e_")
            RING = 2 * GPB1
            PAIRS = BATCH1 // 2
            wfc1 = sb("wfc1", [P, PAIRS, P])
            wfc2 = sb("wfc2", [P, 2, 192])
            vis_start = sb("vis_start", [1, P * G1.cols], i32)
            bucket_i = sb("bucket_i", [1, G1.visits], i32)
            first_node = sb("first_node", [P, G1.visits])
            rec = sb("rec", [P, RING, VG, REC1])
            fg = sb("fg", [P, RING, VG, D0])
            rel = sb("rel", [P, 2, VG])
            onehot = sb("onehot", [P, 2, BATCH1, 4, 32])
            onehot_sh = sb("onehot_sh", [P, 2, BATCH1, 4, 32])
            scal = sb("scal", [P, BATCH1, 16])
            scal_t = sb("scal_t", [P, P])
            hidden = sb("hidden", [P, 2, PAIRS, P])
            prod = sb("prod", [P, 2, BATCH1, 2 * D0 + 1])
            ones = sb("ones", [P, 1])
            ps_t = ps("ps_t", [P, 512])
            ps_h = ps("ps_h", [P, PAIRS, P])
            ps_w = ps("ps_w", [P, 2, 512])
            ps_m = ps("ps_m", [P, 4, 512])
            s_zero, s_w, s_prep, s_dve = (sem(n) for n in ("zero", "w", "prep", "dve"))
            s_rec = [sem(f"rec{i}") for i in range(RING)]
            s_fg = [sem(f"fg{i}") for i in range(RING)]
            s_oh = sem("oh")
            s_scal, s_t, s_scal_t, s_h, s_hid = (sem(n) for n in ("scal", "t", "scal_t", "h", "hid"))
            s_wt = sem("wt")
            s_prod = sem("prod")
            s_m = sem("m")
            s_add = sem("add")
            s_begun = sem("begun")
            s_tab = sem("tab")
            tab = scratch["tables1"]

            with nc.Block() as block:
                @block.sync
                def _(sp):
                    sp.wait_ge(s_zero, 2)
                    for v in range(BATCH1):
                        sp.dma_start(wfc1[16 * v:16 * v + 16, v // 2, (v % 2) * 64:(v % 2) * 64 + 64], A["Wfc1"]).then_inc(s_w, 16)
                    for v in range(2):
                        sp.dma_start(wfc2[64 * v:64 * v + 64, v, :], A["Wfc2"]).then_inc(s_w, 16)
                    sp.dma_start(vis_start[:, :], tab["start"].rearrange("(o v) -> o v", o=1)).then_inc(s_tab, 16)
                    sp.dma_start(first_node[:, :], tab["bucket"][0:G1.visits].rearrange("(o v) -> o v", o=1).broadcast_to([P, G1.visits])).then_inc(s_tab, 16)
                    sp.wait_ge(s_tab, 32)

                    def group(t, i, first):
                        n = t * RING + i
                        if not first:
                            sp.wait_ge(s_prod, (n - RING + 1) * 2)
                            sp.wait_ge(s_oh, n - RING + 1)
                            sp.wait_ge(s_scal, t * 2 + (i // GPB1 - 1))
                            sp.wait_ge(s_tab, 32)
                        for v in range(VG):
                            row = sp.value_load(vis_start[0:1, bass.ds(n * VG + v, 1)], min_val=0, max_val=N_EDGES)
                            sp.dma_start(rec[:, i, v, :], rec1[bass.ds(row, P), :]).then_inc(s_rec[i], 16)

                    for i in range(RING):
                        group(0, i, True)
                    with sp.Fori(1, BATCHES1 // 2) as t:
                        for i in range(RING):
                            group(t, i, False)

                @block.gpsimd
                def _(pool):
                    nc.gpsimd.memset(wfc1[:, :, :], 0.0).then_inc(s_zero, 1)
                    nc.gpsimd.memset(wfc2[:, :, :], 0.0).then_inc(s_zero, 1)

                    def group(t, i, first):
                        n = t * RING + i
                        if not first:
                            pool.wait_ge(s_prod, (n - RING + 1) * 2)
                        pool.wait_ge(s_rec[i], (t + 1) * (16 * VG))
                        pool.sem_inc(s_begun, 1)
                        for v in range(VG):
                            nc.gpsimd.indirect_dma_start(out=fg[:, i, v, :], out_offset=None, in_=f_tab,
                                                         in_offset=bass.IndirectOffsetOnAxis(ap=rec[:, i, v, REC1 - 2:REC1 - 1].bitcast(i32), axis=0)).then_inc(s_fg[i], 16)

                    for i in range(RING):
                        group(0, i, True)
                    with pool.Fori(1, BATCHES1 // 2) as t:
                        for i in range(RING):
                            group(t, i, False)

                @block.vector
                def _(dve):
                    nc.vector.memset(mid[:, :, :], 0.0).then_inc(s_add, 2)
                    nc.vector.memset(prod[:, :, :, D0:D0 + 1], 0.0).then_inc(s_prep, 1)
                    nc.vector.memset(ones[:, :], 1.0).then_inc(s_prep, 1)
                    nc.vector.memset(onehot[:, :, :, :, :], 0.0).then_inc(s_prep, 1)
                    dve.wait_ge(s_tab, 32)
                    nc.vector.tensor_copy(bucket_i[:, :], first_node[0:1, :]).then_inc(s_prep, 1)
                    dve.wait_ge(s_prep, 4)
                    nc.vector.tensor_scalar(first_node[:, :], first_node[:, :], float(G1.width), None, ALU.mult).then_inc(s_prep, 1)
                    dve.wait_ge(s_prep, 5)

                    def onehots(t, h, g, first):
                        i, k = h * GPB1 + g, t * 2 + h
                        n = t * RING + i
                        if g == 0 and not first:
                            dve.wait_ge(s_m, (k - 1) * PAIRS)
                        dve.wait_ge(s_rec[i], (t + 1) * (16 * VG))
                        nc.vector.tensor_tensor(rel[:, g, :], rec[:, i, :, REC1 - 1].bitcast(i32), first_node[:, bass.ds(n * VG, VG)], ALU.subtract).then_inc(s_dve, 1)
                        dve.wait_ge(s_dve, n * 2 + 1)
                        oh = onehot[:, h, g * VG:(g + 1) * VG, 3, :]
                        nc.vector.tensor_tensor(oh, iota[:, 0:32].unsqueeze(1).broadcast_to([P, VG, 32]),
                                                rel[:, g, :].unsqueeze(2).broadcast_to([P, VG, 32]), ALU.is_equal).then_inc(s_dve, 1)
                        dve.wait_ge(s_dve, n * 2 + 2)
                        nc.vector.tensor_tensor(onehot_sh[:, h, g * VG:(g + 1) * VG, :, :], oh.unsqueeze(2).broadcast_to([P, VG, 4, 32]),
                                                rec[:, i, :, 16:20].unsqueeze(3).broadcast_to([P, VG, 4, 32]), ALU.mult).then_inc(s_oh, 1)

                    def messages(t, h, j):
                        g, v = j // 2, 2 * (j % 2)
                        i, k = h * GPB1 + g, t * 2 + h
                        m = k * PAIRS + j
                        dve.wait_ge(s_fg[i], (t + 1) * (16 * VG))
                        dve.wait_ge(s_wt, m + 1)
                        w = ps_w[:, j % 2, 0:384].rearrange("p (v w) -> p v w", v=2)
                        f = fg[:, i, v:v + 2, :]
                        to = prod[:, h, 2 * j:2 * j + 2, :]
                        for c, at in ((0, 0), (64, W1_)):
                            nc.vector.tensor_tensor(to[:, :, at:at + NS], w[:, :, c:c + 64], f[:, :, 0:NS], ALU.mult)
                        for c, at in ((128, NS), (160, W1_ + NS)):
                            last = nc.vector.tensor_tensor(to[:, :, at:at + 3 * NV].rearrange("p v (i u) -> p v i u", u=NV),
                                                           w[:, :, c:c + NV].unsqueeze(2).broadcast_to([P, 2, 3, NV]),
                                                           f[:, :, NS:D0].rearrange("p v (i u) -> p v i u", u=NV), ALU.mult)
                        last.then_inc(s_prod, 1)

                    def add(k, j):
                        for v in range(2):
                            b = 2 * (j % 2) + v
                            no = (k * PAIRS + j) * 2 + v
                            bucket = dve.value_load(bucket_i[0:1, bass.ds(no, 1)], min_val=0, max_val=G1.buckets - 1)
                            at = bass.ds(bucket, 1)
                            dve.wait_ge(s_add, no * 2 + 2)
                            dve.wait_ge(s_m, k * PAIRS + j + 1)
                            nc.vector.tensor_tensor(mid[0:96, at, 0:D0], mid[0:96, at, 0:D0], ps_m[0:96, b, W1_:W1_ + D0].unsqueeze(1), ALU.add).then_inc(s_add, 1)
                            nc.vector.tensor_tensor(mid[96:128, at, :], mid[96:128, at, :], ps_m[96:128, b, 0:W1_].unsqueeze(1), ALU.add).then_inc(s_add, 1)

                    def batch(t, h, lag1=True, lag2=True, first=False):
                        k = t * 2 + h
                        t1 = t if h == 1 else t - 1
                        if lag1:
                            for g in range(GPB1):
                                onehots(t1, 1 - h, g, first)
                        for j in range(PAIRS):
                            if lag1:
                                messages(t1, 1 - h, j)
                            if lag2 and j >= 1:
                                add(k - 2, j - 1)
                        if lag2:
                            add(k - 2, PAIRS - 1)

                    batch(0, 1, True, False, True)
                    batch(1, 0, True, True, True)
                    batch(1, 1)
                    with dve.Fori(2, BATCHES1 // 2) as t:
                        for h in range(2):
                            batch(t, h)
                    for g in range(GPB1):
                        onehots(BATCHES1 // 2 - 1, 1, g, False)
                    for j in range(PAIRS):
                        messages(BATCHES1 // 2 - 1, 1, j)
                        add(BATCHES1 - 2, j)
                    for j in range(PAIRS):
                        add(BATCHES1 - 1, j)

                @block.scalar
                def _(act):
                    def batch(t, h, first, early=False):
                        k = t * 2 + h
                        for g in range(GPB1):
                            act.wait_ge(s_rec[h * GPB1 + g], (t + 1) * (16 * VG))
                        if not first:
                            act.wait_ge(s_t, k)
                        nc.scalar.copy(scal[:, :, :].rearrange("p (g v) a -> p g v a", g=GPB1), rec[:, h * GPB1:(h + 1) * GPB1, :, 0:16]).then_inc(s_scal, 1)
                        if not first:
                            act.wait_ge(s_h, k)
                        act.wait_ge(s_t, k + 1)
                        nc.scalar.copy(scal_t[:, :], ps_t[:, 0:P]).then_inc(s_scal_t, 1)
                        if not early:
                            act.wait_ge(s_wt, (k - 1) * PAIRS)
                        act.wait_ge(s_h, k + 1)
                        nc.scalar.activation(hidden[:, h, :, :], ps_h[:, :, :], ACT.Silu, scale=0.25).then_inc(s_hid, 1)

                    batch(0, 0, True, True)
                    batch(0, 1, False, True)
                    with act.Fori(1, BATCHES1 // 2) as t:
                        for h in range(2):
                            batch(t, h, False)

                @block.tensor
                def _(pe):
                    pe.wait_ge(s_w, 160)
                    pe.wait_ge(s_prep, 5)

                    def transposed(k, first):
                        pe.wait_ge(s_scal, k + 1)
                        if not first:
                            pe.wait_ge(s_scal_t, k)
                        nc.tensor.transpose(ps_t[:, 0:P], scal[:, :, :].rearrange("p v a -> p (v a)"), ident[:, :]).then_inc(s_t, 1)

                    def hidden_layer(k, first):
                        if not first:
                            pe.wait_ge(s_hid, k)
                        pe.wait_ge(s_scal_t, k + 1)
                        for j in range(PAIRS):
                            last = nc.tensor.matmul(ps_h[:, j, :], wfc1[:, j, :], scal_t[:, :], start=(j == 0), stop=(j == PAIRS - 1))
                        last.then_inc(s_h, 1)

                    def edge_weights(k, h, j, first):
                        if j == 0:
                            pe.wait_ge(s_hid, k + 1)
                        if not first or j >= 2:
                            pe.wait_ge(s_prod, k * PAIRS + j - 1)
                        nc.tensor.matmul(ps_w[:, j % 2, 0:384], hidden[:, h, j, :], wfc2[:, :, :].rearrange("p v w -> p (v w)"), start=True, stop=True).then_inc(s_wt, 1)

                    def node_sums(k, h, j, first):
                        m = k * PAIRS + j
                        if j == 0:
                            pe.wait_ge(s_oh, (k + 1) * GPB1)
                        pe.wait_ge(s_prod, m + 1)
                        if not first or j >= 2:
                            pe.wait_ge(s_add, (m - 1) * 4 + 2)
                        for v in range(2):
                            b, at = 2 * (j % 2) + v, 2 * j + v
                            nc.tensor.matmul(ps_m[:, b, 0:2 * D0 + 1], onehot_sh[:, h, at, :, :].rearrange("p c m -> p (c m)"), prod[:, h, at, :], start=True, stop=False)
                            last = nc.tensor.matmul(ps_m[:, b, D0:D0 + 1], onehot[:, h, at, :, :].rearrange("p c m -> p (c m)"), ones[:, :], start=False, stop=True)
                        last.then_inc(s_m, 1)

                    def batch(t, h, lag1=True, lag2=True, first1=False, first2=False):
                        k = t * 2 + h
                        transposed(k, not lag1)
                        for j in range(PAIRS):
                            if lag1:
                                edge_weights(k - 1, 1 - h, j, first1)
                            if lag2:
                                node_sums(k - 2, h, j, first2)
                            if j == 0:
                                hidden_layer(k, not lag1)

                    batch(0, 0, False, False)
                    batch(0, 1, True, False, True)
                    batch(1, 0, True, True, False, True)
                    batch(1, 1)
                    with pe.Fori(2, BATCHES1 // 2) as t:
                        for h in range(2):
                            batch(t, h)
                    for j in range(PAIRS):
                        edge_weights(BATCHES1 - 1, 1, j, False)
                        node_sums(BATCHES1 - 2, 0, j, False)
                    for j in range(PAIRS):
                        node_sums(BATCHES1 - 1, 1, j, False)

        with ExitStack() as ctx:
            sb, ps, sem = sb_in(ctx, "f_"), ps_in(ctx, "f_"), sem_in(ctx, "f_")
            CX, CY, CZ, C0, CB0, CBZ = range(6)
            OUT = D0 + 2
            wl2 = sb("wl2", [P, 6, OUT])
            factor2 = sb("factor2", [P, 6])
            cur = sb("cur", [P, 2, 4, W1_])
            ta = sb("ta", [P, 2, 4, 4, 32])
            tb = sb("tb", [P, 2, 4, 4, 32])
            base = sb("base", [P, 2, D0])
            count = sb("count", [P, 2, 4])
            y = sb("y", [P, 2, D0])
            stats = sb("stats", [P, 2, 6])
            mean_var = sb("mean_var", [P, 2, 2])
            std = sb("std", [P, 2, 1])
            rstd = sb("rstd", [P, 2, 1])
            x2 = sb("x2", [P, 2, D0])
            ps_ta = [ps(f"ps_ta{r}", [P, 512]) for r in range(2)]
            ps_tb = [ps(f"ps_tb{r}", [P, 512]) for r in range(2)]
            ps_o = [ps(f"ps_o{r}", [P, 512]) for r in range(2)]
            WEIGHTS = 16 * 16
            s_zero, s_scaled, s_cur, s_t, s_ta, s_o = (sem(n) for n in ("zero", "scaled", "cur", "t", "ta", "o"))
            s_c1, s_c2, s_c3, s_c4, s_y, s_bn, s_var, s_std, s_rstd, s_x2 = (sem(n) for n in ("c1", "c2", "c3", "c4", "y", "bn", "var", "std", "rstd", "x2"))
            s_base = [sem(f"base{r}") for r in range(2)]
            s_out = [sem(f"out{r}") for r in range(2)]
            s_w = sem("w")
            MORE = P - NV - 1

            with nc.Block() as block:
                @block.sync
                def _(sp):
                    sp.wait_ge(s_zero, 1)
                    S_, V_, A_ = A["Wl2_s"], A["Wl2_v"], A["Wa"]
                    al = D0
                    pieces = [(wl2[0:64, C0, 0:64], S_[0:64, :]), (wl2[0:64, C0, al:al + 1], A_[0:64, :]),
                              (wl2[64:96, C0, 64:96], V_[64:96, :]), (wl2[96:128, C0, 96:128], V_[64:96, :]),
                              (wl2[0:64, CX, 64:96], V_[0:64, :]), (wl2[64:96, CX, 0:64], S_[64:96, :]), (wl2[64:96, CX, al:al + 1], A_[64:96, :]),
                              (wl2[0:64, CY, 96:128], V_[0:64, :]), (wl2[96:128, CY, 0:64], S_[64:96, :]), (wl2[96:128, CY, al:al + 1], A_[64:96, :]),
                              (wl2[0:64, CZ, 128:160], V_[0:64, :]),
                              (wl2[MORE:MORE + NV, CB0, 128:160], V_[64:96, :]), (wl2[P - 1:P, CB0, al + 1:al + 2], A["ident"][0:1, 0:1]),
                              (wl2[MORE:MORE + NV, CBZ, 0:64], S_[64:96, :]), (wl2[MORE:MORE + NV, CBZ, al:al + 1], A_[64:96, :]),
                              (factor2[:, :], A["factor2"])]
                    for tile, dram in pieces:
                        sp.dma_start(tile, dram).then_inc(s_w, 16)

                    def load(i, r):
                        sp.dma_start(base[:, r, :], base_tab[bass.ds(i * P, P), :]).then_inc(s_base[r], 16)

                    def store(i, r):
                        sp.wait_ge(s_x2, i + 1)
                        sp.dma_start(out[bass.ds(i * P, P), :], x2[:, r, :]).then_inc(s_out[r], 16)

                    for r in range(2):
                        load(r, r)
                    with sp.Fori(1, NODE_TILES // 2) as t:
                        for r in range(2):
                            sp.wait_ge(s_y, t * 2 + r - 1)
                            load(t * 2 + r, r)
                            store(t * 2 + r - 2, r)
                    for r in range(2):
                        store(NODE_TILES - 2 + r, r)
                    for r in range(2):
                        sp.wait_ge(s_out[r], 16 * (NODE_TILES // 2))

                @block.gpsimd
                def _(pool):
                    nc.gpsimd.memset(wl2[:, :, :], 0.0).then_inc(s_zero, 1)

                    def pick(i, r):
                        nc.gpsimd.tensor_copy(cur[:, r, :, :], mid[:, bass.ds(i * 4, 4), :]).then_inc(s_cur, 1)

                    for r in range(2):
                        pick(r, r)
                    with pool.Fori(1, NODE_TILES // 2) as t:
                        for r in range(2):
                            pool.wait_ge(s_t, t * 2 + r - 1)
                            pick(t * 2 + r, r)

                @block.vector
                def _(dve):
                    dve.wait_ge(s_w, WEIGHTS)
                    nc.vector.tensor_tensor(wl2[:, :, :], wl2[:, :, :], factor2[:, :].unsqueeze(2).broadcast_to([P, 6, OUT]), ALU.mult).then_inc(s_scaled, 1)

                    def finish(t, r, first):
                        i = t * 2 + r
                        dve.wait_ge(s_o, i + 1)
                        c = count[:, r, :]
                        nc.vector.tensor_scalar(c[:, 0:1], ps_o[r][:, D0 + 1:D0 + 2], 1.0, None, ALU.max).then_inc(s_c1, 1)
                        dve.wait_ge(s_c1, i + 1)
                        nc.vector.reciprocal(c[:, 1:2], c[:, 0:1]).then_inc(s_c2, 1)
                        dve.wait_ge(s_c2, i + 1)
                        nc.vector.tensor_scalar(c[:, 2:3], c[:, 1:2], vec[:, bass.ds(i, 1)], None, ALU.mult).then_inc(s_c3, 1)
                        dve.wait_ge(s_c3, i + 1)
                        nc.vector.tensor_scalar(c[:, 3:4], ps_o[r][:, D0:D0 + 1], c[:, 2:3], c[:, 2:3], ALU.mult, ALU.mult).then_inc(s_c4, 1)
                        dve.wait_ge(s_c4, i + 1)
                        dve.wait_ge(s_base[r], (t + 1) * 16)
                        nc.vector.scalar_tensor_tensor(y[:, r, :], ps_o[r][:, 0:D0], c[:, 3:4], base[:, r, :], ALU.mult, ALU.add).then_inc(s_y, 1)
                        dve.wait_ge(s_y, i + 1)
                        nc.vector.bn_stats(stats[:, r, :], y[:, r, :]).then_inc(s_bn, 1)
                        dve.wait_ge(s_w, WEIGHTS)
                        dve.wait_ge(s_bn, i + 1)
                        nc.vector.bn_aggr(mean_var[:, r, :], stats[:, r, :]).then_inc(s_var, 1)

                    def normalise(t, r, first):
                        j = t * 2 + r
                        dve.wait_ge(s_std, j + 1)
                        nc.vector.reciprocal(rstd[:, r, :], std[:, r, :]).then_inc(s_rstd, 1)
                        if not first:
                            dve.wait_ge(s_out[r], t * 16)
                        dve.wait_ge(s_rstd, j + 1)
                        nc.vector.tensor_scalar(x2[:, r, :], y[:, r, :], mean_var[:, r, 0:1], rstd[:, r, :], ALU.subtract, ALU.mult).then_inc(s_x2, 1)

                    finish(0, 0, True)
                    finish(0, 1, True)
                    normalise(0, 0, True)
                    finish(1, 0, False)
                    normalise(0, 1, True)
                    finish(1, 1, False)
                    with dve.Fori(2, NODE_TILES // 2) as t:
                        for r in range(2):
                            normalise(t - 1, r, False)
                            finish(t, r, False)
                    for r in range(2):
                        normalise(NODE_TILES // 2 - 1, r, False)

                @block.scalar
                def _(act):
                    def features(i, r, first):
                        if not first:
                            act.wait_ge(s_o, i - 1)
                        act.wait_ge(s_t, i + 1)
                        for dst_t, src_t in ((ta, ps_ta), (tb, ps_tb)):
                            nc.scalar.copy(dst_t[:, r, :, :, :], src_t[r][:, :].rearrange("p (q c n) -> p c q n", q=4, c=4)).then_inc(s_ta, 1)

                    def deviation(j, r):
                        act.wait_ge(s_var, j + 1)
                        nc.scalar.activation(std[:, r, :], mean_var[:, r, 1:2], ACT.Sqrt, bias=eps[:, :]).then_inc(s_std, 1)

                    features(0, 0, True)
                    features(1, 1, True)
                    deviation(0, 0)
                    with act.Fori(1, NODE_TILES // 2) as t:
                        features(t * 2, 0, False)
                        deviation(t * 2 - 1, 1)
                        features(t * 2 + 1, 1, False)
                        deviation(t * 2, 0)
                    deviation(NODE_TILES - 1, 1)

                @block.tensor
                def _(pe):
                    pe.wait_ge(s_scaled, 1)

                    def transposes(i, r, first):
                        if not first:
                            pe.wait_ge(s_ta, i * 2 - 2)
                        pe.wait_ge(s_cur, i + 1)
                        for q in range(4):
                            nc.tensor.transpose(ps_ta[r][:, q * P:(q + 1) * P], cur[:, r, q, 0:P], ident[:, :])
                            last = nc.tensor.transpose(ps_tb[r][:, q * P:(q + 1) * P], cur[:, r, q, W1_ - P:W1_], ident[:, :])
                        last.then_inc(s_t, 1)

                    def products(i, r, first):
                        if not first:
                            pe.wait_ge(s_y, i - 1)
                        pe.wait_ge(s_ta, i * 2 + 2)
                        for c in range(4):
                            nc.tensor.matmul(ps_o[r][:, 0:OUT], ta[:, r, c, :, :].rearrange("p q n -> p (q n)"), wl2[:, c, :], start=(c == 0), stop=False)
                        nc.tensor.matmul(ps_o[r][:, 0:OUT], tb[:, r, C0, :, :].rearrange("p q n -> p (q n)"), wl2[:, CB0, :], start=False, stop=False)
                        nc.tensor.matmul(ps_o[r][:, 0:OUT], tb[:, r, CZ, :, :].rearrange("p q n -> p (q n)"), wl2[:, CBZ, :], start=False, stop=True).then_inc(s_o, 1)

                    transposes(0, 0, True)
                    transposes(1, 1, True)
                    products(0, 0, True)
                    transposes(2, 0, False)
                    products(1, 1, True)
                    transposes(3, 1, False)
                    with pe.Fori(2, NODE_TILES // 2) as t:
                        products(t * 2 - 2, 0, False)
                        transposes(t * 2, 0, False)
                        products(t * 2 - 1, 1, False)
                        transposes(t * 2 + 1, 1, False)
                    products(NODE_TILES - 2, 0, False)
                    products(NODE_TILES - 1, 1, False)
        mid_ctx.close()



def _vectors_by_component(n):
    import numpy as np
    return np.concatenate([np.arange(64), 64 + 3 * np.arange(n)[None, :].repeat(3, 0).reshape(3, n).ravel() + np.repeat(np.arange(3), n)])


def kernel(**inputs):
    import numpy as np
    import concourse.bacc as bacc
    from concourse import mybir as my
    from concourse.bass_utils import run_bass_kernel_spmd

    G0, G1 = Grouping("src", 3, 32), Grouping("dst", 5, 32)
    a = {k: np.asarray(v) for k, v in inputs.items()}
    cols = _vectors_by_component(32)

    def pad(v, rows, value=0):
        return np.concatenate([v, np.full((rows - v.shape[0],) + v.shape[1:], value, v.dtype)])

    x = np.ascontiguousarray(pad(a["x"][:, cols], NODE_ROWS))
    edge_cols = np.concatenate([np.arange(8)] + [8 + 3 * np.arange(8) + c for c in (2, 0, 1)])
    Wu = a["L0_gnn_Wu"]
    arrays = {
        "src": pad(a["src"], SLOTS, PAD_NODE).reshape(P, TILES),
        "dst": pad(a["dst"], SLOTS, PAD_NODE).reshape(P, TILES),
        "edge_attr_32": pad(a["edge_attr_32"][:, edge_cols], SLOTS).reshape(P, TILES, 32),
        "edge_attr_16": pad(a["edge_attr_16"], SLOTS).reshape(P, TILES, 16),
        "edge_attr_4": pad(a["edge_attr_4"][:, [1, 2, 3, 0]], SLOTS).reshape(P, TILES, 4),
        "x": x,
        "xT": np.ascontiguousarray(x.T),
        "node_vec1": np.ascontiguousarray(pad(a["node_vec1"][:, 0], NODE_ROWS).reshape(NODE_TILES, P).T),
        "WmT": np.ascontiguousarray(np.concatenate([a["L0_gnn_Wm"][cols], a["L0_gnn_bm"][None]]).T),
        "Wu": np.ascontiguousarray(np.concatenate([Wu[:160][cols], Wu[160:]])[:, cols]),
        "bu": a["L0_gnn_bu"][cols],
        **{n: a["L0_gnn_" + n] for n in ("W1", "W2", "W3", "W4")},
        **{n: a["L1_gnn_" + n] for n in ("Wfc1", "Wfc2", "Wsc0", "Wsc1", "Wl1_0", "Wl1_1", "Wl2_s", "Wl2_v", "Wa")},
    }
    arrays.update(rank_constants([G0, G1]))
    k = np.arange(P)
    half = 2.0 ** -0.5
    f0 = np.zeros((P, 4))
    f0[:, 0] = np.where(k < 64, 512 ** -0.5, 256 ** -0.5) * half
    f0[:, 1] = np.where(k < 64, 512 ** -0.5, 768 ** -0.5) * half
    arrays["factor0"] = f0.astype(np.float32)
    arrays["spread0"] = ((k[:, None] // 8 == np.arange(16)).astype(np.float32) - (np.arange(16) == 0)).astype(np.float32)
    arrays["in_bucket0"] = (k % 8).astype(np.float32).reshape(P, 1)
    arrays["factor1"] = np.stack([np.where(k < 64, 64 ** -0.5, 32 ** -0.5), np.full(P, 32 ** -0.5)], 1).astype(np.float32)
    f2 = np.full((P, 6), 96 ** -0.5 / 8)
    f2[64:, 0] *= 3 ** -0.5
    f2[64:, 1] *= 3 ** -0.5
    f2[:, 5] *= 3 ** -0.5
    f2[P - 1, 4] = 1.0
    arrays["factor2"] = f2.astype(np.float32)

    nc = bacc.Bacc("TRN2", target_bir_lowering=False, num_devices=1)
    f32, int32 = my.dt.float32, my.dt.int32
    A, given = {"groupings": (G0, G1)}, {}
    for n, v in arrays.items():
        v = np.ascontiguousarray(v)
        given["in_" + n] = v
        A[n] = nc.dram_tensor("in_" + n, v.shape, my.dt.from_np(v.dtype), kind="ExternalInput").ap()

    def scratch(n, shape, dt=f32):
        return nc.dram_tensor(n, shape, dt, kind="Internal").ap()

    def tables(g):
        return {"vb": scratch(f"{g.name}_vb", (1024,)), "s": scratch(f"{g.name}_s", (1024,)),
                "bucket": scratch(f"{g.name}_bucket", (P * g.cols,)), "start": scratch(f"{g.name}_start", (P * g.cols,), int32)}

    S = {"rec0": scratch("rec0", (SLOTS, 34)), "rec1": scratch("rec1", (SLOTS, 22)), "f": scratch("f", (NODE_ROWS, 160)),
         "base": scratch("base", (NODE_ROWS, 160)), "tables0": tables(G0), "tables1": tables(G1)}
    out = nc.dram_tensor("out", (NODE_ROWS, 160), f32, kind="ExternalOutput").ap()
    gnn_kernel(nc, A, out, S)
    r = run_bass_kernel_spmd(nc, [given], core_ids=[0])
    got = r.results[0]["out"]
    back = np.empty(160, np.int64)
    back[cols] = np.arange(160)
    return np.ascontiguousarray(got[:N_NODES][:, back])
```

```python
import concourse.bass as bass
from concourse import mybir
from contextlib import ExitStack
import numpy as np

fp32 = mybir.dt.float32
bf16 = mybir.dt.bfloat16
i32 = mybir.dt.int32
ALU = mybir.AluOpType
ACT = mybir.ActivationFunctionType
AX = mybir.AxisListType

P = 128
N_NODES = 6250
N_EDGES = 200000
GROUPS = 16
TILES = 1568
STEPS = TILES // GROUPS
SLOTS = P * TILES
NODE_TILES = 50
NODE_ROWS = NODE_TILES * P
PAD_NODE = NODE_ROWS - 1
DIGIT = 32


class Grouping:

    def __init__(self, name, shift, per_step):
        self.name, self.shift = name, shift
        self.width = 1 << shift
        self.buckets = -(-N_NODES // self.width)
        most = self.buckets + N_EDGES // P
        self.visits = -(-most // per_step) * per_step
        self.cols = -(-self.visits // P)


class Rank:
    pass


def alloc_rank(ctx, nc, g):
    R = Rank()

    def sb(n, s, d=fp32):
        return ctx.enter_context(nc.sbuf_tensor(f"{g.name}_{n}", s, d))

    def ps(n, s, d=fp32):
        return ctx.enter_context(nc.psum_tensor(f"{g.name}_{n}", s, d))

    def sem(n):
        return ctx.enter_context(nc.semaphore(f"{g.name}_{n}"))

    R.digit_i = sb("digit_i", [P, TILES], i32)
    R.digits = sb("digits", [P, 2, TILES], bf16)
    R.onehot = sb("onehot", [P, 2, 2, GROUPS, DIGIT], bf16)
    R.hi_t = sb("hi_t", [P, 4, P], bf16)
    R.hi_t32 = sb("hi_t32", [P, 4, P])
    R.earlier = sb("earlier", [P, GROUPS, P], bf16)
    R.count = sb("count", [P, 4, 4, DIGIT])
    R.fresh = sb("fresh", [P, 4, 4, DIGIT])
    R.by_group = sb("by_group", [P, 4, DIGIT])
    R.picked = sb("picked", [P, GROUPS, DIGIT])
    R.pos_f = sb("pos_f", [P, TILES])
    R.small = sb("small", [P, 16, DIGIT])
    R.small_i = sb("small_i", [P, 2, DIGIT], i32)
    R.vb_row = sb("vb_row", [P, g.buckets])
    R.s_row = sb("s_row", [P, g.buckets])
    R.ds_row = sb("ds_row", [P, g.buckets])
    R.mask = sb("mask", [P, g.buckets])
    R.junk = sb("junk", [P, g.buckets])
    R.ones = sb("ones", [P, max(g.buckets, DIGIT)])
    R.vtab = sb("vtab", [P, 4, g.cols])
    R.vtab_i = sb("vtab_i", [P, g.cols], i32)
    R.ps_t = ps("ps_t", [P, 4, P], bf16)
    R.ps_eq = ps("ps_eq", [P, GROUPS, P])
    R.ps_g = ps("ps_g", [P, GROUPS, DIGIT])
    R.ps_h = ps("ps_h", [P, 4, 4, DIGIT])
    R.ps_s = ps("ps_s", [P, 3 * DIGIT])
    R.s_onehot_ready = sem("onehot_ready")
    R.s_onehot_counted = sem("onehot_counted")
    R.s_counted = sem("counted")
    R.s_sums_ready = sem("sums_ready")
    R.s_sums_done = sem("sums_done")
    R.s_hi_t_ps = sem("hi_t_ps")
    R.s_hi_t_ready = sem("hi_t_ready")
    R.s_eq_ps = sem("eq_ps")
    R.s_earlier_ready = sem("earlier_ready")
    R.s_hist_ps = sem("hist_ps")
    R.s_count_ready = sem("count_ready")
    R.s_rank_ps = sem("rank_ps")
    R.s_rank_read = sem("rank_read")
    R.s_dve = sem("dve")
    R.s_tables_ready = sem("tables_ready")
    R.s_tables_out = sem("tables_out")
    R.s_rows_in = sem("rows_in")
    R.s_visits_ready = sem("visits_ready")
    R.s_visits_out = sem("visits_out")
    R.s_pos_ready = sem("pos_ready")
    return R


def rank_vector(nc, dve, g, R, C, node, s_node, pos):
    done = [0]

    def link(ins):
        done[0] += 1
        ins.then_inc(R.s_dve, 1)
        dve.wait_ge(R.s_dve, done[0])

    link(nc.vector.memset(R.ones[:, :], 1.0))
    dve.wait_ge(s_node, 16)
    link(nc.vector.tensor_scalar(R.digit_i[:, :], node[:, :], g.shift + 5, None, ALU.logical_shift_right))
    link(nc.vector.tensor_copy(R.digits[:, 0, :], R.digit_i[:, :]))
    link(nc.vector.tensor_scalar(R.digit_i[:, :], node[:, :], g.shift, DIGIT - 1, ALU.logical_shift_right, ALU.bitwise_and))
    link(nc.vector.tensor_copy(R.digits[:, 1, :], R.digit_i[:, :]))

    def onehots(step, par):
        return nc.vector.tensor_tensor(
            R.onehot[:, par, :, :, :],
            R.digits[:, :, bass.ds(step * GROUPS, GROUPS)].unsqueeze(3).broadcast_to([P, 2, GROUPS, DIGIT]),
            C["iota"][:, 0:DIGIT].unsqueeze(1).unsqueeze(1).broadcast_to([P, 2, GROUPS, DIGIT]),
            ALU.is_equal)

    for par in range(2):
        onehots(par, par).then_inc(R.s_onehot_ready, 1)
    with dve.Fori(1, STEPS // 2) as t:
        for par in range(2):
            dve.wait_ge(R.s_onehot_counted, t * 2 + par - 1)
            onehots(t * 2 + par, par).then_inc(R.s_onehot_ready, 1)

    small = R.small
    dve.wait_ge(R.s_counted, 1)
    own = C["own_group"].unsqueeze(1).broadcast_to([P, 4, 4, DIGIT])
    link(nc.vector.tensor_tensor(R.fresh[:, :, :, :], R.ps_h[:, :, :, :], own, ALU.mult))
    link(nc.vector.tensor_reduce(R.by_group[:, :, :], R.fresh[:, :, :, :].rearrange("p q g l -> p q l g"), AX.X, ALU.add))
    nc.vector.tensor_reduce(small[:, 0, :], R.by_group[:, :, :].rearrange("p q l -> p l q"), AX.X, ALU.add).then_inc(R.s_sums_ready, 1)
    dve.wait_ge(R.s_sums_done, 1)
    link(nc.vector.tensor_copy(small[:, 1:3, :], R.ps_s[:, 0:2 * DIGIT].rearrange("p (a l) -> p a l", l=DIGIT)))
    link(nc.vector.tensor_tensor_scan(small[:, 3, :], R.ones[:, 0:DIGIT], small[:, 1, :], 0.0, ALU.mult, ALU.add))
    link(nc.vector.tensor_scalar(small[:, 4, :], small[:, 1, :], float(P - 1), None, ALU.add))
    link(nc.vector.tensor_copy(R.small_i[:, 0, :], small[:, 4, :]))
    link(nc.vector.tensor_scalar(R.small_i[:, 1, :], R.small_i[:, 0, :], 7, None, ALU.logical_shift_right))
    link(nc.vector.tensor_copy(small[:, 5, :], R.small_i[:, 1, :]))
    link(nc.vector.tensor_scalar(small[:, 6, :], small[:, 5, :], 1.0, None, ALU.max))
    link(nc.vector.tensor_tensor_scan(small[:, 7, :], R.ones[:, 0:DIGIT], small[:, 6, :], 0.0, ALU.mult, ALU.add))
    link(nc.vector.tensor_copy(small[:, 8, 0:1], small[:, 3, DIGIT - 1:DIGIT]))
    nc.vector.tensor_copy(small[:, 8, 1:2], small[:, 7, DIGIT - 1:DIGIT]).then_inc(R.s_sums_ready, 1)
    dve.wait_ge(R.s_sums_done, 2)
    link(nc.vector.tensor_copy(small[:, 8, 2:4], R.ps_s[:, 2 * DIGIT:2 * DIGIT + 2]))
    link(nc.vector.tensor_tensor(small[:, 9, :], small[:, 3, :], small[:, 1, :], ALU.subtract))
    link(nc.vector.tensor_scalar(small[:, 9, :], small[:, 9, :], small[:, 8, 2:3], None, ALU.add))
    link(nc.vector.tensor_tensor(small[:, 10, :], small[:, 7, :], small[:, 6, :], ALU.subtract))
    link(nc.vector.tensor_scalar(small[:, 10, :], small[:, 10, :], small[:, 8, 3:4], None, ALU.add))
    nc.vector.scalar_tensor_tensor(small[:, 11, :], small[:, 10, :], -float(P), small[:, 9, :], ALU.mult, ALU.add).then_inc(R.s_tables_ready, 1)
    link(nc.vector.tensor_tensor(small[:, 13, :], small[:, 9, :], small[:, 2, :], ALU.add))
    for q in range(4):
        last = nc.vector.tensor_tensor(R.count[:, q, :, :], C["own_group"], small[:, 13, :].unsqueeze(1).broadcast_to([P, 4, DIGIT]), ALU.mult)
        if q < 3:
            link(last)
            link(nc.vector.tensor_tensor(small[:, 13, :], small[:, 13, :], R.by_group[:, q, :], ALU.add))
    last.then_inc(R.s_count_ready, 1)
    for par in range(2):
        onehots(par, par).then_inc(R.s_onehot_ready, 1)

    first = done[0]
    per_step = 2

    def place(step, par):
        base = step * per_step + first
        dve.wait_ge(R.s_hist_ps, step + 1)
        nc.vector.tensor_tensor(R.fresh[:, :, :, :], R.ps_h[:, :, :, :], own, ALU.mult).then_inc(R.s_dve, 1)
        dve.wait_ge(R.s_rank_ps, step + 1)
        nc.vector.tensor_tensor(R.picked[:, :, :], R.ps_g[:, :, :], R.onehot[:, par, 1, :, :], ALU.mult).then_inc(R.s_dve, 1)
        dve.wait_ge(R.s_dve, base + 1)
        nc.vector.tensor_tensor(R.count[:, :, :, :], R.count[:, :, :, :], R.fresh[:, :, :, :], ALU.add).then_inc(R.s_count_ready, 1)
        dve.wait_ge(R.s_dve, base + 2)
        nc.vector.tensor_reduce(R.pos_f[:, bass.ds(step * GROUPS, GROUPS)], R.picked[:, :, :], AX.X, ALU.add).then_inc(R.s_rank_read, 1)

    with dve.Fori(0, STEPS // 2 - 1) as t:
        for par in range(2):
            place(t * 2 + par, par)
            onehots(t * 2 + par + 2, par).then_inc(R.s_onehot_ready, 1)
    for par in range(2):
        place(STEPS - 2 + par, par)
    done[0] = first + per_step * STEPS
    dve.wait_ge(R.s_rank_read, STEPS)
    nc.vector.tensor_copy(pos[:, :], R.pos_f[:, :]).then_inc(R.s_pos_ready, 1)

    dve.wait_ge(R.s_rows_in, 32)
    nc.vector.tensor_copy(R.ds_row[:, 0:1], R.s_row[:, 0:1]).then_inc(R.s_dve, 1)
    done[0] += 1
    link(nc.vector.tensor_tensor(R.ds_row[:, 1:], R.s_row[:, 1:], R.s_row[:, :g.buckets - 1], ALU.subtract))
    for c in range(g.cols):
        link(nc.vector.tensor_scalar(R.mask[:, :], R.vb_row[:, :], C["visit_" + g.name][:, c:c + 1], None, ALU.is_le))
        link(nc.vector.tensor_tensor_reduce(out=R.junk[:, :], in0=R.mask[:, :], in1=R.ones[:, 0:g.buckets], scale=1.0, scalar=0.0,
                                            op0=ALU.mult, op1=ALU.add, accum_out=R.vtab[:, 0, c:c + 1]))
        link(nc.vector.tensor_tensor_reduce(out=R.junk[:, :], in0=R.mask[:, :], in1=R.ds_row[:, :], scale=1.0, scalar=0.0,
                                            op0=ALU.mult, op1=ALU.add, accum_out=R.vtab[:, 1, c:c + 1]))
    link(nc.vector.tensor_scalar(R.vtab[:, 2, :], R.vtab[:, 0, :], -1.0, None, ALU.add))
    link(nc.vector.scalar_tensor_tensor(R.vtab[:, 3, :], C["visit_" + g.name][:, 0:g.cols], float(P), R.vtab[:, 1, :], ALU.mult, ALU.add))
    link(nc.vector.tensor_scalar(R.vtab[:, 3, :], R.vtab[:, 3, :], float(N_EDGES), None, ALU.min))
    nc.vector.tensor_copy(R.vtab_i[:, :], R.vtab[:, 3, :]).then_inc(R.s_visits_ready, 1)


def rank_tensor(nc, pe, g, R, C):
    def counts(par, start, stop):
        for q in range(4):
            hi, lo = (R.onehot[:, par, d, 4 * q:4 * q + 4, :].rearrange("p g k -> p (g k)") for d in range(2))
            last = nc.tensor.matmul(R.ps_h[:, q, :, :], hi, lo, start=start and q == 0, stop=stop and q == 3)
        return last

    for par in range(2):
        pe.wait_ge(R.s_onehot_ready, par + 1)
        counts(par, par == 0, False).then_inc(R.s_onehot_counted, 1)
    with pe.Fori(1, STEPS // 2 - 1) as t:
        for par in range(2):
            pe.wait_ge(R.s_onehot_ready, t * 2 + par + 1)
            counts(par, False, False).then_inc(R.s_onehot_counted, 1)
    for par in range(2):
        pe.wait_ge(R.s_onehot_ready, STEPS - 1 + par)
        last = counts(par, False, par == 1)
        last.then_inc(R.s_onehot_counted if par == 0 else R.s_counted, 1)

    pe.wait_ge(R.s_sums_ready, 1)
    nc.tensor.matmul(R.ps_s[:, 0:DIGIT], C["all_groups"], R.small[:, 0, :], start=True, stop=True)
    nc.tensor.matmul(R.ps_s[:, DIGIT:2 * DIGIT], C["groups_before"], R.small[:, 0, :], start=True, stop=True).then_inc(R.s_sums_done, 1)
    pe.wait_ge(R.s_sums_ready, 2)
    nc.tensor.matmul(R.ps_s[:, 2 * DIGIT:2 * DIGIT + 2], C["digits_before"], R.small[:, 8, 0:2], start=True, stop=True).then_inc(R.s_sums_done, 1)

    def step(s, par, first):
        pe.wait_ge(R.s_onehot_ready, s + STEPS + 1)
        for q in range(4):
            last = nc.tensor.transpose(R.ps_t[:, q, :], R.onehot[:, par, 0, 4 * q:4 * q + 4, :].rearrange("p g d -> p (g d)"), C["ident16"])
        last.then_inc(R.s_hi_t_ps, 1)
        pe.wait_ge(R.s_count_ready, s + 1)
        counts(par, True, True).then_inc(R.s_hist_ps, 1)
        if not first:
            pe.wait_ge(R.s_earlier_ready, s * 4)
        for b in range(4):
            nc.tensor.matmul(R.ps_eq[:, 4 * b:4 * b + 4, :], C["ident16"], C["not_earlier"], start=True, stop=False)
        pe.wait_ge(R.s_hi_t_ready, s * 2 + 2)
        for b in range(4):
            for q in range(4):
                hi_t = R.hi_t[32 * b:32 * b + 32, q, :]
                last = nc.tensor.matmul(R.ps_eq[:, 4 * b + q, :], hi_t, hi_t, start=False, stop=(q == 3), tile_position=(32 * b, 0))
            last.then_inc(R.s_eq_ps, 1)
        if not first:
            pe.wait_ge(R.s_rank_read, s)
        for q in range(4):
            nc.tensor.matmul(R.ps_g[:, 4 * q:4 * q + 4, :], R.hi_t32[:, q, :], R.count[:, q, :, :], start=(q == 0), stop=False)
        for slot in range(GROUPS):
            b, q = slot // 4, slot % 4
            if q == 0:
                pe.wait_ge(R.s_earlier_ready, s * 4 + b + 1)
            last = nc.tensor.matmul(R.ps_g[:, 4 * q + b, :], R.earlier[:, slot, :], R.onehot[:, par, 1, 4 * q + b, :],
                                    start=False, stop=(slot == GROUPS - 1))
        last.then_inc(R.s_rank_ps, 1)

    for par in range(2):
        step(par, par, par == 0)
    with pe.Fori(1, STEPS // 2) as t:
        for par in range(2):
            step(t * 2 + par, par, False)


def rank_scalar(nc, act, g, R, C, D):
    def step(s, first):
        act.wait_ge(R.s_hi_t_ps, s + 1)
        if not first:
            act.wait_ge(R.s_rank_ps, s)
        nc.scalar.copy(R.hi_t[:, :, :], R.ps_t[:, :, :]).then_inc(R.s_hi_t_ready, 1)
        nc.scalar.copy(R.hi_t32[:, :, :], R.ps_t[:, :, :]).then_inc(R.s_hi_t_ready, 1)
        for b in range(4):
            act.wait_ge(R.s_eq_ps, s * 4 + b + 1)
            nc.scalar.activation(R.earlier[:, 4 * b:4 * b + 4, :], R.ps_eq[:, 4 * b:4 * b + 4, :], ACT.Relu).then_inc(R.s_earlier_ready, 1)

    for s in range(2):
        step(s, s == 0)
    with act.Fori(1, STEPS // 2) as t:
        for par in range(2):
            step(t * 2 + par, False)

    def row(a):
        return a[0:g.buckets].rearrange("(o b) -> o b", o=1).broadcast_to([P, g.buckets])

    act.wait_ge(R.s_tables_ready, 1)
    act.dma_start(D["vb"].rearrange("(h l) -> h l", l=DIGIT), R.small[0:DIGIT, 10, :]).then_inc(R.s_tables_out, 16)
    act.dma_start(D["s"].rearrange("(h l) -> h l", l=DIGIT), R.small[0:DIGIT, 11, :]).then_inc(R.s_tables_out, 16)
    act.wait_ge(R.s_tables_out, 32)
    act.dma_start(R.vb_row[:, :], row(D["vb"])).then_inc(R.s_rows_in, 16)
    act.dma_start(R.s_row[:, :], row(D["s"])).then_inc(R.s_rows_in, 16)
    act.wait_ge(R.s_visits_ready, 1)
    act.dma_start(D["bucket"].rearrange("(p c) -> p c", c=g.cols), R.vtab[:, 2, :]).then_inc(R.s_visits_out, 16)
    act.dma_start(D["start"].rearrange("(p c) -> p c", c=g.cols), R.vtab_i[:, :]).then_inc(R.s_visits_out, 16)
    act.wait_ge(R.s_visits_out, 32)


def rank_constants(groupings):
    k = np.arange(P)
    gp, hi = k // 32, k % 32
    out = {
        "iota": np.tile(np.arange(P, dtype=np.float32), (P, 1)),
        "ident": np.eye(P, dtype=np.float32),
        "not_earlier": np.tile(-(k[:, None] >= k[None, :]).astype(np.float32), (1, 4)),
        "own_group": np.repeat(gp[:, None] == np.arange(4)[None, :], DIGIT, axis=1).astype(np.float32),
        "all_groups": (hi[:, None] == hi[None, :]).astype(np.float32),
        "groups_before": ((hi[:, None] == hi[None, :]) & (gp[:, None] < gp[None, :])).astype(np.float32),
        "digits_before": ((gp[:, None] == gp[None, :]) & (hi[:, None] < hi[None, :])).astype(np.float32),
    }
    for g in groupings:
        out["visit_" + g.name] = np.arange(P * g.cols, dtype=np.float32).reshape(P, g.cols)
    return out



CHUNK = 16
CHUNKS = TILES // CHUNK


class Scatter:

    def __init__(self, ctx, nc, name, width):
        self.name, self.width = name, width
        self.stage = ctx.enter_context(nc.sbuf_tensor(f"{name}_stage", [P, 2, CHUNK, width], fp32))
        self.place = ctx.enter_context(nc.sbuf_tensor(f"{name}_place", [P, 2, CHUNK], i32))
        self.s_in = [ctx.enter_context(nc.semaphore(f"{name}_in{r}")) for r in range(2)]
        self.s_out = [ctx.enter_context(nc.semaphore(f"{name}_out{r}")) for r in range(2)]
        self.s_begun = ctx.enter_context(nc.semaphore(f"{name}_begun"))
        self.s_staged = ctx.enter_context(nc.semaphore(f"{name}_staged"))


def load_attributes(sp, S, parts, t, r):
    for dram, at in parts:
        sp.dma_start(S.stage[:, r, :, at:at + dram.shape[2]], dram[:, bass.ds((t * 2 + r) * CHUNK, CHUNK), :]).then_inc(S.s_in[r], 16)


def load_more_attributes(sp, S, parts, writes):
    with sp.Fori(1, CHUNKS // 2) as t:
        for r in range(2):
            sp.wait_ge(S.s_out[r], t * (16 * writes))
            load_attributes(sp, S, parts, t, r)


def add_nodes(nc, pool, S, src, dst, c, r):
    at = bass.ds(c * CHUNK, CHUNK)
    nc.gpsimd.tensor_copy(S.stage[:, r, :, S.width - 2].bitcast(i32), src[:, at]).then_inc(S.s_staged, 1)
    nc.gpsimd.tensor_copy(S.stage[:, r, :, S.width - 1].bitcast(i32), dst[:, at]).then_inc(S.s_staged, 1)


def scatter_records(nc, pool, S, n_parts, src, dst, pos, out):
    def chunk(t, r, first):
        c = t * 2 + r
        if not first:
            pool.wait_ge(S.s_out[r], t * (16 * CHUNK))
        add_nodes(nc, pool, S, src, dst, c, r)
        nc.gpsimd.tensor_copy(S.place[:, r, :], pos[:, bass.ds(c * CHUNK, CHUNK)]).then_inc(S.s_staged, 1)
        pool.wait_ge(S.s_in[r], (t + 1) * (16 * n_parts))
        pool.wait_ge(S.s_staged, c * 3 + 3)
        pool.sem_inc(S.s_begun, 1)
        for j in range(CHUNK):
            nc.gpsimd.indirect_dma_start(out=out, out_offset=bass.IndirectOffsetOnAxis(ap=S.place[:, r, j:j + 1], axis=0),
                                         in_=S.stage[:, r, j, :], in_offset=None).then_inc(S.s_out[r], 16)

    for r in range(2):
        chunk(0, r, True)
    with pool.Fori(1, CHUNKS // 2) as t:
        for r in range(2):
            chunk(t, r, False)
    for r in range(2):
        pool.wait_ge(S.s_out[r], 16 * CHUNK * (CHUNKS // 2))


def store_records(nc, pool, S, n_parts, src, dst, out):
    rows = out.rearrange("(p j) w -> p j w", p=P)

    def chunk(t, r, first):
        c = t * 2 + r
        if not first:
            pool.wait_ge(S.s_out[r], t * 16)
        add_nodes(nc, pool, S, src, dst, c, r)
        pool.wait_ge(S.s_in[r], (t + 1) * (16 * n_parts))
        pool.wait_ge(S.s_staged, c * 2 + 2)
        pool.sem_inc(S.s_begun, 1)
        pool.dma_start(rows[:, bass.ds(c * CHUNK, CHUNK), :], S.stage[:, r, :, :]).then_inc(S.s_out[r], 16)

    for r in range(2):
        chunk(0, r, True)
    with pool.Fori(1, CHUNKS // 2) as t:
        for r in range(2):
            chunk(t, r, False)
    for r in range(2):
        pool.wait_ge(S.s_out[r], 16 * (CHUNKS // 2))


def gnn_kernel(nc, A, out, scratch):
    D0 = 160
    NS, NV = 64, 32
    VG = 4
    G0, G1 = A["groupings"]
    REC0, REC1 = 34, 22
    BATCH0, BATCHES0 = 16, G0.visits // 16
    GPB0 = BATCH0 // VG
    BATCH1, BATCHES1 = 8, G1.visits // 8
    GPB1 = BATCH1 // VG
    WIN = P
    rec0, rec1, f_tab, base_tab = scratch["rec0"], scratch["rec1"], scratch["f"], scratch["base"]

    outer = ExitStack()
    with outer:
        def sb_in(ctx, stage=""):
            return lambda n, s, d=fp32: ctx.enter_context(nc.sbuf_tensor(stage + n, s, d))

        def ps_in(ctx, stage=""):
            return lambda n, s, d=fp32: ctx.enter_context(nc.psum_tensor(stage + n, s, d))

        def sem_in(ctx, stage=""):
            return lambda n: ctx.enter_context(nc.semaphore(stage + n))

        sb = sb_in(outer)
        ident = sb("ident", [P, P])
        ident16 = sb("ident16", [P, P], bf16)
        iota = sb("iota", [P, P])

        with ExitStack() as ctx:
            sb, sem = sb_in(ctx), sem_in(ctx)
            src = sb("src", [P, TILES], i32)
            dst = sb("dst", [P, TILES], i32)
            src_pos = sb("src_pos", [P, TILES], i32)
            dst_pos = sb("dst_pos", [P, TILES], i32)
            iota16 = sb("iota16", [P, DIGIT], bf16)
            not_earlier32 = sb("not_earlier32", [P, 4 * P])
            not_earlier = sb("not_earlier", [P, 4 * P], bf16)
            own_group = sb("own_group", [P, 4, DIGIT])
            sums = {n: sb(n, [P, P]) for n in ("all_groups", "groups_before", "digits_before")}
            visit_no = {g.name: sb("visit_" + g.name, [P, g.cols]) for g in (G0, G1)}
            s_const, s_made = sem("s_const"), sem("s_made")
            C = {"iota": iota16, "ident16": ident16[:, :], "not_earlier": not_earlier[:, :], "own_group": own_group[:, :, :],
                 **{n: t[:, :] for n, t in sums.items()}, **{"visit_" + n: t for n, t in visit_no.items()}}
            consts = [(ident, A["ident"]), (iota, A["iota"]), (not_earlier32, A["not_earlier"]), (own_group, A["own_group"].rearrange("p (g l) -> p g l", l=DIGIT))]
            consts += [(sums[n], A[n]) for n in sums] + [(visit_no[n], A["visit_" + n]) for n in visit_no]

            with nc.Block() as block:
                @block.sync
                def _(sp):
                    for tile, dram in consts:
                        sp.dma_start(tile[:], dram).then_inc(s_const, 16)

                @block.vector
                def _(dve):
                    dve.wait_ge(s_const, 16 * len(consts))
                    nc.vector.tensor_copy(ident16[:, :], ident[:, :])
                    nc.vector.tensor_copy(iota16[:, :], iota[:, 0:DIGIT])
                    nc.vector.tensor_copy(not_earlier[:, :], not_earlier32[:, :]).then_inc(s_made, 1)

            out_of_order = sb("out_of_order", [1, 1], i32)
            s_src, s_dst, s_next, s_order = (sem(n) for n in ("s_src", "s_dst", "s_next", "s_order"))
            S1 = Scatter(ctx, nc, "edges1", REC1)
            parts0 = [(A["edge_attr_32"], 0)]
            parts1 = [(A["edge_attr_16"], 0), (A["edge_attr_4"], 16)]

            def edges_out_of_order(engine):
                engine.wait_ge(s_order, 1)
                return engine.value_load(out_of_order[0:1, 0:1], min_val=0, max_val=SLOTS)

            with ExitStack() as rank_ctx:
                R0 = alloc_rank(rank_ctx, nc, G0)
                next_dst = sb_in(rank_ctx)("next_dst", [P, TILES], i32)
                falls = sb_in(rank_ctx)("falls", [P, TILES])
                n_falls = sb_in(rank_ctx)("n_falls", [P, 1])
                one = sb_in(rank_ctx)("one", [P, 1])
                s_falls, s_falls_ps = (sem_in(rank_ctx)(n) for n in ("s_falls", "s_falls_ps"))
                with nc.Block() as block:
                    @block.sync
                    def _(sp):
                        sp.dma_start(dst[:, :], A["dst"]).then_inc(s_dst, 16)
                        sp.dma_start(next_dst[:, :], A["next_dst"]).then_inc(s_next, 16)
                        sp.dma_start(src[:, :], A["src"]).then_inc(s_src, 16)
                        with sp.If(edges_out_of_order(sp) < 1):
                            for r in range(2):
                                load_attributes(sp, S1, parts1, 0, r)
                            load_more_attributes(sp, S1, parts1, 1)

                    @block.vector
                    def _(dve):
                        nc.vector.memset(one[:, :], 1.0).then_inc(s_falls, 1)
                        dve.wait_ge(s_dst, 16)
                        dve.wait_ge(s_next, 16)
                        nc.vector.tensor_tensor(falls[:, :], dst[:, :], next_dst[:, :], ALU.is_gt).then_inc(s_falls, 1)
                        dve.wait_ge(s_falls, 2)
                        nc.vector.tensor_reduce(n_falls[:, :], falls[:, :], AX.X, ALU.add).then_inc(s_falls, 1)
                        dve.wait_ge(s_falls_ps, 1)
                        nc.vector.tensor_copy(out_of_order[:, :], R0.ps_s[0:1, 0:1]).then_inc(s_order, 1)
                        rank_vector(nc, dve, G0, R0, C, src, s_src, src_pos)

                    @block.tensor
                    def _(pe):
                        pe.wait_ge(s_falls, 3)
                        nc.tensor.matmul(R0.ps_s[0:1, 0:1], n_falls[:, :], one[:, :], start=True, stop=True).then_inc(s_falls_ps, 1)
                        rank_tensor(nc, pe, G0, R0, C)

                    @block.scalar
                    def _(act):
                        rank_scalar(nc, act, G0, R0, C, scratch["tables0"])

                    @block.gpsimd
                    def _(pool):
                        with pool.If(edges_out_of_order(pool) < 1):
                            pool.wait_ge(s_src, 16)
                            store_records(nc, pool, S1, 2, src, dst, rec1)

            with ExitStack() as rank_ctx:
                S0 = Scatter(rank_ctx, nc, "edges0", REC0)
                R1 = alloc_rank(rank_ctx, nc, G1)
                with nc.Block() as block:
                    @block.sync
                    def _(sp):
                        for r in range(2):
                            load_attributes(sp, S0, parts0, 0, r)
                        load_more_attributes(sp, S0, parts0, CHUNK)
                        with sp.If(edges_out_of_order(sp) > 0):
                            for r in range(2):
                                load_attributes(sp, S1, parts1, 0, r)
                            load_more_attributes(sp, S1, parts1, CHUNK)

                    @block.scalar
                    def _(act):
                        rank_scalar(nc, act, G1, R1, C, scratch["tables1"])

                    @block.vector
                    def _(dve):
                        rank_vector(nc, dve, G1, R1, C, dst, s_dst, dst_pos)

                    @block.tensor
                    def _(pe):
                        rank_tensor(nc, pe, G1, R1, C)

                    @block.gpsimd
                    def _(pool):
                        scatter_records(nc, pool, S0, 1, src, dst, src_pos, rec0)
                        with pool.If(edges_out_of_order(pool) > 0):
                            pool.wait_ge(R1.s_pos_ready, 1)
                            scatter_records(nc, pool, S1, 2, src, dst, dst_pos, rec1)

        sb = sb_in(outer)
        vec = sb("node_attr", [P, NODE_TILES])
        eps = sb("eps", [P, 1])

        acc_ctx = ExitStack()
        acc_a = sb_in(acc_ctx)("acc_a", [P, NODE_ROWS])
        acc_b = sb_in(acc_ctx)("acc_b", [NV + 1, NODE_ROWS])

        with ExitStack() as ctx:
            sb, ps, sem = sb_in(ctx, "z_"), ps_in(ctx, "z_"), sem_in(ctx, "z_")
            RING = 2 * GPB0
            w_es = sb("w_es", [P, 8, D0])
            w_ex = sb("w_ex", [P, 8, NS + NV])
            w_ey = sb("w_ey", [P, 8, P])
            w_ez = sb("w_ez", [P, 8, NV])
            wb_es = sb("wb_es", [P, 8, NV])
            wb_ez = sb("wb_ez", [P, 8, NS])
            factor = sb("factor", [P, 4])
            vis_start = sb("vis_start", [1, P * G0.cols], i32)
            first_node = sb("first_node", [P, G0.visits])
            win_i = sb("win_i", [1, BATCHES0], i32)
            spread = sb("spread", [P, BATCH0])
            picked = sb("picked", [P, BATCHES0, BATCH0])
            in_bucket = sb("in_bucket", [P, 1])
            rel2 = sb("rel2", [P, BATCHES0])
            rec = sb("rec", [P, RING, VG, REC0])
            xg = sb("xg", [P, RING, VG, D0])
            rel = sb("rel", [P, 2, VG])
            onehot = sb("onehot", [P, 2, BATCH0, 8])
            outer_p = sb("outer_p", [P, 2, VG, 8, 32])
            za = sb("za", [P, 2, 32, P])
            zb = sb("zb", [P, 2, 16, P])
            o_sb = sb("o_sb", [P, 2 * P])
            onehot2 = sb("onehot2", [P, WIN])
            ones = sb("ones", [P, 1])
            begun = sb("begun", [1, 8])
            ps_a = ps("ps_a", [P, 2, VG, 8 * 32])
            ps_b = ps("ps_b", [P, 2, VG, 8 * 16])
            ps_o = ps("ps_o", [P, 512])
            ps_w = ps("ps_w", [P, 4, WIN])
            s_zero, s_w, s_prep, s_dve = (sem(n) for n in ("zero", "w", "prep", "dve"))
            s_rec = [sem(f"rec{r}") for r in range(RING // 2)]
            s_xg = [sem(f"xg{r}") for r in range(RING // 2)]
            HALF = 2 * VG * 16
            s_outer = sem("outer")
            s_z = sem("z")
            s_za, s_zb = sem("za"), sem("zb")
            s_o_ps, s_o = sem("o_ps"), sem("o")
            s_oh2 = sem("oh2")
            s_win = sem("win")
            s_acc = sem("acc")
            s_begun = sem("begun")
            s_tab = sem("tab")
            tab = scratch["tables0"]
            FREE = {"z": RING, "za": 2, "zb": 2, "o_ps": 2, "o": 1, "win": 1, "acc": 2}

            with nc.Block() as block:
                @block.sync
                def _(sp):
                    sp.wait_ge(s_zero, 6)
                    W1, W2, W3, W4 = (A[n] for n in ("W1", "W2", "W3", "W4"))
                    pieces = [(w_es[0:64, :, 0:64], W1), (w_es[64:96, :, 64:96], W4), (w_es[96:128, :, 96:128], W4), (wb_es[96:128, :, :], W4),
                              (w_ex[0:64, :, 64:96], W3), (w_ey[0:64, :, 96:128], W3), (w_ez[0:64, :, :], W3),
                              (w_ex[64:96, :, 0:64], W2), (w_ey[96:128, :, 0:64], W2), (wb_ez[96:128, :, :], W2)]
                    for tile, dram in pieces:
                        sp.dma_start(tile, dram).then_inc(s_w, 16)
                    sp.dma_start(factor[:, :], A["factor0"]).then_inc(s_w, 16)
                    sp.dma_start(vis_start[:, :], tab["start"].rearrange("(o v) -> o v", o=1)).then_inc(s_tab, 16)
                    sp.dma_start(first_node[:, :], tab["bucket"][0:G0.visits].rearrange("(o v) -> o v", o=1).broadcast_to([P, G0.visits])).then_inc(s_tab, 16)
                    sp.dma_start(spread[:, :], A["spread0"]).then_inc(s_tab, 16)
                    sp.dma_start(in_bucket[:, :], A["in_bucket0"]).then_inc(s_tab, 16)
                    sp.wait_ge(s_tab, 64)

                    def group(t, i):
                        n = t * RING + i
                        sp.wait_ge(s_z, n + 1)
                        sp.wait_ge(s_tab, 64)
                        for v in range(VG):
                            row = sp.value_load(vis_start[0:1, bass.ds(n * VG + v, 1)], min_val=0, max_val=N_EDGES)
                            sp.dma_start(rec[:, i, v, :], rec0[bass.ds(row, P), :]).then_inc(s_rec[i // 2], 16)

                    with sp.Fori(0, BATCHES0 // 2) as t:
                        for i in range(RING):
                            group(t, i)

                @block.gpsimd
                def _(pool):
                    for tile in (w_es, w_ex, w_ey, w_ez, wb_es, wb_ez):
                        nc.gpsimd.memset(tile[:], 0.0).then_inc(s_zero, 1)

                    def group(t, i):
                        n = t * RING + i
                        pool.wait_ge(s_z, n + 1)
                        pool.wait_ge(s_rec[i // 2], (t + 1) * HALF)
                        pool.sem_inc(s_begun, 1)
                        for v in range(VG):
                            nc.gpsimd.indirect_dma_start(out=xg[:, i, v, :], out_offset=None, in_=A["x"],
                                                         in_offset=bass.IndirectOffsetOnAxis(ap=rec[:, i, v, REC0 - 1:REC0].bitcast(i32), axis=0)).then_inc(s_xg[i // 2], 16)

                    with pool.Fori(0, BATCHES0 // 2) as t:
                        for i in range(RING):
                            group(t, i)

                @block.vector
                def _(dve):
                    done = [0]

                    def link(ins):
                        done[0] += 1
                        ins.then_inc(s_dve, 1)
                        dve.wait_ge(s_dve, done[0])

                    nc.vector.memset(acc_a[:, :], 0.0).then_inc(s_acc, 1)
                    nc.vector.memset(acc_b[:, :], 0.0).then_inc(s_acc, 1)
                    link(nc.vector.memset(ones[:, :], 1.0))
                    nc.vector.memset(o_sb[:, :], 0.0).then_inc(s_prep, 1)
                    dve.wait_ge(s_w, 16 * 11)
                    for tile, col in ((w_es, 0), (wb_es, 0), (w_ex, 1), (w_ey, 1), (w_ez, 1), (wb_ez, 1)):
                        nc.vector.tensor_scalar(tile[:], tile[:], factor[:, col:col + 1], None, ALU.mult).then_inc(s_prep, 1)
                    dve.wait_ge(s_tab, 64)
                    link(nc.vector.tensor_scalar(first_node[:, :], first_node[:, :], float(G0.width), None, ALU.mult))
                    link(nc.vector.tensor_copy(win_i[:, :], first_node[0:1, ::BATCH0]))
                    link(nc.vector.tensor_tensor(picked[:, :, :], first_node[:, :].rearrange("p (k v) -> p k v", v=BATCH0),
                                                 spread[:, :].unsqueeze(1).broadcast_to([P, BATCHES0, BATCH0]), ALU.mult))
                    link(nc.vector.tensor_reduce(rel2[:, :], picked[:, :, :], AX.X, ALU.add))
                    link(nc.vector.tensor_scalar(rel2[:, :], rel2[:, :], in_bucket[:, 0:1], None, ALU.add))
                    for c, (s, n) in enumerate(((s_z, "z"), (s_za, "za"), (s_zb, "zb"), (s_o_ps, "o_ps"), (s_o, "o"), (s_win, "win"))):
                        nc.vector.memset(begun[:, c:c + 1], 1.0).then_inc(s, FREE[n])
                    first = done[0]

                    def products(t, h, g):
                        i, k = h * GPB0 + g, t * 2 + h
                        n = t * RING + i
                        if g == 0:
                            dve.wait_ge(s_o_ps, k + 1)
                        dve.wait_ge(s_rec[i // 2], (t + 1) * HALF)
                        nc.vector.tensor_tensor(rel[:, g % 2, :], rec[:, i, :, REC0 - 2].bitcast(i32), first_node[:, bass.ds(n * VG, VG)], ALU.subtract).then_inc(s_dve, 1)
                        dve.wait_ge(s_dve, n * 2 + first + 1)
                        oh = onehot[:, h, g * VG:(g + 1) * VG, :]
                        nc.vector.tensor_tensor(oh, iota[:, 0:8].unsqueeze(1).broadcast_to([P, VG, 8]),
                                                rel[:, g % 2, :].unsqueeze(2).broadcast_to([P, VG, 8]), ALU.is_equal).then_inc(s_dve, 1)
                        dve.wait_ge(s_dve, n * 2 + first + 2)
                        dve.wait_ge(s_z, n + (RING - 1))
                        nc.vector.tensor_tensor(outer_p[:, g % 2, :, :, :], oh.unsqueeze(3).broadcast_to([P, VG, 8, 32]),
                                                rec[:, i, :, 0:32].unsqueeze(2).broadcast_to([P, VG, 8, 32]), ALU.mult).then_inc(s_outer, 1)

                    def add_window(k):
                        node = dve.value_load(win_i[0:1, bass.ds(k, 1)], min_val=0, max_val=NODE_ROWS - WIN)
                        dve.wait_ge(s_acc, k * 2 + 2)
                        dve.wait_ge(s_win, k + 2)
                        at = bass.ds(node, WIN)
                        nc.vector.tensor_tensor(acc_a[:, at], acc_a[:, at], ps_w[:, 0, :], ALU.add).then_inc(s_acc, 1)
                        nc.vector.tensor_tensor(acc_b[:, at], acc_b[:, at], ps_w[0:NV + 1, 1, :], ALU.add).then_inc(s_acc, 1)

                    def second_onehot(k):
                        dve.wait_ge(s_win, k + 1)
                        nc.vector.tensor_scalar(onehot2[:, :], iota[:, :], rel2[:, bass.ds(k, 1)], None, ALU.is_equal).then_inc(s_oh2, 1)

                    def batch(t, h, lag1=True, lag2=True):
                        k = t * 2 + h
                        products(t, h, 0)
                        products(t, h, 1)
                        if lag2:
                            add_window(k - 2)
                        if lag1:
                            second_onehot(k - 1)
                        products(t, h, 2)
                        products(t, h, 3)

                    batch(0, 0, False, False)
                    batch(0, 1, True, False)
                    with dve.Fori(1, BATCHES0 // 2) as t:
                        for h in range(2):
                            batch(t, h)
                    add_window(BATCHES0 - 2)
                    second_onehot(BATCHES0 - 1)
                    add_window(BATCHES0 - 1)

                @block.scalar
                def _(act):
                    def evacuate(t, h, g):
                        i, k = h * GPB0 + g, t * 2 + h
                        n = t * RING + i
                        if g == 0:
                            act.wait_ge(s_o_ps, k + 1)
                        act.wait_ge(s_z, n + (RING + 1))
                        rows = slice(g * VG * 8, (g + 1) * VG * 8)
                        nc.scalar.copy(za[:, h, :, rows], ps_a[:, g % 2, :, :].rearrange("p v (m b) -> p b (v m)", b=32)).then_inc(s_za, 1)
                        nc.scalar.copy(zb[:, h, :, rows], ps_b[:, g % 2, :, :].rearrange("p v (m b) -> p b (v m)", b=16)).then_inc(s_zb, 1)

                    def copy_out(k):
                        act.wait_ge(s_win, k + 1)
                        act.wait_ge(s_o_ps, k + 3)
                        nc.scalar.copy(o_sb[:, 0:D0 + 1], ps_o[:, 0:D0 + 1]).then_inc(s_o, 1)

                    def batch(t, h, lag1=True):
                        for g in range(GPB0):
                            evacuate(t, h, g)
                            if g == 1 and lag1:
                                copy_out(t * 2 + h - 1)

                    batch(0, 0, False)
                    batch(0, 1)
                    with act.Fori(1, BATCHES0 // 2) as t:
                        for h in range(2):
                            batch(t, h)
                    copy_out(BATCHES0 - 1)

                @block.tensor
                def _(pe):
                    pe.wait_ge(s_prep, 7)

                    def sums(t, h, g):
                        i = h * GPB0 + g
                        n = t * RING + i
                        pe.wait_ge(s_za, n + 1)
                        pe.wait_ge(s_zb, n + 1)
                        pe.wait_ge(s_xg[i // 2], (t + 1) * HALF)
                        pe.wait_ge(s_outer, n + 1)
                        for v in range(VG):
                            prod = outer_p[:, g % 2, v, :, :]
                            nc.tensor.matmul(ps_a[:, g % 2, v, :], xg[:, i, v, 0:P], prod, start=(v % 2 == 0), stop=(v % 2 == 1))
                            last = nc.tensor.matmul(ps_b[:, g % 2, v, :], xg[:, i, v, NV:NV + P], prod[:, :, 0:16], start=(v == 0), stop=(v == VG - 1))
                        last.then_inc(s_z, 1)

                    def contract(k, h):
                        pe.wait_ge(s_za, k * GPB0 + (GPB0 + FREE["za"]))
                        pe.wait_ge(s_zb, k * GPB0 + (GPB0 + FREE["zb"]))
                        pe.wait_ge(s_o, k + 1)
                        for b in range(8):
                            wide = D0 if b == 0 else P
                            nc.tensor.matmul(ps_o[:, 0:wide], za[:, h, b, :], w_es[:, b, 0:wide], start=(b == 0), stop=False)
                            nc.tensor.matmul(ps_o[:, P:D0], zb[:, h, b, :], wb_es[:, b, :], start=False, stop=False)
                            nc.tensor.matmul(ps_o[:, P:D0], za[:, h, 8 + b, :], w_ez[:, b, :], start=False, stop=False)
                            nc.tensor.matmul(ps_o[:, 0:NS], zb[:, h, 8 + b, :], wb_ez[:, b, :], start=False, stop=False)
                            nc.tensor.matmul(ps_o[:, 0:NS + NV], za[:, h, 16 + b, :], w_ex[:, b, :], start=False, stop=False)
                            nc.tensor.matmul(ps_o[:, 0:P], za[:, h, 24 + b, :], w_ey[:, b, :], start=False, stop=False)
                        nc.tensor.matmul(ps_o[:, D0:D0 + 1], onehot[:, h, :, :].rearrange("p v m -> p (v m)"), ones[:, :], start=False, stop=True).then_inc(s_o_ps, 1)

                    def window(k):
                        pe.wait_ge(s_o, k + 2)
                        pe.wait_ge(s_oh2, k + 1)
                        pe.wait_ge(s_acc, k * 2 + 2)
                        nc.tensor.matmul(ps_w[:, 0, :], o_sb[:, 0:P], onehot2[:, :], start=True, stop=False)
                        nc.tensor.matmul(ps_w[:, 1, :], o_sb[:, P:], onehot2[:, :], start=False, stop=True).then_inc(s_win, 1)

                    def batch(t, h, lag1=True):
                        k = t * 2 + h
                        sums(t, h, 0)
                        sums(t, h, 1)
                        if lag1:
                            contract(k - 1, 1 - h)
                        sums(t, h, 2)
                        sums(t, h, 3)
                        if lag1:
                            window(k - 1)

                    batch(0, 0, False)
                    batch(0, 1)
                    with pe.Fori(1, BATCHES0 // 2) as t:
                        for h in range(2):
                            batch(t, h)
                    contract(BATCHES0 - 1, 1)
                    window(BATCHES0 - 1)

        with ExitStack() as ctx:
            sb, ps, sem = sb_in(ctx, "n_"), ps_in(ctx, "n_"), sem_in(ctx, "n_")
            wm_ta = sb("wm_ta", [P, D0 + 1])
            wm_tb = sb("wm_tb", [NV, D0 + 1])
            wu1_a = sb("wu1_a", [P, D0])
            wu1_b = sb("wu1_b", [NV, D0])
            wu0_a = sb("wu0_a", [P, D0])
            wu0_b = sb("wu0_b", [NV, D0])
            wc_a = sb("wc_a", [P, D0])
            wc_b = sb("wc_b", [NV + 1, D0])
            bu = sb("bu", [P, D0])
            wn_a = sb("wn_a", [P, 2 * D0])
            wn_b = sb("wn_b", [P, 2 * D0])
            factor1 = sb("factor1", [P, 2])
            x = sb("x", [P, 2, D0])
            xt_a = sb("xt_a", [P, 2, P])
            xt_b = sb("xt_b", [NV, 2, P])
            sum_a = sb("sum_a", [P, 2, P])
            sum_b = sb("sum_b", [NV + 1, 2, P])
            y = sb("y", [P, 2, D0])
            stats = sb("stats", [P, 2, 6])
            mean_var = sb("mean_var", [P, 2, 2])
            std = sb("std", [P, 2, 1])
            rstd = sb("rstd", [P, 2, 1])
            x1 = sb("x1", [P, 2, D0])
            x1t = sb("x1t", [P, 2, 2, P])
            f_out = sb("f_out", [P, 2, D0])
            base_out = sb("base_out", [P, 2, D0])
            ps_u = [ps(f"ps_u{r}", [P, 512]) for r in range(2)]
            ps_t = [ps(f"ps_t{r}", [P, 512]) for r in range(2)]
            ps_f = [ps(f"ps_f{r}", [P, 512]) for r in range(2)]
            ps_s = [ps(f"ps_s{r}", [P, 512]) for r in range(2)]
            WEIGHTS = 16 * 17
            s_zero, s_scaled, s_wc_ps, s_wc = (sem(n) for n in ("zero", "scaled", "wc_ps", "wc"))
            s_x = [sem(f"in{r}") for r in range(2)]
            s_sum = sem("sum")
            s_u = sem("u")
            s_y = sem("y")
            s_yb, s_bn, s_var, s_std, s_rstd, s_x1 = (sem(n) for n in ("yb", "bn", "var", "std", "rstd", "x1"))
            s_t, s_x1t = sem("t"), sem("x1t")
            s_f, s_fo, s_bo = sem("f"), sem("fo"), sem("bo")
            s_st = [sem(f"st{r}") for r in range(2)]
            s_w = sem("w")

            with nc.Block() as block:
                @block.sync
                def _(sp):
                    sp.wait_ge(s_zero, 2)
                    WU, WMT = A["Wu"], A["WmT"]
                    pieces = [(wm_ta[:, :], WMT[0:P, :]), (wm_tb[:, :], WMT[P:D0, :]), (wu0_a[:, :], WU[0:P, :]), (wu0_b[:, :], WU[P:D0, :]),
                              (wu1_a[:, :], WU[D0:D0 + P, :]), (wu1_b[:, :], WU[D0 + P:2 * D0, :]),
                              (bu[:, :], A["bu"].rearrange("(o d) -> o d", o=1).broadcast_to([P, D0])),
                              (factor1[:, :], A["factor1"]), (vec[:, :], A["node_vec1"])]
                    for c, (scal, vect) in enumerate((("Wl1_0", "Wl1_1"), ("Wsc0", "Wsc1"))):
                        pieces += [(wn_a[0:64, c * D0:c * D0 + 64], A[scal]), (wn_a[64:96, c * D0 + 64:c * D0 + 96], A[vect]),
                                   (wn_a[96:128, c * D0 + 96:c * D0 + 128], A[vect]), (wn_b[96:128, c * D0 + 128:c * D0 + 160], A[vect])]
                    for tile, dram in pieces:
                        sp.dma_start(tile, dram).then_inc(s_w, 16)

                    def load(i, r):
                        at = bass.ds(i * P, P)
                        sp.dma_start(x[:, r, :], A["x"][at, :]).then_inc(s_x[r], 16)
                        sp.dma_start(xt_a[:, r, :], A["xT"][0:P, at]).then_inc(s_x[r], 16)
                        sp.dma_start(xt_b[:, r, :], A["xT"][P:D0, at]).then_inc(s_x[r], 16)

                    def store(t, r):
                        i = t * 2 + r
                        at = bass.ds(i * P, P)
                        sp.wait_ge(s_fo, i + 1)
                        sp.dma_start(f_tab[at, :], f_out[:, r, :]).then_inc(s_st[r], 16)
                        sp.wait_ge(s_bo, i + 1)
                        sp.dma_start(base_tab[at, :], base_out[:, r, :]).then_inc(s_st[r], 16)

                    for r in range(2):
                        load(r, r)
                    for r in range(2):
                        sp.wait_ge(s_y, 1 + r)
                        load(2 + r, r)
                    with sp.Fori(2, NODE_TILES // 2) as t:
                        for r in range(2):
                            sp.wait_ge(s_y, t * 2 + r - 1)
                            sp.wait_ge(s_u, t * 2 + r - 1)
                            load(t * 2 + r, r)
                            store(t - 2, r)
                    for t in (NODE_TILES // 2 - 2, NODE_TILES // 2 - 1):
                        for r in range(2):
                            store(t, r)
                    for r in range(2):
                        sp.wait_ge(s_st[r], 16 * NODE_TILES)

                @block.gpsimd
                def _(pool):
                    nc.gpsimd.memset(wn_a[:, :], 0.0).then_inc(s_zero, 1)
                    nc.gpsimd.memset(wn_b[:, :], 0.0).then_inc(s_zero, 1)

                    def pick(i, r):
                        at = bass.ds(i * P, P)
                        nc.gpsimd.tensor_copy(sum_a[:, r, :], acc_a[:, at]).then_inc(s_sum, 1)
                        nc.gpsimd.tensor_copy(sum_b[:, r, :], acc_b[:, at]).then_inc(s_sum, 1)

                    for r in range(2):
                        pick(r, r)
                    with pool.Fori(1, NODE_TILES // 2) as t:
                        for r in range(2):
                            pool.wait_ge(s_u, t * 2 + r - 1)
                            pick(t * 2 + r, r)

                @block.vector
                def _(dve):
                    nc.vector.memset(eps[:, :], 1e-5)
                    dve.wait_ge(s_w, WEIGHTS)
                    nc.vector.tensor_scalar(wn_a[:, :], wn_a[:, :], factor1[:, 0:1], None, ALU.mult).then_inc(s_scaled, 1)
                    nc.vector.tensor_scalar(wn_b[:, :], wn_b[:, :], factor1[:, 1:2], None, ALU.mult).then_inc(s_scaled, 1)
                    dve.wait_ge(s_wc_ps, 1)
                    nc.vector.tensor_copy(wc_a[:, :], ps_u[0][:, 0:D0]).then_inc(s_wc, 1)
                    nc.vector.tensor_copy(wc_b[:, :], ps_u[1][0:NV + 1, 0:D0]).then_inc(s_wc, 1)

                    def update(t, r):
                        i = t * 2 + r
                        dve.wait_ge(s_x[r], (t + 1) * 48)
                        dve.wait_ge(s_u, i + 1)
                        nc.vector.scalar_tensor_tensor(y[:, r, :], x[:, r, :], 2.0, ps_u[r][:, 0:D0], ALU.mult, ALU.add).then_inc(s_y, 1)
                        dve.wait_ge(s_y, i + 1)
                        nc.vector.tensor_tensor(y[:, r, :], y[:, r, :], bu[:, :], ALU.add).then_inc(s_yb, 1)
                        dve.wait_ge(s_yb, i + 1)
                        nc.vector.bn_stats(stats[:, r, :], y[:, r, :]).then_inc(s_bn, 1)
                        dve.wait_ge(s_w, WEIGHTS)
                        dve.wait_ge(s_bn, i + 1)
                        nc.vector.bn_aggr(mean_var[:, r, :], stats[:, r, :]).then_inc(s_var, 1)

                    def normalise(j, r):
                        dve.wait_ge(s_std, j + 1)
                        nc.vector.reciprocal(rstd[:, r, :], std[:, r, :]).then_inc(s_rstd, 1)
                        dve.wait_ge(s_rstd, j + 1)
                        nc.vector.tensor_scalar(x1[:, r, :], y[:, r, :], mean_var[:, r, 0:1], rstd[:, r, :], ALU.subtract, ALU.mult).then_inc(s_x1, 1)

                    def residual(t, r, first):
                        j = t * 2 + r
                        dve.wait_ge(s_f, j + 1)
                        if not first:
                            dve.wait_ge(s_st[r], t * 32)
                        nc.vector.scalar_tensor_tensor(base_out[:, r, :], ps_s[r][:, 0:D0], vec[:, bass.ds(j, 1)], x1[:, r, :], ALU.mult, ALU.add).then_inc(s_bo, 1)

                    update(0, 0)
                    update(0, 1)
                    normalise(0, 0)
                    update(1, 0)
                    normalise(1, 1)
                    residual(0, 0, True)
                    update(1, 1)
                    normalise(2, 0)
                    residual(0, 1, True)
                    with dve.Fori(2, NODE_TILES // 2) as t:
                        update(t, 0)
                        normalise(t * 2 - 1, 1)
                        residual(t - 1, 0, False)
                        update(t, 1)
                        normalise(t * 2, 0)
                        residual(t - 1, 1, False)
                    normalise(NODE_TILES - 1, 1)
                    residual(NODE_TILES // 2 - 1, 0, False)
                    residual(NODE_TILES // 2 - 1, 1, False)

                @block.scalar
                def _(act):
                    def deviation(i, r):
                        act.wait_ge(s_var, i + 1)
                        nc.scalar.activation(std[:, r, :], mean_var[:, r, 1:2], ACT.Sqrt, bias=eps[:, :]).then_inc(s_std, 1)

                    def transposed(j, r):
                        act.wait_ge(s_t, j + 1)
                        nc.scalar.copy(x1t[:, r, :, :], ps_t[r][:, 0:2 * P].rearrange("p (a n) -> p a n", a=2)).then_inc(s_x1t, 1)

                    def products(t, r, first):
                        j = t * 2 + r
                        if not first:
                            act.wait_ge(s_st[r], t * 32)
                        act.wait_ge(s_f, j + 1)
                        nc.scalar.activation(f_out[:, r, :], ps_f[r][:, 0:D0], ACT.Copy, scale=vec[:, bass.ds(j, 1)]).then_inc(s_fo, 1)

                    deviation(0, 0)
                    deviation(1, 1)
                    transposed(0, 0)
                    deviation(2, 0)
                    transposed(1, 1)
                    products(0, 0, True)
                    deviation(3, 1)
                    transposed(2, 0)
                    products(0, 1, True)
                    with act.Fori(2, NODE_TILES // 2) as t:
                        deviation(t * 2, 0)
                        transposed(t * 2 - 1, 1)
                        products(t - 1, 0, False)
                        deviation(t * 2 + 1, 1)
                        transposed(t * 2, 0)
                        products(t - 1, 1, False)
                    transposed(NODE_TILES - 1, 1)
                    products(NODE_TILES // 2 - 1, 0, False)
                    products(NODE_TILES // 2 - 1, 1, False)

                @block.tensor
                def _(pe):
                    pe.wait_ge(s_w, WEIGHTS)
                    nc.tensor.matmul(ps_u[0][:, 0:D0], wm_ta[:, 0:P], wu1_a[:, :], start=True, stop=False)
                    nc.tensor.matmul(ps_u[0][:, 0:D0], wm_tb[:, 0:P], wu1_b[:, :], start=False, stop=True)
                    nc.tensor.matmul(ps_u[1][0:NV + 1, 0:D0], wm_ta[:, P:D0 + 1], wu1_a[:, :], start=True, stop=False)
                    nc.tensor.matmul(ps_u[1][0:NV + 1, 0:D0], wm_tb[:, P:D0 + 1], wu1_b[:, :], start=False, stop=True).then_inc(s_wc_ps, 1)
                    pe.wait_ge(s_wc, 2)
                    pe.wait_ge(s_scaled, 2)

                    def update(t, r, first):
                        i = t * 2 + r
                        if not first:
                            pe.wait_ge(s_y, i - 1)
                        pe.wait_ge(s_x[r], (t + 1) * 48)
                        pe.wait_ge(s_sum, i * 2 + 2)
                        nc.tensor.matmul(ps_u[r][:, 0:D0], xt_a[:, r, :], wu0_a[:, :], start=True, stop=False)
                        nc.tensor.matmul(ps_u[r][:, 0:D0], xt_b[:, r, :], wu0_b[:, :], start=False, stop=False)
                        nc.tensor.matmul(ps_u[r][:, 0:D0], sum_a[:, r, :], wc_a[:, :], start=False, stop=False)
                        nc.tensor.matmul(ps_u[r][:, 0:D0], sum_b[:, r, :], wc_b[:, :], start=False, stop=True).then_inc(s_u, 1)

                    def transposes(j, r, first):
                        if not first:
                            pe.wait_ge(s_x1t, j - 1)
                        pe.wait_ge(s_x1, j + 1)
                        nc.tensor.transpose(ps_t[r][:, 0:P], x1[:, r, 0:P], ident[:, :])
                        nc.tensor.transpose(ps_t[r][:, P:2 * P], x1[:, r, NV:D0], ident[:, :]).then_inc(s_t, 1)

                    def products(j, r, first):
                        if not first:
                            pe.wait_ge(s_fo, j - 1)
                            pe.wait_ge(s_bo, j - 1)
                        pe.wait_ge(s_x1t, j + 1)
                        for bank, c in ((ps_f[r], 0), (ps_s[r], D0)):
                            nc.tensor.matmul(bank[:, 0:D0], x1t[:, r, 0, :], wn_a[:, c:c + D0], start=True, stop=False)
                            last = nc.tensor.matmul(bank[:, 0:D0], x1t[:, r, 1, :], wn_b[:, c:c + D0], start=False, stop=True)
                        last.then_inc(s_f, 1)

                    update(0, 0, True)
                    update(0, 1, True)
                    transposes(0, 0, True)
                    update(1, 0, False)
                    transposes(1, 1, True)
                    products(0, 0, True)
                    update(1, 1, False)
                    transposes(2, 0, False)
                    products(1, 1, True)
                    with pe.Fori(2, NODE_TILES // 2) as t:
                        update(t, 0, False)
                        transposes(t * 2 - 1, 1, False)
                        products(t * 2 - 2, 0, False)
                        update(t, 1, False)
                        transposes(t * 2, 0, False)
                        products(t * 2 - 1, 1, False)
                    transposes(NODE_TILES - 1, 1, False)
                    products(NODE_TILES - 2, 0, False)
                    products(NODE_TILES - 1, 1, False)
        acc_ctx.close()

        W1_ = D0 + 1
        sums_tab = scratch["sums"]
        with ExitStack() as ctx:
            sb, ps, sem = sb_in(ctx, "e_"), ps_in(ctx, "e_"), sem_in(ctx, "e_")
            AHEAD = 4
            RING = AHEAD * GPB1
            PAIRS = BATCH1 // 2
            wfc1 = sb("wfc1", [P, PAIRS, P])
            wfc2 = sb("wfc2", [P, 2, 192])
            vis_start = sb("vis_start", [1, P * G1.cols], i32)
            first_node = sb("first_node", [P, G1.visits])
            same = sb("same", [P, G1.visits])
            rec = sb("rec", [P, AHEAD, BATCH1, REC1])
            fg = sb("fg", [P, RING, VG, D0])
            rel = sb("rel", [P, 2, BATCH1])
            onehot = sb("onehot", [P, AHEAD, BATCH1, 4, 32], bf16)
            onehot_sh = sb("onehot_sh", [P, AHEAD, BATCH1, 4, 32])
            scal = sb("scal", [P, BATCH1, 16])
            scal_t = sb("scal_t", [P, P])
            hidden = sb("hidden", [P, 2, PAIRS, P])
            prod = sb("prod", [P, 2, BATCH1, 2, D0])
            run = sb("run", [P, 2, BATCH1, W1_])
            ones = sb("ones", [P, 1], bf16)
            ps_t = ps("ps_t", [P, 512])
            ps_h = ps("ps_h", [P, PAIRS, P])
            ps_w = ps("ps_w", [P, GPB1, 2, 2, 256])
            ps_m = ps("ps_m", [P, 2, 512])
            s_zero, s_w, s_prep, s_dve = (sem(n) for n in ("zero", "w", "prep", "dve"))
            s_rec = [sem(f"rec{i}") for i in range(AHEAD)]
            s_fg = [sem(f"fg{i}") for i in range(AHEAD)]
            s_free, s_free2 = sem("free"), sem("free2")
            LOADED = 16 * BATCH1
            s_oh = sem("oh")
            s_scal, s_t, s_scal_t, s_h, s_hid = (sem(n) for n in ("scal", "t", "scal_t", "h", "hid"))
            s_wt = sem("wt")
            s_msg = sem("msg")
            s_m = sem("m")
            s_run = sem("run")
            s_st = [sem(f"st{r}") for r in range(2)]
            s_begun = sem("begun")
            s_tab = sem("tab")
            tab = scratch["tables1"]
            STORED = 16 * GPB1

            def load_records(engine, half, t, h, s_free, first):
                k = t * AHEAD + h
                if not first:
                    engine.wait_ge(s_msg, (k - AHEAD + 1) * GPB1)
                    engine.wait_ge(s_oh, k - AHEAD + 1)
                    engine.wait_ge(s_scal, k - AHEAD + 1)
                    engine.sem_inc(s_free, 1)
                for v in range(half * VG, (half + 1) * VG):
                    row = engine.value_load(vis_start[0:1, bass.ds(k * BATCH1 + v, 1)], min_val=0, max_val=N_EDGES)
                    engine.dma_start(rec[:, h, v, :], rec1[bass.ds(row, P), :]).then_inc(s_rec[h], 16)

            with nc.Block() as block:
                @block.sync
                def _(sp):
                    sp.wait_ge(s_zero, 2)
                    for v in range(BATCH1):
                        sp.dma_start(wfc1[16 * v:16 * v + 16, v // 2, (v % 2) * 64:(v % 2) * 64 + 64], A["Wfc1"]).then_inc(s_w, 16)
                    for v in range(2):
                        sp.dma_start(wfc2[64 * v:64 * v + 64, v, :], A["Wfc2"]).then_inc(s_w, 16)
                    sp.dma_start(vis_start[:, :], tab["start"].rearrange("(o v) -> o v", o=1)).then_inc(s_tab, 16)
                    sp.dma_start(first_node[:, :], tab["bucket"][0:G1.visits].rearrange("(o v) -> o v", o=1).broadcast_to([P, G1.visits])).then_inc(s_tab, 16)
                    sp.wait_ge(s_tab, 32)

                    for h in range(AHEAD):
                        load_records(sp, 0, 0, h, s_free, True)
                    with sp.Fori(1, BATCHES1 // AHEAD) as t:
                        for h in range(AHEAD):
                            load_records(sp, 0, t, h, s_free, False)

                @block.gpsimd
                def _(pool):
                    nc.gpsimd.memset(wfc1[:, :, :], 0.0).then_inc(s_zero, 1)
                    nc.gpsimd.memset(wfc2[:, :, :], 0.0).then_inc(s_zero, 1)

                    def group(t, i, first):
                        n = t * RING + i
                        if not first:
                            pool.wait_ge(s_msg, n - RING + 1)
                        pool.wait_ge(s_rec[i // GPB1], (t + 1) * LOADED)
                        pool.sem_inc(s_begun, 1)
                        for v in range(VG):
                            nc.gpsimd.indirect_dma_start(out=fg[:, i, v, :], out_offset=None, in_=f_tab,
                                                         in_offset=bass.IndirectOffsetOnAxis(ap=rec[:, i // GPB1, i % GPB1 * VG + v, REC1 - 2:REC1 - 1].bitcast(i32), axis=0)).then_inc(s_fg[i // GPB1], 16)

                    for i in range(RING):
                        group(0, i, True)
                    with pool.Fori(1, BATCHES1 // AHEAD) as t:
                        for i in range(RING):
                            group(t, i, False)

                @block.vector
                def _(dve):
                    nc.vector.memset(run[:, :, :, :], 0.0).then_inc(s_prep, 1)
                    nc.vector.memset(ones[:, :], 1.0).then_inc(s_prep, 1)
                    nc.vector.memset(onehot[:, :, :, :, :], 0.0).then_inc(s_prep, 1)
                    nc.vector.memset(same[:, 0:1], 0.0).then_inc(s_prep, 1)
                    dve.wait_ge(s_tab, 32)
                    nc.vector.tensor_tensor(same[:, 1:], first_node[:, 1:], first_node[:, :G1.visits - 1], ALU.is_equal).then_inc(s_prep, 1)
                    dve.wait_ge(s_prep, 5)
                    nc.vector.tensor_scalar(first_node[:, :], first_node[:, :], float(G1.width), None, ALU.mult).then_inc(s_prep, 1)
                    dve.wait_ge(s_prep, 6)

                    def onehots(t, h, first=False):
                        k = t * AHEAD + h
                        if not first:
                            dve.wait_ge(s_m, (k - AHEAD + 1) * PAIRS)
                        dve.wait_ge(s_rec[h], (t + 1) * LOADED)
                        rows = rec[:, h, :, :]
                        nc.vector.tensor_tensor(rel[:, h % 2, :], rows[:, :, REC1 - 1].bitcast(i32), first_node[:, bass.ds(k * BATCH1, BATCH1)], ALU.subtract).then_inc(s_dve, 1)
                        dve.wait_ge(s_dve, k * 2 + 1)
                        oh = onehot[:, h, :, 3, :]
                        nc.vector.tensor_tensor(oh, iota[:, 0:32].unsqueeze(1).broadcast_to([P, BATCH1, 32]),
                                                rel[:, h % 2, :].unsqueeze(2).broadcast_to([P, BATCH1, 32]), ALU.is_equal).then_inc(s_dve, 1)
                        dve.wait_ge(s_dve, k * 2 + 2)
                        nc.vector.tensor_tensor(onehot_sh[:, h, :, :, :], oh.unsqueeze(2).broadcast_to([P, BATCH1, 4, 32]),
                                                rows[:, :, 16:20].unsqueeze(3).broadcast_to([P, BATCH1, 4, 32]), ALU.mult).then_inc(s_oh, 1)

                    def message(t, h, g, step, first):
                        i, k = h * GPB1 + g, t * AHEAD + h
                        if step == 0:
                            if g == 0 and not first:
                                dve.wait_ge(s_m, (k - 1) * PAIRS)
                            dve.wait_ge(s_fg[h], (t + 1) * LOADED)
                            dve.wait_ge(s_wt, k * GPB1 + g + 1)
                        w = ps_w[:, g, :, :, :].rearrange("p b v w -> p (b v) w")
                        part, c = step % 2, (0, 64, 128, 160)[step]
                        to = prod[:, h % 2, g * VG:(g + 1) * VG, part, :]
                        if step < 2:
                            nc.vector.tensor_tensor(to[:, :, 0:NS], w[:, :, c:c + NS], fg[:, i, :, 0:NS], ALU.mult)
                        else:
                            last = nc.vector.tensor_tensor(to[:, :, NS:D0].rearrange("p v (i u) -> p v i u", u=NV),
                                                           w[:, :, c:c + NV].unsqueeze(2).broadcast_to([P, VG, 3, NV]),
                                                           fg[:, i, :, NS:D0].rearrange("p v (i u) -> p v i u", u=NV), ALU.mult)
                            if step == 3:
                                last.then_inc(s_msg, 1)

                    def running(k, par, at, first=False):
                        if at == 0 and not first:
                            dve.wait_ge(s_st[par], (k - par) * (STORED // 2))
                        if at % 2 == 0:
                            dve.wait_ge(s_m, k * PAIRS + at // 2 + 1)
                        no = k * BATCH1 + at
                        before = run[:, par, at - 1, :] if at else run[:, 1 - par, BATCH1 - 1, :]
                        if not (first and k == 0 and at == 0):
                            dve.wait_ge(s_run, no)
                        v = at % 2
                        nc.vector.scalar_tensor_tensor(run[:, par, at, :], before, same[:, bass.ds(no, 1)],
                                                       ps_m[:, at // 2 % 2, v * W1_:(v + 1) * W1_], ALU.mult, ALU.add).then_inc(s_run, 1)

                    def batch(t, h, first=0, last=False, begin=False):
                        k = t * AHEAD + h
                        par = h % 2
                        for step in range(4):
                            message(t, h, 0, step, first >= 2)
                            if first < 2:
                                running(k - 2, par, VG + step, first >= 1)
                        for step in range(4):
                            message(t, h, 1, step, first >= 2)
                            if first < 3:
                                running(k - 1, 1 - par, step, first >= 1)
                        if not last:
                            onehots(t + (h + 1) // AHEAD, (h + 1) % AHEAD, begin and h < AHEAD - 1)

                    onehots(0, 0, True)
                    for h in range(AHEAD):
                        batch(0, h, first=max(0, 3 - h), begin=True)
                    with dve.Fori(1, BATCHES1 // AHEAD - 1) as t:
                        for h in range(AHEAD):
                            batch(t, h)
                    for h in range(AHEAD):
                        batch(BATCHES1 // AHEAD - 1, h, last=(h == AHEAD - 1))
                    for at in range(VG, BATCH1):
                        running(BATCHES1 - 2, 0, at)
                    for at in range(BATCH1):
                        running(BATCHES1 - 1, 1, at)

                @block.scalar
                def _(act):
                    def copy_scalars(t, h, first=False):
                        act.wait_ge(s_rec[h], (t + 1) * LOADED)
                        if not first:
                            act.wait_ge(s_t, t * AHEAD + h)
                        nc.scalar.copy(scal[:, :, :], rec[:, h, :, 0:16]).then_inc(s_scal, 1)

                    def copy_transposed(k, first=False):
                        if not first:
                            act.wait_ge(s_h, k)
                        act.wait_ge(s_t, k + 1)
                        nc.scalar.copy(scal_t[:, :], ps_t[:, 0:P]).then_inc(s_scal_t, 1)

                    def silu(k, par, first=False):
                        if not first:
                            act.wait_ge(s_wt, (k - 1) * GPB1)
                        act.wait_ge(s_h, k + 1)
                        nc.scalar.activation(hidden[:, par, :, :], ps_h[:, :, :], ACT.Silu, scale=0.25).then_inc(s_hid, 1)

                    def store(k, par):
                        act.wait_ge(s_run, (k + 1) * BATCH1)
                        for g in range(GPB1):
                            act.dma_start(sums_tab[bass.ds(k * BATCH1 + g * VG, VG), :, :].rearrange("v p w -> p v w"),
                                          run[:, par, g * VG:(g + 1) * VG, :]).then_inc(s_st[par], 16)

                    act.wait_ge(s_tab, 32)
                    for h in range(AHEAD):
                        load_records(act, 1, 0, h, s_free2, True)
                    for h in range(AHEAD):
                        copy_scalars(0, h, h == 0)
                        if h:
                            silu(h - 1, (h - 1) % 2, h < 3)
                        copy_transposed(h, h == 0)
                    load_records(act, 1, 1, 0, s_free2, False)

                    def batch(t, h, last=False):
                        k = t * AHEAD + h
                        copy_scalars(t, h)
                        silu(k - 1, (h + 1) % 2)
                        copy_transposed(k)
                        store(k - AHEAD, h % 2)
                        if not last:
                            load_records(act, 1, t + (h + 1) // AHEAD, (h + 1) % AHEAD, s_free2, False)

                    with act.Fori(1, BATCHES1 // AHEAD - 1) as t:
                        for h in range(AHEAD):
                            batch(t, h)
                    for h in range(AHEAD):
                        batch(BATCHES1 // AHEAD - 1, h, h == AHEAD - 1)
                    silu(BATCHES1 - 1, 1)
                    for k in range(BATCHES1 - AHEAD, BATCHES1):
                        store(k, k % 2)
                    for par in range(2):
                        act.wait_ge(s_st[par], STORED * (BATCHES1 // 2))

                @block.tensor
                def _(pe):
                    pe.wait_ge(s_w, 160)
                    pe.wait_ge(s_prep, 6)

                    def transposed(k, first=False):
                        pe.wait_ge(s_scal, k + 1)
                        if not first:
                            pe.wait_ge(s_scal_t, k)
                        nc.tensor.transpose(ps_t[:, 0:P], scal[:, :, :].rearrange("p v a -> p (v a)"), ident[:, :]).then_inc(s_t, 1)

                    def hidden_layer(k, first=False):
                        if not first:
                            pe.wait_ge(s_hid, k)
                        pe.wait_ge(s_scal_t, k + 1)
                        for j in range(PAIRS):
                            last = nc.tensor.matmul(ps_h[:, j, :], wfc1[:, j, :], scal_t[:, :], start=(j == 0), stop=(j == PAIRS - 1))
                        last.then_inc(s_h, 1)

                    def edge_weights(k, par, g, first=False):
                        if g == 0:
                            pe.wait_ge(s_hid, k + 1)
                        if not first:
                            pe.wait_ge(s_msg, (k - 1) * GPB1 + g + 1)
                        for b in range(2):
                            last = nc.tensor.matmul(ps_w[:, g, b, :, 0:192], hidden[:, par, 2 * g + b, :], wfc2[:, :, :], start=True, stop=True)
                        last.then_inc(s_wt, 1)

                    def node_sums(k, h, j, first=False):
                        par = h % 2
                        if j == 0:
                            pe.wait_ge(s_oh, k + 1)
                        if j % 2 == 0:
                            pe.wait_ge(s_msg, k * GPB1 + j // 2 + 1)
                        if not first or j >= 2:
                            pe.wait_ge(s_run, (k * PAIRS + j - 1) * 2)
                        bank = ps_m[:, j % 2, :]
                        for v in range(2):
                            at = 2 * j + v
                            oh_sh = onehot_sh[:, h, at, :, :].rearrange("p c m -> p (c m)")
                            nc.tensor.matmul(bank[0:96, v * W1_:v * W1_ + D0], oh_sh[:, 0:96], prod[:, par, at, 1, :], start=(v == 0), stop=False)
                            nc.tensor.matmul(bank[96:128, v * W1_:v * W1_ + D0], oh_sh[:, 96:128], prod[:, par, at, 0, :], start=(v == 0), stop=False, tile_position=(0, 96))
                            last = nc.tensor.matmul(bank[:, v * W1_ + D0:(v + 1) * W1_], onehot[:, h, at, :, :].rearrange("p c m -> p (c m)"), ones[:, :],
                                                    start=False, stop=(v == 1))
                        last.then_inc(s_m, 1)

                    def batch(t, h, first=0, last=0):
                        k, before = t * AHEAD + h, (h - 1) % AHEAD
                        edge_weights(k, h % 2, 0, first == 2)
                        edge_weights(k, h % 2, 1, first == 2)
                        if first < 2:
                            node_sums(k - 1, before, 0, first == 1)
                            node_sums(k - 1, before, 1, first == 1)
                        if last < 2:
                            hidden_layer(k + 1)
                        if last < 1:
                            transposed(k + 2)
                        if first < 2:
                            node_sums(k - 1, before, 2)
                            node_sums(k - 1, before, 3)

                    transposed(0, True)
                    hidden_layer(0, True)
                    transposed(1)
                    for h in range(AHEAD):
                        batch(0, h, first=max(0, 2 - h))
                    with pe.Fori(1, BATCHES1 // AHEAD - 1) as t:
                        for h in range(AHEAD):
                            batch(t, h)
                    for h in range(AHEAD):
                        batch(BATCHES1 // AHEAD - 1, h, last=max(0, h - 1))
                    for j in range(PAIRS):
                        node_sums(BATCHES1 - 1, AHEAD - 1, j)

        with ExitStack() as ctx:
            sb, ps, sem = sb_in(ctx, "f_"), ps_in(ctx, "f_"), sem_in(ctx, "f_")
            CX, CY, CZ, C0, CB0, CBZ = range(6)
            OUT = D0 + 2
            BUCKETS = NODE_TILES * P // G1.width
            wl2 = sb("wl2", [P, 6, OUT])
            first_visit = sb("first_visit", [1, BUCKETS + 1])
            last_visit = sb("last_visit", [1, BUCKETS])
            last_i = sb("last_i", [1, BUCKETS], i32)
            factor2 = sb("factor2", [P, 6])
            cur = sb("cur", [P, 2, 4, W1_])
            ta = sb("ta", [P, 2, 4, 4, 32])
            tb = sb("tb", [P, 2, 4, 4, 32])
            base = sb("base", [P, 2, D0])
            count = sb("count", [P, 2, 4])
            y = sb("y", [P, 2, D0])
            stats = sb("stats", [P, 2, 6])
            mean_var = sb("mean_var", [P, 2, 2])
            std = sb("std", [P, 2, 1])
            rstd = sb("rstd", [P, 2, 1])
            x2 = sb("x2", [P, 2, D0])
            ps_ta = [ps(f"ps_ta{r}", [P, 512]) for r in range(2)]
            ps_tb = [ps(f"ps_tb{r}", [P, 512]) for r in range(2)]
            ps_o = [ps(f"ps_o{r}", [P, 512]) for r in range(2)]
            WEIGHTS = 16 * 16
            s_zero, s_scaled, s_first, s_t, s_ta, s_o = (sem(n) for n in ("zero", "scaled", "first", "t", "ta", "o"))
            s_cur = [[sem(f"cur{h}_{r}") for r in range(2)] for h in range(2)]
            s_last = sem("last")
            s_y, s_bn, s_var, s_std, s_rstd, s_x2 = (sem(n) for n in ("y", "bn", "var", "std", "rstd", "x2"))
            s_gate = sem("gate")
            s_base = [sem(f"base{r}") for r in range(2)]
            s_out = [sem(f"out{r}") for r in range(2)]
            s_w = sem("w")
            MORE = P - NV - 1

            def load_sums(engine, q, i, r, first):
                if not first:
                    engine.wait_ge(s_t, i - 1)
                engine.wait_ge(s_last, 2)
                for b in (q, q + 1):
                    row = engine.value_load(last_i[0:1, bass.ds(i * 4 + b, 1)], min_val=0, max_val=G1.visits - 1)
                    engine.dma_start(cur[:, r, b, :], sums_tab[bass.ds(row, 1), :, :].rearrange("o p w -> p (o w)")).then_inc(s_cur[q // 2][r], 16)

            with nc.Block() as block:
                @block.sync
                def _(sp):
                    sp.dma_start(first_visit[:, :], scratch["tables1"]["vb"][0:BUCKETS + 1].rearrange("(o b) -> o b", o=1)).then_inc(s_first, 16)
                    sp.wait_ge(s_zero, 1)
                    S_, V_, A_ = A["Wl2_s"], A["Wl2_v"], A["Wa"]
                    al = D0
                    pieces = [(wl2[0:64, C0, 0:64], S_[0:64, :]), (wl2[0:64, C0, al:al + 1], A_[0:64, :]),
                              (wl2[64:96, C0, 64:96], V_[64:96, :]), (wl2[96:128, C0, 96:128], V_[64:96, :]),
                              (wl2[0:64, CX, 64:96], V_[0:64, :]), (wl2[64:96, CX, 0:64], S_[64:96, :]), (wl2[64:96, CX, al:al + 1], A_[64:96, :]),
                              (wl2[0:64, CY, 96:128], V_[0:64, :]), (wl2[96:128, CY, 0:64], S_[64:96, :]), (wl2[96:128, CY, al:al + 1], A_[64:96, :]),
                              (wl2[0:64, CZ, 128:160], V_[0:64, :]),
                              (wl2[MORE:MORE + NV, CB0, 128:160], V_[64:96, :]), (wl2[P - 1:P, CB0, al + 1:al + 2], A["ident"][0:1, 0:1]),
                              (wl2[MORE:MORE + NV, CBZ, 0:64], S_[64:96, :]), (wl2[MORE:MORE + NV, CBZ, al:al + 1], A_[64:96, :]),
                              (factor2[:, :], A["factor2"])]
                    for tile, dram in pieces:
                        sp.dma_start(tile, dram).then_inc(s_w, 16)

                    def load_base(i, r):
                        sp.dma_start(base[:, r, :], base_tab[bass.ds(i * P, P), :]).then_inc(s_base[r], 16)

                    def store(i, r):
                        sp.wait_ge(s_x2, i + 1)
                        sp.dma_start(out[bass.ds(i * P, P), :], x2[:, r, :]).then_inc(s_out[r], 16)

                    for r in range(2):
                        load_sums(sp, 0, r, r, True)
                        load_base(r, r)
                    load_sums(sp, 0, 2, 0, False)
                    with sp.Fori(1, NODE_TILES // 2 - 1) as t:
                        for r in range(2):
                            load_sums(sp, 0, t * 2 + r + 1, 1 - r, False)
                            sp.wait_ge(s_y, t * 2 + r - 1)
                            load_base(t * 2 + r, r)
                            store(t * 2 + r - 2, r)
                    load_sums(sp, 0, NODE_TILES - 1, 1, False)
                    for r in range(2):
                        sp.wait_ge(s_y, NODE_TILES - 3 + r)
                        load_base(NODE_TILES - 2 + r, r)
                        store(NODE_TILES - 4 + r, r)
                    for r in range(2):
                        store(NODE_TILES - 2 + r, r)
                    for r in range(2):
                        sp.wait_ge(s_out[r], 16 * (NODE_TILES // 2))

                @block.gpsimd
                def _(pool):
                    nc.gpsimd.memset(wl2[:, :, :], 0.0).then_inc(s_zero, 1)

                    for r in range(2):
                        load_sums(pool, 2, r, r, True)
                    with pool.Fori(1, NODE_TILES // 2) as t:
                        for r in range(2):
                            load_sums(pool, 2, t * 2 + r, r, False)

                @block.vector
                def _(dve):
                    dve.wait_ge(s_first, 16)
                    nc.vector.tensor_scalar(last_visit[:, :], first_visit[:, 1:], -1.0, float(G1.visits - 1), ALU.add, ALU.min).then_inc(s_last, 1)
                    dve.wait_ge(s_last, 1)
                    nc.vector.tensor_copy(last_i[:, :], last_visit[:, :]).then_inc(s_last, 1)
                    dve.wait_ge(s_w, WEIGHTS)
                    nc.vector.tensor_tensor(wl2[:, :, :], wl2[:, :, :], factor2[:, :].unsqueeze(2).broadcast_to([P, 6, OUT]), ALU.mult).then_inc(s_scaled, 1)

                    def finish(t, r, first):
                        i = t * 2 + r
                        dve.wait_ge(s_o, i + 1)
                        c = count[:, r, :]
                        nc.vector.tensor_scalar(c[:, 0:1], ps_o[r][:, D0 + 1:D0 + 2], 1.0, None, ALU.max).then_inc(s_gate, 1)
                        dve.wait_ge(s_gate, i * 4 + 1)
                        nc.vector.reciprocal(c[:, 1:2], c[:, 0:1]).then_inc(s_gate, 1)
                        dve.wait_ge(s_gate, i * 4 + 2)
                        nc.vector.tensor_scalar(c[:, 2:3], c[:, 1:2], vec[:, bass.ds(i, 1)], None, ALU.mult).then_inc(s_gate, 1)
                        dve.wait_ge(s_gate, i * 4 + 3)
                        nc.vector.tensor_scalar(c[:, 3:4], ps_o[r][:, D0:D0 + 1], c[:, 2:3], c[:, 2:3], ALU.mult, ALU.mult).then_inc(s_gate, 1)
                        dve.wait_ge(s_gate, i * 4 + 4)
                        dve.wait_ge(s_base[r], (t + 1) * 16)
                        nc.vector.scalar_tensor_tensor(y[:, r, :], ps_o[r][:, 0:D0], c[:, 3:4], base[:, r, :], ALU.mult, ALU.add).then_inc(s_y, 1)
                        dve.wait_ge(s_y, i + 1)
                        nc.vector.bn_stats(stats[:, r, :], y[:, r, :]).then_inc(s_bn, 1)
                        dve.wait_ge(s_w, WEIGHTS)
                        dve.wait_ge(s_bn, i + 1)
                        nc.vector.bn_aggr(mean_var[:, r, :], stats[:, r, :]).then_inc(s_var, 1)

                    def normalise(t, r, first):
                        j = t * 2 + r
                        dve.wait_ge(s_std, j + 1)
                        nc.vector.reciprocal(rstd[:, r, :], std[:, r, :]).then_inc(s_rstd, 1)
                        if not first:
                            dve.wait_ge(s_out[r], t * 16)
                        dve.wait_ge(s_rstd, j + 1)
                        nc.vector.tensor_scalar(x2[:, r, :], y[:, r, :], mean_var[:, r, 0:1], rstd[:, r, :], ALU.subtract, ALU.mult).then_inc(s_x2, 1)

                    finish(0, 0, True)
                    finish(0, 1, True)
                    normalise(0, 0, True)
                    finish(1, 0, False)
                    normalise(0, 1, True)
                    finish(1, 1, False)
                    with dve.Fori(2, NODE_TILES // 2) as t:
                        for r in range(2):
                            normalise(t - 1, r, False)
                            finish(t, r, False)
                    for r in range(2):
                        normalise(NODE_TILES // 2 - 1, r, False)

                @block.scalar
                def _(act):
                    def features(i, r, first):
                        if not first:
                            act.wait_ge(s_o, i - 1)
                        act.wait_ge(s_t, i + 1)
                        for dst_t, src_t in ((ta, ps_ta), (tb, ps_tb)):
                            nc.scalar.copy(dst_t[:, r, :, :, :], src_t[r][:, :].rearrange("p (q c n) -> p c q n", q=4, c=4)).then_inc(s_ta, 1)

                    def deviation(j, r):
                        act.wait_ge(s_var, j + 1)
                        nc.scalar.activation(std[:, r, :], mean_var[:, r, 1:2], ACT.Sqrt, bias=eps[:, :]).then_inc(s_std, 1)

                    features(0, 0, True)
                    features(1, 1, True)
                    deviation(0, 0)
                    with act.Fori(1, NODE_TILES // 2) as t:
                        features(t * 2, 0, False)
                        deviation(t * 2 - 1, 1)
                        features(t * 2 + 1, 1, False)
                        deviation(t * 2, 0)
                    deviation(NODE_TILES - 1, 1)

                @block.tensor
                def _(pe):
                    pe.wait_ge(s_scaled, 1)

                    def transposes(t, r, first):
                        i = t * 2 + r
                        if not first:
                            pe.wait_ge(s_ta, i * 2 - 2)
                        for h in range(2):
                            pe.wait_ge(s_cur[h][r], (t + 1) * 32)
                        for q in range(4):
                            nc.tensor.transpose(ps_ta[r][:, q * P:(q + 1) * P], cur[:, r, q, 0:P], ident[:, :])
                            last = nc.tensor.transpose(ps_tb[r][:, q * P:(q + 1) * P], cur[:, r, q, W1_ - P:W1_], ident[:, :])
                        last.then_inc(s_t, 1)

                    def products(i, r, first):
                        if not first:
                            pe.wait_ge(s_y, i - 1)
                        pe.wait_ge(s_ta, i * 2 + 2)
                        for c in range(4):
                            nc.tensor.matmul(ps_o[r][:, 0:OUT], ta[:, r, c, :, :].rearrange("p q n -> p (q n)"), wl2[:, c, :], start=(c == 0), stop=False)
                        nc.tensor.matmul(ps_o[r][:, 0:OUT], tb[:, r, C0, :, :].rearrange("p q n -> p (q n)"), wl2[:, CB0, :], start=False, stop=False)
                        nc.tensor.matmul(ps_o[r][:, 0:OUT], tb[:, r, CZ, :, :].rearrange("p q n -> p (q n)"), wl2[:, CBZ, :], start=False, stop=True).then_inc(s_o, 1)

                    transposes(0, 0, True)
                    transposes(0, 1, True)
                    products(0, 0, True)
                    transposes(1, 0, False)
                    products(1, 1, True)
                    transposes(1, 1, False)
                    with pe.Fori(2, NODE_TILES // 2) as t:
                        products(t * 2 - 2, 0, False)
                        transposes(t, 0, False)
                        products(t * 2 - 1, 1, False)
                        transposes(t, 1, False)
                    products(NODE_TILES - 2, 0, False)
                    products(NODE_TILES - 1, 1, False)



def _vectors_by_component(n):
    import numpy as np
    return np.concatenate([np.arange(64), 64 + 3 * np.arange(n)[None, :].repeat(3, 0).reshape(3, n).ravel() + np.repeat(np.arange(3), n)])


def kernel(**inputs):
    import numpy as np
    import concourse.bacc as bacc
    from concourse import mybir as my
    from concourse.bass_utils import run_bass_kernel_spmd

    G0, G1 = Grouping("src", 3, 32), Grouping("dst", 5, 32)
    a = {k: np.asarray(v) for k, v in inputs.items()}
    cols = _vectors_by_component(32)

    def pad(v, rows, value=0):
        return np.concatenate([v, np.full((rows - v.shape[0],) + v.shape[1:], value, v.dtype)])

    x = np.ascontiguousarray(pad(a["x"][:, cols], NODE_ROWS))
    edge_cols = np.concatenate([np.arange(8)] + [8 + 3 * np.arange(8) + c for c in (2, 0, 1)])
    Wu = a["L0_gnn_Wu"]
    arrays = {
        "src": pad(a["src"], SLOTS, PAD_NODE).reshape(P, TILES),
        "dst": pad(a["dst"], SLOTS, PAD_NODE).reshape(P, TILES),
        "next_dst": pad(a["dst"], SLOTS + 1, PAD_NODE)[1:].reshape(P, TILES),
        "edge_attr_32": pad(a["edge_attr_32"][:, edge_cols], SLOTS).reshape(P, TILES, 32),
        "edge_attr_16": pad(a["edge_attr_16"], SLOTS).reshape(P, TILES, 16),
        "edge_attr_4": pad(a["edge_attr_4"][:, [1, 2, 3, 0]], SLOTS).reshape(P, TILES, 4),
        "x": x,
        "xT": np.ascontiguousarray(x.T),
        "node_vec1": np.ascontiguousarray(pad(a["node_vec1"][:, 0], NODE_ROWS).reshape(NODE_TILES, P).T),
        "WmT": np.ascontiguousarray(np.concatenate([a["L0_gnn_Wm"][cols], a["L0_gnn_bm"][None]]).T),
        "Wu": np.ascontiguousarray(np.concatenate([Wu[:160][cols], Wu[160:]])[:, cols]),
        "bu": a["L0_gnn_bu"][cols],
        **{n: a["L0_gnn_" + n] for n in ("W1", "W2", "W3", "W4")},
        **{n: a["L1_gnn_" + n] for n in ("Wfc1", "Wfc2", "Wsc0", "Wsc1", "Wl1_0", "Wl1_1", "Wl2_s", "Wl2_v", "Wa")},
    }
    arrays.update(rank_constants([G0, G1]))
    k = np.arange(P)
    half = 2.0 ** -0.5
    f0 = np.zeros((P, 4))
    f0[:, 0] = np.where(k < 64, 512 ** -0.5, 256 ** -0.5) * half
    f0[:, 1] = np.where(k < 64, 512 ** -0.5, 768 ** -0.5) * half
    arrays["factor0"] = f0.astype(np.float32)
    arrays["spread0"] = ((k[:, None] // 8 == np.arange(16)).astype(np.float32) - (np.arange(16) == 0)).astype(np.float32)
    arrays["in_bucket0"] = (k % 8).astype(np.float32).reshape(P, 1)
    arrays["factor1"] = np.stack([np.where(k < 64, 64 ** -0.5, 32 ** -0.5), np.full(P, 32 ** -0.5)], 1).astype(np.float32)
    f2 = np.full((P, 6), 96 ** -0.5 / 8)
    f2[64:, 0] *= 3 ** -0.5
    f2[64:, 1] *= 3 ** -0.5
    f2[:, 5] *= 3 ** -0.5
    f2[P - 1, 4] = 1.0
    arrays["factor2"] = f2.astype(np.float32)

    nc = bacc.Bacc("TRN2", target_bir_lowering=False, num_devices=1)
    f32, int32 = my.dt.float32, my.dt.int32
    A, given = {"groupings": (G0, G1)}, {}
    for n, v in arrays.items():
        v = np.ascontiguousarray(v)
        given["in_" + n] = v
        A[n] = nc.dram_tensor("in_" + n, v.shape, my.dt.from_np(v.dtype), kind="ExternalInput").ap()

    def scratch(n, shape, dt=f32):
        return nc.dram_tensor(n, shape, dt, kind="Internal").ap()

    def tables(g):
        return {"vb": scratch(f"{g.name}_vb", (1024,)), "s": scratch(f"{g.name}_s", (1024,)),
                "bucket": scratch(f"{g.name}_bucket", (P * g.cols,)), "start": scratch(f"{g.name}_start", (P * g.cols,), int32)}

    S = {"rec0": scratch("rec0", (SLOTS, 34)), "rec1": scratch("rec1", (SLOTS, 22)), "f": scratch("f", (NODE_ROWS, 160)),
         "base": scratch("base", (NODE_ROWS, 160)), "sums": scratch("sums", (G1.visits, P, 161)), "tables0": tables(G0), "tables1": tables(G1)}
    out = nc.dram_tensor("out", (NODE_ROWS, 160), f32, kind="ExternalOutput").ap()
    gnn_kernel(nc, A, out, S)
    r = run_bass_kernel_spmd(nc, [given], core_ids=[0])
    got = r.results[0]["out"]
    back = np.empty(160, np.int64)
    back[cols] = np.arange(160)
    return np.ascontiguousarray(got[:N_NODES][:, back])
```

```python
import concourse.bass as bass
from concourse import mybir
from contextlib import ExitStack
import numpy as np

fp32 = mybir.dt.float32
bf16 = mybir.dt.bfloat16
i32 = mybir.dt.int32
ALU = mybir.AluOpType
ACT = mybir.ActivationFunctionType
AX = mybir.AxisListType

P = 128
N_NODES = 6250
N_EDGES = 200000
GROUPS = 8
Q = GROUPS // 4
TILES = 1568
STEPS = TILES // GROUPS
SLOTS = P * TILES
NODE_TILES = 50
NODE_ROWS = NODE_TILES * P
PAD_NODE = NODE_ROWS - 1
ROUND = 32
HI, LO = 32, 64
LO_BITS = 6
SPAN = 8


class Grouping:

    def __init__(self, name, shift, by_tile):
        self.name, self.shift, self.by_tile = name, shift, by_tile
        self.width = 1 << shift
        self.buckets = -(-N_NODES // self.width)
        self.step = SPAN // self.width
        self.tiles = -(-N_EDGES // P)
        self.tile_cols = -(-(self.tiles + ROUND) // P)
        most = self.tiles + self.buckets // self.step if by_tile else self.buckets + N_EDGES // P
        self.visits = -(-most // ROUND) * ROUND
        self.cols = -(-self.visits // P)


class Rank:
    pass


def alloc_rank(ctx, nc, g, banks):
    R = Rank()

    def sb(n, s, d=fp32):
        return ctx.enter_context(nc.sbuf_tensor(f"{g.name}_{n}", s, d))

    def sem(n):
        return ctx.enter_context(nc.semaphore(f"{g.name}_{n}"))

    R.digit_i = sb("digit_i", [P, TILES], i32)
    R.digits = sb("digits", [P, 2, TILES], bf16)
    R.onehot_hi = sb("onehot_hi", [P, 2, GROUPS, HI], bf16)
    R.onehot_lo = sb("onehot_lo", [P, 2, GROUPS, LO], bf16)
    R.hi_t = sb("hi_t", [P, Q, P], bf16)
    R.hi_t32 = sb("hi_t32", [P, Q, P])
    R.earlier = sb("earlier", [P, GROUPS, P], bf16)
    R.count = sb("count", [P, Q, 4, LO])
    R.fresh = sb("fresh", [P, Q, 4, LO])
    R.by_group = sb("by_group", [P, Q, LO])
    R.picked = sb("picked", [P, GROUPS, LO])
    R.pos_f = sb("pos_f", [P, TILES])
    R.small = sb("small", [P, 16, LO])
    R.small_i = sb("small_i", [P, 2, LO], i32)
    row = P * g.tile_cols if g.by_tile else g.buckets
    R.vb_row = sb("vb_row", [P, row + 1])
    R.s_row = sb("s_row", [P, g.buckets])
    R.ds_row = sb("ds_row", [P, row])
    R.mask = sb("mask", [P, row])
    R.junk = sb("junk", [P, row])
    R.ones = sb("ones", [P, row])
    if g.by_tile:
        R.tile_last = sb("tile_last", [P, g.tile_cols])
        R.last_row = sb("last_row", [P, row + 1])
        R.steps_i = sb("steps_i", [P, row], i32)
    R.vtab = sb("vtab", [P, 4, g.cols])
    R.vtab_i = sb("vtab_i", [P, g.cols], i32)
    R.ps_t, R.ps_eq, R.ps_g, R.ps_h, R.ps_s = banks
    R.s_onehot_ready = sem("onehot_ready")
    R.s_onehot_counted = sem("onehot_counted")
    R.s_counted = sem("counted")
    R.s_sums_ready = sem("sums_ready")
    R.s_sums_done = sem("sums_done")
    R.s_hi_t_ps = sem("hi_t_ps")
    R.s_hi_t_ready = sem("hi_t_ready")
    R.s_eq_ps = sem("eq_ps")
    R.s_earlier_ready = sem("earlier_ready")
    R.s_hist_ps = sem("hist_ps")
    R.s_count_ready = sem("count_ready")
    R.s_rank_ps = sem("rank_ps")
    R.s_rank_read = sem("rank_read")
    R.s_dve = sem("dve")
    R.s_tables_ready = sem("tables_ready")
    R.s_tables_out = sem("tables_out")
    R.s_rows_in = sem("rows_in")
    R.s_visits_ready = sem("visits_ready")
    R.s_visits_out = sem("visits_out")
    return R


def rank_vector(nc, dve, g, R, C, node, s_node, rounds, needed=None):
    done = [0]

    def link(ins):
        done[0] += 1
        ins.then_inc(R.s_dve, 1)
        dve.wait_ge(R.s_dve, done[0])

    link(nc.vector.memset(R.ones[:, :], 1.0))
    dve.wait_ge(s_node, 16)
    link(nc.vector.tensor_scalar(R.digit_i[:, :], node[:, :], g.shift + LO_BITS, None, ALU.logical_shift_right))
    link(nc.vector.tensor_copy(R.digits[:, 0, :], R.digit_i[:, :]))
    link(nc.vector.tensor_scalar(R.digit_i[:, :], node[:, :], g.shift, LO - 1, ALU.logical_shift_right, ALU.bitwise_and))
    link(nc.vector.tensor_copy(R.digits[:, 1, :], R.digit_i[:, :]))

    def onehots(step, par):
        for d, (tile, size) in enumerate(((R.onehot_hi, HI), (R.onehot_lo, LO))):
            last = nc.vector.tensor_tensor(
                tile[:, par, :, :], R.digits[:, d, bass.ds(step * GROUPS, GROUPS)].unsqueeze(2).broadcast_to([P, GROUPS, size]),
                C["iota"][:, 0:size].unsqueeze(1).broadcast_to([P, GROUPS, size]), ALU.is_equal)
            if d == 0:
                last.then_inc(R.s_onehot_ready, 1)
        return last

    for par in range(2):
        onehots(par, par).then_inc(R.s_onehot_ready, 1)
    with dve.Fori(1, STEPS // 2) as t:
        for par in range(2):
            dve.wait_ge(R.s_onehot_counted, t * 2 + par - 1)
            onehots(t * 2 + par, par).then_inc(R.s_onehot_ready, 1)

    small = R.small
    dve.wait_ge(R.s_counted, 1)
    own = C["own_group"].unsqueeze(1).broadcast_to([P, Q, 4, LO])
    link(nc.vector.tensor_tensor(R.fresh[:, :, :, :], R.ps_h[:, :, :, :], own, ALU.mult))
    link(nc.vector.tensor_reduce(R.by_group[:, :, :], R.fresh[:, :, :, :].rearrange("p q g l -> p q l g"), AX.X, ALU.add))
    nc.vector.tensor_reduce(small[:, 0, :], R.by_group[:, :, :].rearrange("p q l -> p l q"), AX.X, ALU.add).then_inc(R.s_sums_ready, 1)
    dve.wait_ge(R.s_sums_done, 1)
    link(nc.vector.tensor_copy(small[:, 1:3, :], R.ps_s[:, 0:2 * LO].rearrange("p (a l) -> p a l", l=LO)))
    link(nc.vector.tensor_tensor_scan(small[:, 3, :], R.ones[:, 0:LO], small[:, 1, :], 0.0, ALU.mult, ALU.add))
    link(nc.vector.tensor_scalar(small[:, 4, :], small[:, 1, :], float(P - 1), None, ALU.add))
    link(nc.vector.tensor_copy(R.small_i[:, 0, :], small[:, 4, :]))
    link(nc.vector.tensor_scalar(R.small_i[:, 1, :], R.small_i[:, 0, :], 7, None, ALU.logical_shift_right))
    link(nc.vector.tensor_copy(small[:, 5, :], R.small_i[:, 1, :]))
    link(nc.vector.tensor_scalar(small[:, 6, :], small[:, 5, :], 1.0, None, ALU.max))
    link(nc.vector.tensor_tensor_scan(small[:, 7, :], R.ones[:, 0:LO], small[:, 6, :], 0.0, ALU.mult, ALU.add))
    link(nc.vector.tensor_copy(small[:, 8, 0:1], small[:, 3, LO - 1:LO]))
    nc.vector.tensor_copy(small[:, 8, 1:2], small[:, 7, LO - 1:LO]).then_inc(R.s_sums_ready, 1)
    dve.wait_ge(R.s_sums_done, 2)
    link(nc.vector.tensor_copy(small[:, 8, 2:4], R.ps_s[:, 2 * LO:2 * LO + 2]))
    link(nc.vector.tensor_tensor(small[:, 9, :], small[:, 3, :], small[:, 1, :], ALU.subtract))
    link(nc.vector.tensor_scalar(small[:, 9, :], small[:, 9, :], small[:, 8, 2:3], None, ALU.add))
    link(nc.vector.tensor_tensor(small[:, 10, :], small[:, 7, :], small[:, 6, :], ALU.subtract))
    link(nc.vector.tensor_scalar(small[:, 10, :], small[:, 10, :], small[:, 8, 3:4], None, ALU.add))
    nc.vector.scalar_tensor_tensor(small[:, 11, :], small[:, 10, :], -float(P), small[:, 9, :], ALU.mult, ALU.add).then_inc(R.s_tables_ready, 1)
    link(nc.vector.tensor_tensor(small[:, 13, :], small[:, 9, :], small[:, 2, :], ALU.add))
    for q in range(Q):
        last = nc.vector.tensor_tensor(R.count[:, q, :, :], C["own_group"], small[:, 13, :].unsqueeze(1).broadcast_to([P, 4, LO]), ALU.mult)
        if q < Q - 1:
            link(last)
            link(nc.vector.tensor_tensor(small[:, 13, :], small[:, 13, :], R.by_group[:, q, :], ALU.add))
    last.then_inc(R.s_count_ready, 1)
    def places():
        first = done[0]
        per_step = 2
        for par in range(2):
            onehots(par, par).then_inc(R.s_onehot_ready, 1)

        def place(step, par):
            base = step * per_step + first
            dve.wait_ge(R.s_hist_ps, step + 1)
            nc.vector.tensor_tensor(R.fresh[:, :, :, :], R.ps_h[:, :, :, :], own, ALU.mult).then_inc(R.s_dve, 1)
            dve.wait_ge(R.s_rank_ps, step + 1)
            nc.vector.tensor_tensor(R.picked[:, :, :], R.ps_g[:, :, :], R.onehot_lo[:, par, :, :], ALU.mult).then_inc(R.s_dve, 1)
            dve.wait_ge(R.s_dve, base + 1)
            nc.vector.tensor_tensor(R.count[:, :, :, :], R.count[:, :, :, :], R.fresh[:, :, :, :], ALU.add).then_inc(R.s_count_ready, 1)
            dve.wait_ge(R.s_dve, base + 2)
            nc.vector.tensor_reduce(R.pos_f[:, bass.ds(step * GROUPS, GROUPS)], R.picked[:, :, :], AX.X, ALU.add).then_inc(R.s_rank_read, 1)

        with dve.Fori(0, STEPS // 2 - 1) as t:
            for par in range(2):
                place(t * 2 + par, par)
                onehots(t * 2 + par + 2, par).then_inc(R.s_onehot_ready, 1)
        for par in range(2):
            place(STEPS - 2 + par, par)
        done[0] = first + per_step * STEPS

    def count_rounds(n_visits):
        link(nc.vector.tensor_scalar(R.small[0:1, 14, 0:1], n_visits, float(ROUND - 1), None, ALU.add))
        link(nc.vector.tensor_copy(R.small_i[0:1, 0, 0:1], R.small[0:1, 14, 0:1]))
        link(nc.vector.tensor_scalar(rounds, R.small_i[0:1, 0, 0:1], 5, None, ALU.logical_shift_right))

    def sum_below(row, values, bound, out):
        n = row.shape[-1]
        link(nc.vector.tensor_scalar(R.mask[:, 0:n], row, bound, None, ALU.is_le))
        link(nc.vector.tensor_tensor_reduce(out=R.junk[:, 0:n], in0=R.mask[:, 0:n], in1=values, scale=1.0, scalar=0.0,
                                            op0=ALU.mult, op1=ALU.add, accum_out=out))

    def visits_by_tile():
        tiles = P * g.tile_cols
        vb, ds = R.vb_row[:, 0:tiles], R.ds_row[:, :]
        dve.wait_ge(R.s_rows_in, 16)
        for c in range(g.tile_cols):
            sum_below(R.s_row[:, :], R.ones[:, 0:g.buckets], C["tile_end"][:, c:c + 1], R.tile_last[:, c:c + 1])
        nc.vector.tensor_scalar(R.tile_last[:, :], R.tile_last[:, :], -1.0, None, ALU.add).then_inc(R.s_tables_ready, 1)
        link(nc.vector.memset(R.last_row[:, 0:1], 0.0))
        dve.wait_ge(R.s_rows_in, 32)
        link(nc.vector.tensor_tensor(ds, R.last_row[:, 1:], R.last_row[:, 0:tiles], ALU.subtract))
        link(nc.vector.tensor_copy(R.steps_i[:, :], ds))
        link(nc.vector.tensor_scalar(R.steps_i[:, :], R.steps_i[:, :], g.step.bit_length() - 1, None, ALU.logical_shift_right))
        link(nc.vector.tensor_copy(ds, R.steps_i[:, :]))
        link(nc.vector.tensor_scalar(ds, ds, 1.0, None, ALU.add))
        link(nc.vector.memset(R.vb_row[:, 0:1], 0.0))
        link(nc.vector.tensor_tensor_scan(R.vb_row[:, 1:], R.ones[:, :], ds, 0.0, ALU.mult, ALU.add))
        count_rounds(R.vb_row[0:1, g.tiles:g.tiles + 1])
        link(nc.vector.scalar_tensor_tensor(R.last_row[:, 0:tiles], vb, -float(g.step), R.last_row[:, 0:tiles], ALU.mult, ALU.add))
        nc.vector.tensor_copy(ds[:, 0:1], R.last_row[:, 0:1]).then_inc(R.s_dve, 1)
        done[0] += 1
        link(nc.vector.tensor_tensor(ds[:, 1:], R.last_row[:, 1:tiles], R.last_row[:, 0:tiles - 1], ALU.subtract))
        for c in range(g.cols):
            visit = C["visit_" + g.name][:, c:c + 1]
            sum_below(vb, R.ones[:, :], visit, R.vtab[:, 0, c:c + 1])
            link(nc.vector.tensor_tensor_reduce(out=R.junk[:, :], in0=R.mask[:, :], in1=ds, scale=1.0, scalar=0.0,
                                                op0=ALU.mult, op1=ALU.add, accum_out=R.vtab[:, 1, c:c + 1]))
        link(nc.vector.scalar_tensor_tensor(R.vtab[:, 2, :], C["visit_" + g.name][:, 0:g.cols], float(g.step), R.vtab[:, 1, :], ALU.mult, ALU.add))
        link(nc.vector.tensor_scalar(R.vtab[:, 2, :], R.vtab[:, 2, :], float(g.buckets - 1), None, ALU.min))
        link(nc.vector.tensor_scalar(R.vtab[:, 3, :], R.vtab[:, 0, :], float(P), -float(P), ALU.mult, ALU.add))
        link(nc.vector.tensor_scalar(R.vtab[:, 3, :], R.vtab[:, 3, :], float(g.tiles * P), None, ALU.min))
        nc.vector.tensor_copy(R.vtab_i[:, :], R.vtab[:, 3, :]).then_inc(R.s_visits_ready, 1)

    def visits_by_bucket():
        dve.wait_ge(R.s_rows_in, 32)
        count_rounds(R.vb_row[0:1, g.buckets:])
        nc.vector.tensor_copy(R.ds_row[:, 0:1], R.s_row[:, 0:1]).then_inc(R.s_dve, 1)
        done[0] += 1
        link(nc.vector.tensor_tensor(R.ds_row[:, 1:], R.s_row[:, 1:], R.s_row[:, :g.buckets - 1], ALU.subtract))
        for c in range(g.cols):
            link(nc.vector.tensor_scalar(R.mask[:, :], R.vb_row[:, 0:g.buckets], C["visit_" + g.name][:, c:c + 1], None, ALU.is_le))
            link(nc.vector.tensor_tensor_reduce(out=R.junk[:, :], in0=R.mask[:, :], in1=R.ones[:, 0:g.buckets], scale=1.0, scalar=0.0,
                                                op0=ALU.mult, op1=ALU.add, accum_out=R.vtab[:, 0, c:c + 1]))
            link(nc.vector.tensor_tensor_reduce(out=R.junk[:, :], in0=R.mask[:, :], in1=R.ds_row[:, :], scale=1.0, scalar=0.0,
                                                op0=ALU.mult, op1=ALU.add, accum_out=R.vtab[:, 1, c:c + 1]))
        link(nc.vector.tensor_scalar(R.vtab[:, 2, :], R.vtab[:, 0, :], -1.0, None, ALU.add))
        link(nc.vector.scalar_tensor_tensor(R.vtab[:, 3, :], C["visit_" + g.name][:, 0:g.cols], float(P), R.vtab[:, 1, :], ALU.mult, ALU.add))
        link(nc.vector.tensor_scalar(R.vtab[:, 3, :], R.vtab[:, 3, :], float(N_EDGES), None, ALU.min))
        nc.vector.tensor_copy(R.vtab_i[:, :], R.vtab[:, 3, :]).then_inc(R.s_visits_ready, 1)

    if needed is None:
        places()
        visits_by_tile() if g.by_tile else visits_by_bucket()
    else:
        visits_by_tile() if g.by_tile else visits_by_bucket()
        with dve.If(needed(dve) > 0):
            places()


def rank_tensor(nc, pe, g, R, C, needed=None):
    def counts(par, start, stop):
        for q in range(Q):
            hi, lo = (tile[:, par, 4 * q:4 * q + 4, :].rearrange("p g k -> p (g k)") for tile in (R.onehot_hi, R.onehot_lo))
            last = nc.tensor.matmul(R.ps_h[:, q, :, :], hi, lo, start=start and q == 0, stop=stop and q == Q - 1)
        return last

    for par in range(2):
        pe.wait_ge(R.s_onehot_ready, par * 2 + 2)
        counts(par, par == 0, False).then_inc(R.s_onehot_counted, 1)
    with pe.Fori(1, STEPS // 2 - 1) as t:
        for par in range(2):
            pe.wait_ge(R.s_onehot_ready, t * 4 + (par * 2 + 2))
            counts(par, False, False).then_inc(R.s_onehot_counted, 1)
    for par in range(2):
        pe.wait_ge(R.s_onehot_ready, (STEPS - 1 + par) * 2)
        last = counts(par, False, par == 1)
        last.then_inc(R.s_onehot_counted if par == 0 else R.s_counted, 1)

    pe.wait_ge(R.s_sums_ready, 1)
    nc.tensor.matmul(R.ps_s[:, 0:LO], C["all_groups"], R.small[:, 0, :], start=True, stop=True)
    nc.tensor.matmul(R.ps_s[:, LO:2 * LO], C["groups_before"], R.small[:, 0, :], start=True, stop=True).then_inc(R.s_sums_done, 1)
    pe.wait_ge(R.s_sums_ready, 2)
    nc.tensor.matmul(R.ps_s[:, 2 * LO:2 * LO + 2], C["digits_before"], R.small[:, 8, 0:2], start=True, stop=True).then_inc(R.s_sums_done, 1)

    def step(s, par, first):
        pe.wait_ge(R.s_onehot_ready, s * 2 + (STEPS * 2 + 2))
        for q in range(Q):
            last = nc.tensor.transpose(R.ps_t[:, q, :], R.onehot_hi[:, par, 4 * q:4 * q + 4, :].rearrange("p g d -> p (g d)"), C["ident16"])
        last.then_inc(R.s_hi_t_ps, 1)
        pe.wait_ge(R.s_count_ready, s + 1)
        counts(par, True, True).then_inc(R.s_hist_ps, 1)
        if not first:
            pe.wait_ge(R.s_earlier_ready, s * Q)
        for b in range(4):
            nc.tensor.matmul(R.ps_eq[:, b, 0:Q, :], C["ident16"], C["not_earlier"], start=True, stop=False)
        pe.wait_ge(R.s_hi_t_ready, s * 2 + 2)
        for slot in range(GROUPS):
            b, q = slot // Q, slot % Q
            hi_t = R.hi_t[32 * b:32 * b + 32, q, :]
            last = nc.tensor.matmul(R.ps_eq[:, b, q, :], hi_t, hi_t, start=False, stop=(q == Q - 1), tile_position=(32 * b, 0))
            if slot % 4 == 3:
                last.then_inc(R.s_eq_ps, 1)
        if not first:
            pe.wait_ge(R.s_rank_read, s)
        for q in range(Q):
            nc.tensor.matmul(R.ps_g[:, 4 * q:4 * q + 4, :], R.hi_t32[:, q, :], R.count[:, q, :, :], start=(q == 0), stop=False)
        for slot in range(GROUPS):
            b, q = slot // Q, slot % Q
            if slot % 4 == 0:
                pe.wait_ge(R.s_earlier_ready, s * Q + slot // 4 + 1)
            last = nc.tensor.matmul(R.ps_g[:, 4 * q + b, :], R.earlier[:, slot, :], R.onehot_lo[:, par, 4 * q + b, :],
                                    start=False, stop=(slot == GROUPS - 1))
        last.then_inc(R.s_rank_ps, 1)

    def places():
        for par in range(2):
            step(par, par, par == 0)
        with pe.Fori(1, STEPS // 2) as t:
            for par in range(2):
                step(t * 2 + par, par, False)

    if needed is None:
        places()
    else:
        with pe.If(needed(pe) > 0):
            places()


def rank_scalar(nc, act, g, R, C, D, needed=None):
    def step(s, first):
        act.wait_ge(R.s_hi_t_ps, s + 1)
        if not first:
            act.wait_ge(R.s_rank_ps, s)
        nc.scalar.copy(R.hi_t[:, :, :], R.ps_t[:, :, :]).then_inc(R.s_hi_t_ready, 1)
        nc.scalar.copy(R.hi_t32[:, :, :], R.ps_t[:, :, :]).then_inc(R.s_hi_t_ready, 1)
        for b in range(Q):
            act.wait_ge(R.s_eq_ps, s * Q + b + 1)
            nc.scalar.activation(R.earlier[:, 4 * b:4 * b + 4, :].rearrange("p (b q) n -> p b q n", q=Q), R.ps_eq[:, 2 * b:2 * b + 2, 0:Q, :], ACT.Relu).then_inc(R.s_earlier_ready, 1)

    def places():
        for s in range(2):
            step(s, s == 0)
        with act.Fori(1, STEPS // 2) as t:
            for par in range(2):
                step(t * 2 + par, False)

    def row(a, n):
        return a[0:n].rearrange("(o b) -> o b", o=1).broadcast_to([P, n])

    def tables():
        act.wait_ge(R.s_tables_ready, 1)
        if g.by_tile:
            tiles = P * g.tile_cols
            act.dma_start(D["s"].rearrange("(h l) -> h l", l=LO), R.small[0:HI, 9, :]).then_inc(R.s_tables_out, 16)
            act.wait_ge(R.s_tables_out, 16)
            act.dma_start(R.s_row[:, :], row(D["s"], g.buckets)).then_inc(R.s_rows_in, 16)
            act.wait_ge(R.s_tables_ready, 2)
            act.dma_start(D["vb"][0:tiles].rearrange("(p c) -> p c", c=g.tile_cols), R.tile_last[:, :]).then_inc(R.s_tables_out, 16)
            act.wait_ge(R.s_tables_out, 32)
            act.dma_start(R.last_row[:, 1:], row(D["vb"], tiles)).then_inc(R.s_rows_in, 16)
        else:
            act.dma_start(D["vb"].rearrange("(h l) -> h l", l=LO), R.small[0:HI, 10, :]).then_inc(R.s_tables_out, 16)
            act.dma_start(D["s"].rearrange("(h l) -> h l", l=LO), R.small[0:HI, 11, :]).then_inc(R.s_tables_out, 16)
            act.wait_ge(R.s_tables_out, 32)
            act.dma_start(R.vb_row[:, :], row(D["vb"], g.buckets + 1)).then_inc(R.s_rows_in, 16)
            act.dma_start(R.s_row[:, :], row(D["s"], g.buckets)).then_inc(R.s_rows_in, 16)
        act.wait_ge(R.s_visits_ready, 1)
        act.dma_start(D["bucket"].rearrange("(p c) -> p c", c=g.cols), R.vtab[:, 2, :]).then_inc(R.s_visits_out, 16)
        act.dma_start(D["start"].rearrange("(p c) -> p c", c=g.cols), R.vtab_i[:, :]).then_inc(R.s_visits_out, 16)
        act.wait_ge(R.s_visits_out, 32)

    if needed is None:
        places()
        tables()
    else:
        tables()
        with act.If(needed(act) > 0):
            places()


def rank_constants(groupings):
    k = np.arange(P)
    gp, hi = k // 32, k % 32
    out = {
        "iota": np.tile(np.arange(P, dtype=np.float32), (P, 1)),
        "ident": np.eye(P, dtype=np.float32),
        "not_earlier": np.tile(-(k[:, None] >= k[None, :]).astype(np.float32), (1, Q)),
        "own_group": np.repeat(gp[:, None] == np.arange(4)[None, :], LO, axis=1).astype(np.float32),
        "all_groups": (hi[:, None] == hi[None, :]).astype(np.float32),
        "groups_before": ((hi[:, None] == hi[None, :]) & (gp[:, None] < gp[None, :])).astype(np.float32),
        "digits_before": ((gp[:, None] == gp[None, :]) & (hi[:, None] < hi[None, :])).astype(np.float32),
    }
    for g in groupings:
        out["visit_" + g.name] = np.arange(P * g.cols, dtype=np.float32).reshape(P, g.cols)
        if g.by_tile:
            out["tile_end"] = (np.arange(P * g.tile_cols, dtype=np.float32) * P + (P - 1)).reshape(P, g.tile_cols)
    return out



CHUNK = 2 * GROUPS
CHUNKS = TILES // CHUNK
WIDE = 28
WIDES = TILES // WIDE


class Scatter:

    def __init__(self, ctx, nc, s_begun, name, width, in_order=False):
        self.name, self.width = name, width
        self.stage = ctx.enter_context(nc.sbuf_tensor(f"{name}_stage", [P, 2, WIDE if in_order else CHUNK, width], fp32))
        self.place = ctx.enter_context(nc.sbuf_tensor(f"{name}_place", [P, 2, CHUNK], i32))
        self.s_in = [ctx.enter_context(nc.semaphore(f"{name}_in{r}")) for r in range(2)]
        self.s_stored = [ctx.enter_context(nc.semaphore(f"{name}_stored{r}")) for r in range(2)] if in_order else None
        self.s_out = [ctx.enter_context(nc.semaphore(f"{name}_out{r}")) for r in range(2)]
        self.s_begun = s_begun
        self.s_staged = ctx.enter_context(nc.semaphore(f"{name}_staged"))


def load_attributes(engine, S, parts, t, r, size=CHUNK):
    for dram, at in parts:
        engine.dma_start(S.stage[:, r, 0:size, at:at + dram.shape[2]], dram[:, bass.ds((t * 2 + r) * size, size), :]).then_inc(S.s_in[r], 16)


def load_all_attributes(sp, S, parts):
    for r in range(2):
        load_attributes(sp, S, parts, 0, r)
    with sp.Fori(1, CHUNKS // 2) as t:
        for r in range(2):
            sp.wait_ge(S.s_out[r], t * (16 * CHUNK))
            load_attributes(sp, S, parts, t, r)


def scatter_records(nc, pool, S, n_parts, src, dst, R, out):
    def chunk(t, r, first):
        c = t * 2 + r
        if not first:
            pool.wait_ge(S.s_out[r], t * (16 * CHUNK))
        pool.wait_ge(R.s_rank_read, c * 2 + 2)
        pool.sem_inc(S.s_begun, 1)
        at = bass.ds(c * CHUNK, CHUNK)
        nc.gpsimd.tensor_copy(S.stage[:, r, 0:CHUNK, S.width - 2].bitcast(i32), src[:, at]).then_inc(S.s_staged, 1)
        nc.gpsimd.tensor_copy(S.stage[:, r, 0:CHUNK, S.width - 1].bitcast(i32), dst[:, at]).then_inc(S.s_staged, 1)
        nc.gpsimd.tensor_copy(S.place[:, r, :], R.pos_f[:, at]).then_inc(S.s_staged, 1)
        pool.wait_ge(S.s_in[r], (t + 1) * (16 * n_parts))
        pool.wait_ge(S.s_staged, c * 3 + 3)
        pool.sem_inc(S.s_begun, 1)
        for j in range(CHUNK):
            nc.gpsimd.indirect_dma_start(out=out, out_offset=bass.IndirectOffsetOnAxis(ap=S.place[:, r, j:j + 1], axis=0),
                                         in_=S.stage[:, r, j, :], in_offset=None).then_inc(S.s_out[r], 16)

    for r in range(2):
        chunk(0, r, True)
    with pool.Fori(1, CHUNKS // 2) as t:
        for r in range(2):
            chunk(t, r, False)
    for r in range(2):
        pool.wait_ge(S.s_out[r], 16 * CHUNK * (CHUNKS // 2))


def store_records(nc, act, S, parts, src, dst, out):
    rows = out.rearrange("(p j) w -> p j w", p=P)

    def chunk(t, r):
        c = t * 2 + r
        at = bass.ds(c * WIDE, WIDE)
        act.wait_ge(S.s_in[r], (t + 1) * (16 * len(parts)))
        act.sem_inc(S.s_begun, 1)
        nc.scalar.copy(S.stage[:, r, :, S.width - 2].bitcast(i32), src[:, at]).then_inc(S.s_staged, 1)
        nc.scalar.copy(S.stage[:, r, :, S.width - 1].bitcast(i32), dst[:, at]).then_inc(S.s_staged, 1)
        act.wait_ge(S.s_staged, c * 2 + 2)
        act.dma_start(rows[:, at, :], S.stage[:, r, :, :]).then_inc(S.s_stored[r], 16)

    def load(t, r, stored):
        act.wait_ge(S.s_stored[r], stored * 16)
        load_attributes(act, S, parts, t, r, WIDE)

    last = WIDES // 2 - 1
    for r in range(2):
        load_attributes(act, S, parts, 0, r, WIDE)
    chunk(0, 0)
    chunk(0, 1)
    load(1, 0, 1)
    with act.Fori(1, last) as t:
        chunk(t, 0)
        load(t, 1, t)
        chunk(t, 1)
        load(t + 1, 0, t + 1)
    chunk(last, 0)
    load(last, 1, last)
    chunk(last, 1)
    for r in range(2):
        act.wait_ge(S.s_stored[r], 16 * (WIDES // 2))


def gnn_kernel(nc, A, out, scratch):
    D0 = 160
    NS, NV = 64, 32
    VG = 4
    G0, G1 = A["groupings"]
    REC0, REC1 = 34, 22
    ROUNDS0, ROUNDS1 = G0.visits // ROUND, G1.visits // ROUND
    BATCH0, BATCHES0 = 16, G0.visits // 16
    GPB0 = BATCH0 // VG
    BATCH1, BATCHES1 = 8, G1.visits // 8
    GPB1 = BATCH1 // VG
    WIN = P
    rec0, rec1, f_tab, base_tab = scratch["rec0"], scratch["rec1"], scratch["f"], scratch["base"]

    outer = ExitStack()
    with outer:
        def sb_in(ctx, stage=""):
            return lambda n, s, d=fp32: ctx.enter_context(nc.sbuf_tensor(stage + n, s, d))

        def ps_in(ctx, stage=""):
            return lambda n, s, d=fp32: ctx.enter_context(nc.psum_tensor(stage + n, s, d))

        def sem_in(ctx, stage=""):
            return lambda n: ctx.enter_context(nc.semaphore(stage + n))

        sb = sb_in(outer)
        rounds_i = sb("rounds", [1, 2], i32)

        def rounds_of(engine, which):
            return engine.value_load(rounds_i[0:1, which:which + 1], min_val=(G0, G1)[which].buckets // ROUND, max_val=(ROUNDS0, ROUNDS1)[which])

        s_begun = sem_in(outer)("begun")
        ident = sb("ident", [P, P])
        ident16 = sb("ident16", [P, P], bf16)
        iota = sb("iota", [P, P])

        with ExitStack() as ctx:
            sb, sem = sb_in(ctx), sem_in(ctx)
            src = sb("src", [P, TILES], i32)
            dst = sb("dst", [P, TILES], i32)
            iota16 = sb("iota16", [P, LO], bf16)
            not_earlier32 = sb("not_earlier32", [P, Q * P])
            not_earlier = sb("not_earlier", [P, Q * P], bf16)
            own_group = sb("own_group", [P, 4, LO])
            sums = {n: sb(n, [P, P]) for n in ("all_groups", "groups_before", "digits_before")}
            visit_no = {g.name: sb("visit_" + g.name, [P, g.cols]) for g in (G0, G1)}
            tile_end = sb("tile_end", [P, G0.tile_cols])
            s_const, s_made = sem("s_const"), sem("s_made")
            C = {"iota": iota16, "ident16": ident16[:, :], "not_earlier": not_earlier[:, :], "own_group": own_group[:, :, :],
                 **{n: t[:, :] for n, t in sums.items()}, **{"visit_" + n: t for n, t in visit_no.items()}, "tile_end": tile_end}
            consts = [(ident, A["ident"]), (iota, A["iota"]), (not_earlier32, A["not_earlier"]), (own_group, A["own_group"].rearrange("p (g l) -> p g l", l=LO))]
            consts += [(sums[n], A[n]) for n in sums] + [(visit_no[n], A["visit_" + n]) for n in visit_no] + [(tile_end, A["tile_end"])]

            with nc.Block() as block:
                @block.sync
                def _(sp):
                    for tile, dram in consts:
                        sp.dma_start(tile[:], dram).then_inc(s_const, 16)

                @block.vector
                def _(dve):
                    dve.wait_ge(s_const, 16 * len(consts))
                    nc.vector.tensor_copy(ident16[:, :], ident[:, :])
                    nc.vector.tensor_copy(iota16[:, :], iota[:, 0:LO])
                    nc.vector.tensor_copy(not_earlier[:, :], not_earlier32[:, :]).then_inc(s_made, 1)

            out_of_order = sb("out_of_order", [1, 1], i32)
            s_src, s_dst, s_next, s_order = (sem(n) for n in ("s_src", "s_dst", "s_next", "s_order"))
            S1 = Scatter(ctx, nc, s_begun, "edges1", REC1, in_order=True)
            parts0 = [(A["edge_attr_32"], 0)]
            parts1 = [(A["edge_attr_16"], 0), (A["edge_attr_4"], 16)]

            def edges_out_of_order(engine):
                engine.wait_ge(s_order, 1)
                return engine.value_load(out_of_order[0:1, 0:1], min_val=0, max_val=SLOTS)

            S0 = Scatter(ctx, nc, s_begun, "edges0", REC0)
            ps = ps_in(ctx)
            banks = (ps("rank_t", [P, Q, P], bf16), ps("rank_eq", [P, 4, 4, P]), ps("rank_g", [P, GROUPS, LO]),
                     ps("rank_h", [P, Q, 4, LO]), ps("rank_s", [P, 3 * LO]))
            R0, R1 = alloc_rank(ctx, nc, G0, banks), alloc_rank(ctx, nc, G1, banks)
            next_dst = sb("next_dst", [P, TILES], i32)
            falls = sb("falls", [P, TILES])
            n_falls = sb("n_falls", [P, 1])
            one = sb("one", [P, 1])
            s_falls, s_falls_ps = sem("s_falls"), sem("s_falls_ps")
            with nc.Block() as block:
                @block.sync
                def _(sp):
                    sp.dma_start(dst[:, :], A["dst"]).then_inc(s_dst, 16)
                    sp.dma_start(next_dst[:, :], A["next_dst"]).then_inc(s_next, 16)
                    sp.dma_start(src[:, :], A["src"]).then_inc(s_src, 16)
                    load_all_attributes(sp, S0, parts0)
                    with sp.If(edges_out_of_order(sp) > 0):
                        load_all_attributes(sp, S1, parts1)

                @block.vector
                def _(dve):
                    nc.vector.memset(one[:, :], 1.0).then_inc(s_falls, 1)
                    dve.wait_ge(s_dst, 16)
                    dve.wait_ge(s_next, 16)
                    nc.vector.tensor_tensor(falls[:, :], dst[:, :], next_dst[:, :], ALU.is_gt).then_inc(s_falls, 1)
                    dve.wait_ge(s_falls, 2)
                    nc.vector.tensor_reduce(n_falls[:, :], falls[:, :], AX.X, ALU.add).then_inc(s_falls, 1)
                    dve.wait_ge(s_falls_ps, 1)
                    nc.vector.tensor_copy(out_of_order[:, :], R0.ps_s[0:1, 0:1]).then_inc(s_order, 1)
                    rank_vector(nc, dve, G0, R0, C, src, s_src, rounds_i[0:1, 0:1])
                    rank_vector(nc, dve, G1, R1, C, dst, s_dst, rounds_i[0:1, 1:2], edges_out_of_order)

                @block.tensor
                def _(pe):
                    pe.wait_ge(s_falls, 3)
                    nc.tensor.matmul(R0.ps_s[0:1, 0:1], n_falls[:, :], one[:, :], start=True, stop=True).then_inc(s_falls_ps, 1)
                    rank_tensor(nc, pe, G0, R0, C)
                    rank_tensor(nc, pe, G1, R1, C, edges_out_of_order)

                @block.scalar
                def _(act):
                    rank_scalar(nc, act, G0, R0, C, scratch["tables0"])
                    rank_scalar(nc, act, G1, R1, C, scratch["tables1"], edges_out_of_order)
                    with act.If(edges_out_of_order(act) < 1):
                        act.wait_ge(s_src, 16)
                        act.wait_ge(s_dst, 16)
                        store_records(nc, act, S1, parts1, src, dst, rec1)

                @block.gpsimd
                def _(pool):
                    pool.wait_ge(s_src, 16)
                    pool.wait_ge(s_dst, 16)
                    scatter_records(nc, pool, S0, 1, src, dst, R0, rec0)
                    with pool.If(edges_out_of_order(pool) > 0):
                        scatter_records(nc, pool, S1, 2, src, dst, R1, rec1)

        sb = sb_in(outer)
        vec = sb("node_attr", [P, NODE_TILES])
        eps = sb("eps", [P, 1])

        acc_ctx = ExitStack()
        acc_a = sb_in(acc_ctx)("acc_a", [P, NODE_ROWS])
        acc_b = sb_in(acc_ctx)("acc_b", [NV + 1, NODE_ROWS])

        with ExitStack() as ctx:
            sb, ps, sem = sb_in(ctx, "z_"), ps_in(ctx, "z_"), sem_in(ctx, "z_")
            RING = 2 * GPB0
            CX, CS, CY, CZ = 0, NV, NV + NS, P
            w_es = sb("w_es", [P, 8, P])
            w_ex = sb("w_ex", [P, 8, NV + NS])
            w_ey = sb("w_ey", [P, 8, NS + NV])
            w_ez = sb("w_ez", [P, 4, NV])
            w_nz = sb("w_nz", [P, 4, P])
            factor = sb("factor", [P, 4])
            vis_start = sb("vis_start", [1, P * G0.cols], i32)
            first_node = sb("first_node", [P, G0.visits])
            win_i = sb("win_i", [1, BATCHES0], i32)
            spread = sb("spread", [P, BATCH0])
            picked = sb("picked", [P, BATCHES0, BATCH0])
            in_bucket = sb("in_bucket", [P, 1])
            rel2 = sb("rel2", [P, BATCHES0])
            rec = sb("rec", [P, RING, VG, REC0])
            xg = sb("xg", [P, RING, VG, D0])
            rel = sb("rel", [P, 2, VG])
            onehot = sb("onehot", [P, 2, BATCH0, 8])
            outer_p = sb("outer_p", [P, 2, VG, 8, 32])
            za = sb("za", [P, 2, 24, P])
            zb = sb("zb", [P, 2, 2, 4, P])
            o_sb = sb("o_sb", [P, 2 * P])
            onehot2 = sb("onehot2", [P, WIN])
            ones = sb("ones", [P, 1])
            begun = sb("begun", [1, 8])
            ps_a = ps("ps_a", [P, 2, VG, 8 * 32])
            ps_b = ps("ps_b", [P, 2, 512])
            ps_o = ps("ps_o", [P, 512])
            ps_w = ps("ps_w", [P, 4, WIN])
            s_zero, s_w, s_prep, s_dve = (sem(n) for n in ("zero", "w", "prep", "dve"))
            s_rec = [sem(f"rec{r}") for r in range(RING // 2)]
            s_xg = [sem(f"xg{r}") for r in range(RING // 2)]
            HALF = 2 * VG * 16
            s_outer = sem("outer")
            s_z = sem("z")
            s_za, s_zb = sem("za"), sem("zb")
            s_o_ps, s_o = sem("o_ps"), sem("o")
            s_oh2 = sem("oh2")
            s_win = sem("win")
            s_acc = sem("acc")
            s_tab = sem("tab")
            tab = scratch["tables0"]
            FREE = {"z": RING, "za": 2, "zb": 2, "o_ps": 2, "o": 1, "win": 1, "acc": 2}

            def load_records(engine, visits, t, i):
                n = t * RING + i
                engine.wait_ge(s_z, n + 1)
                engine.sem_inc(s_begun, 1)
                for v in visits:
                    row = engine.value_load(vis_start[0:1, bass.ds(n * VG + v, 1)], min_val=0, max_val=G0.tiles * P)
                    engine.dma_start(rec[:, i, v, :], rec0[bass.ds(row, P), :]).then_inc(s_rec[i // 2], 16)

            with nc.Block() as block:
                @block.sync
                def _(sp):
                    rounds = rounds_of(sp, 0)
                    sp.dma_start(vis_start[:, :], tab["start"].rearrange("(o v) -> o v", o=1)).then_inc(s_tab, 16)
                    sp.dma_start(first_node[:, :], tab["bucket"][0:G0.visits].rearrange("(o v) -> o v", o=1).broadcast_to([P, G0.visits])).then_inc(s_tab, 16)
                    sp.dma_start(spread[:, :], A["spread0"]).then_inc(s_tab, 16)
                    sp.dma_start(in_bucket[:, :], A["in_bucket0"]).then_inc(s_tab, 16)
                    sp.wait_ge(s_tab, 64)
                    for i in range(RING // 2):
                        load_records(sp, range(0, VG - 1), 0, i)
                    sp.wait_ge(s_zero, 5)
                    W1, W2, W3, W4 = (A[n] for n in ("W1", "W2", "W3", "W4"))
                    XS, XX, XY = slice(0, 64), slice(64, 96), slice(96, 128)
                    pieces = [(w_es[XS, :, CS:CS + NS], W1), (w_es[XX, :, CX:CX + NV], W4), (w_es[XY, :, CY:CY + NV], W4),
                              (w_ex[XS, :, CX:CX + NV], W3), (w_ex[XX, :, CS:CS + NS], W2),
                              (w_ey[XS, :, CY - CS:CY - CS + NV], W3), (w_ey[XY, :, 0:NS], W2)]
                    for half in range(2):
                        four = slice(4 * half, 4 * half + 4)
                        pieces += [(w_nz[32 * half:32 * half + 32, :, 0:NS], W2[:, four, :]),
                                   (w_nz[64 + 32 * half:96 + 32 * half, :, CZ - CS:CZ - CS + NV], W4[:, four, :]),
                                   (w_ez[64 * half:64 * half + 64, :, :], W3[:, four, :])]
                    for tile, dram in pieces:
                        sp.dma_start(tile, dram).then_inc(s_w, 16)
                    sp.dma_start(factor[:, :], A["factor0"]).then_inc(s_w, 16)
                    for i in range(RING // 2, RING):
                        load_records(sp, range(0, VG - 1), 0, i)

                    with sp.Fori(1, ROUNDS0) as t:
                        with sp.If(t < rounds):
                            for i in range(RING):
                                load_records(sp, range(0, VG - 1), t, i)

                @block.gpsimd
                def _(pool):
                    rounds = rounds_of(pool, 0)
                    for tile in (w_es, w_ex, w_ey, w_ez, w_nz):
                        nc.gpsimd.memset(tile[:], 0.0).then_inc(s_zero, 1)

                    def group(t, i):
                        n = t * RING + i
                        pool.wait_ge(s_z, n + 1)
                        pool.wait_ge(s_rec[i // 2], (t + 1) * HALF)
                        pool.sem_inc(s_begun, 1)
                        for v in range(VG):
                            nc.gpsimd.indirect_dma_start(out=xg[:, i, v, :], out_offset=None, in_=A["x"],
                                                         in_offset=bass.IndirectOffsetOnAxis(ap=rec[:, i, v, REC0 - 1:REC0].bitcast(i32), axis=0)).then_inc(s_xg[i // 2], 16)

                    with pool.Fori(0, ROUNDS0) as t:
                        with pool.If(t < rounds):
                            for i in range(RING):
                                group(t, i)

                @block.vector
                def _(dve):
                    rounds = rounds_of(dve, 0)
                    done = [0]

                    def link(ins):
                        done[0] += 1
                        ins.then_inc(s_dve, 1)
                        dve.wait_ge(s_dve, done[0])

                    for c, (s, n) in enumerate(((s_z, "z"), (s_za, "za"), (s_zb, "zb"), (s_o_ps, "o_ps"), (s_o, "o"), (s_win, "win"))):
                        nc.vector.memset(begun[:, c:c + 1], 1.0).then_inc(s, FREE[n])
                    link(nc.vector.memset(ones[:, :], 1.0))
                    nc.vector.memset(o_sb[:, :], 0.0).then_inc(s_prep, 1)
                    dve.wait_ge(s_tab, 64)
                    link(nc.vector.tensor_scalar(first_node[:, :], first_node[:, :], float(G0.width), None, ALU.mult))
                    link(nc.vector.tensor_copy(win_i[:, :], first_node[0:1, ::BATCH0]))
                    link(nc.vector.tensor_tensor(picked[:, :, :], first_node[:, :].rearrange("p (k v) -> p k v", v=BATCH0),
                                                 spread[:, :].unsqueeze(1).broadcast_to([P, BATCHES0, BATCH0]), ALU.mult))
                    link(nc.vector.tensor_reduce(rel2[:, :], picked[:, :, :], AX.X, ALU.add))
                    link(nc.vector.tensor_scalar(rel2[:, :], rel2[:, :], in_bucket[:, 0:1], None, ALU.add))
                    first = done[0]

                    def products(t, h, g):
                        i, k = h * GPB0 + g, t * 2 + h
                        n = t * RING + i
                        if g == 0:
                            dve.wait_ge(s_o_ps, k + 1)
                        dve.wait_ge(s_rec[i // 2], (t + 1) * HALF)
                        nc.vector.tensor_tensor(rel[:, g % 2, :], rec[:, i, :, REC0 - 2].bitcast(i32), first_node[:, bass.ds(n * VG, VG)], ALU.subtract).then_inc(s_dve, 1)
                        dve.wait_ge(s_dve, n * 2 + first + 1)
                        oh = onehot[:, h, g * VG:(g + 1) * VG, :]
                        nc.vector.tensor_tensor(oh, iota[:, 0:8].unsqueeze(1).broadcast_to([P, VG, 8]),
                                                rel[:, g % 2, :].unsqueeze(2).broadcast_to([P, VG, 8]), ALU.is_equal).then_inc(s_dve, 1)
                        dve.wait_ge(s_dve, n * 2 + first + 2)
                        dve.wait_ge(s_z, n + (RING - 1))
                        nc.vector.tensor_tensor(outer_p[:, g % 2, :, :, :], oh.unsqueeze(3).broadcast_to([P, VG, 8, 32]),
                                                rec[:, i, :, 0:32].unsqueeze(2).broadcast_to([P, VG, 8, 32]), ALU.mult).then_inc(s_outer, 1)

                    def add_window(k):
                        node = dve.value_load(win_i[0:1, bass.ds(k, 1)], min_val=0, max_val=NODE_ROWS - WIN)
                        dve.wait_ge(s_acc, k * 2 + 2)
                        dve.wait_ge(s_win, k + 2)
                        at = bass.ds(node, WIN)
                        nc.vector.tensor_tensor(acc_a[:, at], acc_a[:, at], ps_w[:, 0, :], ALU.add).then_inc(s_acc, 1)
                        nc.vector.tensor_tensor(acc_b[:, at], acc_b[:, at], ps_w[0:NV + 1, 1, :], ALU.add).then_inc(s_acc, 1)

                    def second_onehot(k):
                        dve.wait_ge(s_win, k + 1)
                        nc.vector.tensor_scalar(onehot2[:, :], iota[:, :], rel2[:, bass.ds(k, 1)], None, ALU.is_equal).then_inc(s_oh2, 1)

                    def batch(t, h, first=False):
                        k = t * 2 + h
                        products(t, h, 0)
                        products(t, h, 1)
                        if not first:
                            add_window(k - 2)
                            second_onehot(k - 1)
                        products(t, h, 2)
                        products(t, h, 3)

                    batch(0, 0, True)
                    dve.wait_ge(s_w, 16 * 14)
                    for tile, col in ((w_es, 0), (w_ex, 1), (w_ey, 1), (w_ez, 2), (w_nz, 3)):
                        nc.vector.tensor_scalar(tile[:], tile[:], factor[:, col:col + 1], None, ALU.mult).then_inc(s_prep, 1)
                    products(0, 1, 0)
                    nc.vector.memset(acc_a[:, :], 0.0).then_inc(s_acc, 1)
                    products(0, 1, 1)
                    nc.vector.memset(acc_b[:, :], 0.0).then_inc(s_acc, 1)
                    second_onehot(0)
                    products(0, 1, 2)
                    products(0, 1, 3)
                    with dve.Fori(1, ROUNDS0) as t:
                        with dve.If(t < rounds):
                            for h in range(2):
                                batch(t, h)
                        with dve.If(t == rounds - 1):
                            add_window(t * 2)
                            second_onehot(t * 2 + 1)
                            add_window(t * 2 + 1)

                @block.scalar
                def _(act):
                    rounds = rounds_of(act, 0)
                    def evacuate(t, h, g):
                        i, k = h * GPB0 + g, t * 2 + h
                        n = t * RING + i
                        if g == 0:
                            act.wait_ge(s_o_ps, k + 1)
                        act.wait_ge(s_z, n + (RING + 1))
                        rows = slice(g * VG * 8, (g + 1) * VG * 8)
                        nc.scalar.copy(za[:, h, :, rows].rearrange("p b (v m) -> p b v m", v=VG), ps_a[:, g % 2, :, 0:8 * 24].rearrange("p v (m b) -> p b v m", b=24)).then_inc(s_za, 1)
                        nc.scalar.copy(zb[:, h, :, :, rows], ps_b[:, g % 2, 0:2 * P].rearrange("p (s r b) -> p s b r", s=2, b=4)).then_inc(s_zb, 1)

                    def copy_out(k):
                        act.wait_ge(s_win, k + 1)
                        act.wait_ge(s_o_ps, k + 3)
                        nc.scalar.copy(o_sb[:, 0:D0 + 1], ps_o[:, 0:D0 + 1]).then_inc(s_o, 1)

                    def batch(t, h, lag1=True, last=False):
                        for g in range(GPB0):
                            evacuate(t, h, g)
                            if not last:
                                load_records(act, range(VG - 1, VG), t + 1, h * GPB0 + g)
                            if g == 1 and lag1:
                                copy_out(t * 2 + h - 1)

                    act.wait_ge(s_tab, 64)
                    for i in range(RING):
                        load_records(act, range(VG - 1, VG), 0, i)
                    batch(0, 0, False)
                    batch(0, 1)
                    with act.Fori(1, ROUNDS0 - 1) as t:
                        with act.If(t < rounds - 1):
                            for h in range(2):
                                batch(t, h)
                        with act.If(t == rounds - 2):
                            for h in range(2):
                                batch(t + 1, h, last=True)
                            copy_out(t * 2 + 3)

                @block.tensor
                def _(pe):
                    rounds = rounds_of(pe, 0)

                    def sums(t, h, g):
                        i = h * GPB0 + g
                        n = t * RING + i
                        pe.wait_ge(s_za, n + 1)
                        pe.wait_ge(s_zb, n + 1)
                        pe.wait_ge(s_xg[i // 2], (t + 1) * HALF)
                        pe.wait_ge(s_outer, n + 1)
                        op = outer_p[:, g % 2, :, :, :]
                        for v in range(VG):
                            nc.tensor.matmul(ps_a[:, g % 2, v, 0:8 * 24], xg[:, i, v, 0:P], op[:, v, :, 8:32], start=(v % 2 == 0), stop=(v % 2 == 1))
                        for v in range(VG):
                            for quarter in range(4):
                                nc.tensor.matmul(ps_b[32 * quarter:32 * quarter + 32, g % 2, 32 * v:32 * v + 32], xg[:, i, v, P:D0],
                                                 op[:, v, :, 4 * quarter:4 * quarter + 4], start=(v == 0), stop=False, tile_position=(0, 32 * quarter))
                        for v in range(VG):
                            for half in range(2):
                                last = nc.tensor.matmul(ps_b[64 * half:64 * half + 64, g % 2, P + 32 * v:P + 32 * v + 32], xg[:, i, v, 0:NS],
                                                        op[:, v, :, 4 * half:4 * half + 4], start=False, stop=(v == VG - 1), tile_position=(0, 64 * half))
                        last.then_inc(s_z, 1)

                    def contract(k, h):
                        pe.wait_ge(s_za, k * GPB0 + (GPB0 + FREE["za"]))
                        pe.wait_ge(s_zb, k * GPB0 + (GPB0 + FREE["zb"]))
                        pe.wait_ge(s_o, k + 1)
                        for b in range(8):
                            nc.tensor.matmul(ps_o[:, CX:CX + P], za[:, h, b, :], w_es[:, b, :], start=(b == 0), stop=False)
                            nc.tensor.matmul(ps_o[:, CX:CX + NV + NS], za[:, h, 8 + b, :], w_ex[:, b, :], start=False, stop=False)
                            nc.tensor.matmul(ps_o[:, CS:CS + NS + NV], za[:, h, 16 + b, :], w_ey[:, b, :], start=False, stop=False)
                        for j in range(4):
                            nc.tensor.matmul(ps_o[:, CZ:CZ + NV], zb[:, h, 1, j, :], w_ez[:, j, :], start=False, stop=False)
                        for j in range(4):
                            nc.tensor.matmul(ps_o[:, CS:CS + P], zb[:, h, 0, j, :], w_nz[:, j, :], start=False, stop=False)
                        nc.tensor.matmul(ps_o[:, D0:D0 + 1], onehot[:, h, :, :].rearrange("p v m -> p (v m)"), ones[:, :], start=False, stop=True).then_inc(s_o_ps, 1)

                    def window(k):
                        pe.wait_ge(s_o, k + 2)
                        pe.wait_ge(s_oh2, k + 1)
                        pe.wait_ge(s_acc, k * 2 + 2)
                        nc.tensor.matmul(ps_w[:, 0, :], o_sb[:, 0:P], onehot2[:, :], start=True, stop=False)
                        nc.tensor.matmul(ps_w[:, 1, :], o_sb[:, P:], onehot2[:, :], start=False, stop=True).then_inc(s_win, 1)

                    def batch(t, h, lag1=True):
                        k = t * 2 + h
                        sums(t, h, 0)
                        sums(t, h, 1)
                        if lag1:
                            contract(k - 1, 1 - h)
                        sums(t, h, 2)
                        sums(t, h, 3)
                        if lag1:
                            window(k - 1)

                    batch(0, 0, False)
                    pe.wait_ge(s_prep, 6)
                    batch(0, 1)
                    with pe.Fori(1, ROUNDS0) as t:
                        with pe.If(t < rounds):
                            for h in range(2):
                                batch(t, h)
                        with pe.If(t == rounds - 1):
                            contract(t * 2 + 1, 1)
                            window(t * 2 + 1)

        with ExitStack() as ctx:
            sb, ps, sem = sb_in(ctx, "n_"), ps_in(ctx, "n_"), sem_in(ctx, "n_")
            wm_ta = sb("wm_ta", [P, D0 + 1])
            wm_tb = sb("wm_tb", [NV, D0 + 1])
            wu1_a = sb("wu1_a", [P, D0])
            wu1_b = sb("wu1_b", [NV, D0])
            wu0_a = sb("wu0_a", [P, D0])
            wu0_b = sb("wu0_b", [NV, D0])
            wc_a = sb("wc_a", [P, D0])
            wc_b = sb("wc_b", [NV + 1, D0])
            bu = sb("bu", [P, D0])
            wn_a = sb("wn_a", [P, 2 * D0])
            wn_b = sb("wn_b", [P, 2 * D0])
            factor1 = sb("factor1", [P, 2])
            x = sb("x", [P, 2, D0])
            xt_a = sb("xt_a", [P, 2, P])
            xt_b = sb("xt_b", [NV, 2, P])
            sum_a = sb("sum_a", [P, 2, P])
            sum_b = sb("sum_b", [NV + 1, 2, P])
            y = sb("y", [P, 2, D0])
            stats = sb("stats", [P, 2, 6])
            mean_var = sb("mean_var", [P, 2, 2])
            std = sb("std", [P, 2, 1])
            rstd = sb("rstd", [P, 2, 1])
            x1 = sb("x1", [P, 2, D0])
            x1t = sb("x1t", [P, 2, 2, P])
            f_out = sb("f_out", [P, 2, D0])
            base_out = sb("base_out", [P, 2, D0])
            ps_u = [ps(f"ps_u{r}", [P, 512]) for r in range(2)]
            ps_t = [ps(f"ps_t{r}", [P, 512]) for r in range(2)]
            ps_f = [ps(f"ps_f{r}", [P, 512]) for r in range(2)]
            ps_s = [ps(f"ps_s{r}", [P, 512]) for r in range(2)]
            WEIGHTS = 16 * 17
            s_zero, s_scaled, s_wc_ps, s_wc = (sem(n) for n in ("zero", "scaled", "wc_ps", "wc"))
            s_x = [sem(f"in{r}") for r in range(2)]
            s_sum = sem("sum")
            s_u = sem("u")
            s_y = sem("y")
            s_yb, s_bn, s_var, s_std, s_rstd, s_x1 = (sem(n) for n in ("yb", "bn", "var", "std", "rstd", "x1"))
            s_t, s_x1t = sem("t"), sem("x1t")
            s_f, s_fo, s_bo = sem("f"), sem("fo"), sem("bo")
            s_st = [sem(f"st{r}") for r in range(2)]
            s_w = sem("w")

            with nc.Block() as block:
                @block.sync
                def _(sp):
                    sp.wait_ge(s_zero, 2)
                    WU, WMT = A["Wu"], A["WmT"]
                    pieces = [(wm_ta[:, :], WMT[0:P, :]), (wm_tb[:, :], WMT[P:D0, :]), (wu0_a[:, :], WU[0:P, :]), (wu0_b[:, :], WU[P:D0, :]),
                              (wu1_a[:, :], WU[D0:D0 + P, :]), (wu1_b[:, :], WU[D0 + P:2 * D0, :]),
                              (bu[:, :], A["bu"].rearrange("(o d) -> o d", o=1).broadcast_to([P, D0])),
                              (factor1[:, :], A["factor1"]), (vec[:, :], A["node_vec1"])]
                    for c, (scal, vect) in enumerate((("Wl1_0", "Wl1_1"), ("Wsc0", "Wsc1"))):
                        pieces += [(wn_a[0:64, c * D0:c * D0 + 64], A[scal]), (wn_a[64:96, c * D0 + 64:c * D0 + 96], A[vect]),
                                   (wn_a[96:128, c * D0 + 96:c * D0 + 128], A[vect]), (wn_b[96:128, c * D0 + 128:c * D0 + 160], A[vect])]
                    for tile, dram in pieces:
                        sp.dma_start(tile, dram).then_inc(s_w, 16)

                    def load(i, r):
                        at = bass.ds(i * P, P)
                        sp.dma_start(x[:, r, :], A["x"][at, :]).then_inc(s_x[r], 16)
                        sp.dma_start(xt_a[:, r, :], A["xT"][0:P, at]).then_inc(s_x[r], 16)
                        sp.dma_start(xt_b[:, r, :], A["xT"][P:D0, at]).then_inc(s_x[r], 16)

                    def store(t, r):
                        i = t * 2 + r
                        at = bass.ds(i * P, P)
                        sp.wait_ge(s_fo, i + 1)
                        sp.dma_start(f_tab[at, :], f_out[:, r, :]).then_inc(s_st[r], 16)
                        sp.wait_ge(s_bo, i + 1)
                        sp.dma_start(base_tab[at, :], base_out[:, r, :]).then_inc(s_st[r], 16)

                    for r in range(2):
                        load(r, r)
                    for r in range(2):
                        sp.wait_ge(s_y, 1 + r)
                        load(2 + r, r)
                    with sp.Fori(2, NODE_TILES // 2) as t:
                        for r in range(2):
                            sp.wait_ge(s_y, t * 2 + r - 1)
                            sp.wait_ge(s_u, t * 2 + r - 1)
                            load(t * 2 + r, r)
                            store(t - 2, r)
                    for t in (NODE_TILES // 2 - 2, NODE_TILES // 2 - 1):
                        for r in range(2):
                            store(t, r)
                    for r in range(2):
                        sp.wait_ge(s_st[r], 16 * NODE_TILES)

                @block.gpsimd
                def _(pool):
                    nc.gpsimd.memset(wn_a[:, :], 0.0).then_inc(s_zero, 1)
                    nc.gpsimd.memset(wn_b[:, :], 0.0).then_inc(s_zero, 1)

                    def pick(i, r):
                        at = bass.ds(i * P, P)
                        nc.gpsimd.tensor_copy(sum_a[:, r, :], acc_a[:, at]).then_inc(s_sum, 1)
                        nc.gpsimd.tensor_copy(sum_b[:, r, :], acc_b[:, at]).then_inc(s_sum, 1)

                    for r in range(2):
                        pick(r, r)
                    with pool.Fori(1, NODE_TILES // 2) as t:
                        for r in range(2):
                            pool.wait_ge(s_u, t * 2 + r - 1)
                            pick(t * 2 + r, r)

                @block.vector
                def _(dve):
                    nc.vector.memset(eps[:, :], 1e-5)
                    dve.wait_ge(s_w, WEIGHTS)
                    nc.vector.tensor_scalar(wn_a[:, :], wn_a[:, :], factor1[:, 0:1], None, ALU.mult).then_inc(s_scaled, 1)
                    nc.vector.tensor_scalar(wn_b[:, :], wn_b[:, :], factor1[:, 1:2], None, ALU.mult).then_inc(s_scaled, 1)
                    dve.wait_ge(s_wc_ps, 1)
                    nc.vector.tensor_copy(wc_a[:, :], ps_u[0][:, 0:D0]).then_inc(s_wc, 1)
                    nc.vector.tensor_copy(wc_b[:, :], ps_u[1][0:NV + 1, 0:D0]).then_inc(s_wc, 1)

                    def update(t, r):
                        i = t * 2 + r
                        dve.wait_ge(s_x[r], (t + 1) * 48)
                        dve.wait_ge(s_u, i + 1)
                        nc.vector.scalar_tensor_tensor(y[:, r, :], x[:, r, :], 2.0, ps_u[r][:, 0:D0], ALU.mult, ALU.add).then_inc(s_y, 1)
                        dve.wait_ge(s_y, i + 1)
                        nc.vector.tensor_tensor(y[:, r, :], y[:, r, :], bu[:, :], ALU.add).then_inc(s_yb, 1)
                        dve.wait_ge(s_yb, i + 1)
                        nc.vector.bn_stats(stats[:, r, :], y[:, r, :]).then_inc(s_bn, 1)
                        dve.wait_ge(s_w, WEIGHTS)
                        dve.wait_ge(s_bn, i + 1)
                        nc.vector.bn_aggr(mean_var[:, r, :], stats[:, r, :]).then_inc(s_var, 1)

                    def normalise(j, r):
                        dve.wait_ge(s_std, j + 1)
                        nc.vector.reciprocal(rstd[:, r, :], std[:, r, :]).then_inc(s_rstd, 1)
                        dve.wait_ge(s_rstd, j + 1)
                        nc.vector.tensor_scalar(x1[:, r, :], y[:, r, :], mean_var[:, r, 0:1], rstd[:, r, :], ALU.subtract, ALU.mult).then_inc(s_x1, 1)

                    def residual(t, r, first):
                        j = t * 2 + r
                        dve.wait_ge(s_f, j + 1)
                        if not first:
                            dve.wait_ge(s_st[r], t * 32)
                        nc.vector.scalar_tensor_tensor(base_out[:, r, :], ps_s[r][:, 0:D0], vec[:, bass.ds(j, 1)], x1[:, r, :], ALU.mult, ALU.add).then_inc(s_bo, 1)

                    update(0, 0)
                    normalise(0, 0)
                    update(0, 1)
                    normalise(1, 1)
                    update(1, 0)
                    residual(0, 0, True)
                    normalise(2, 0)
                    update(1, 1)
                    residual(0, 1, True)
                    with dve.Fori(2, NODE_TILES // 2) as t:
                        normalise(t * 2 - 1, 1)
                        update(t, 0)
                        residual(t - 1, 0, False)
                        normalise(t * 2, 0)
                        update(t, 1)
                        residual(t - 1, 1, False)
                    normalise(NODE_TILES - 1, 1)
                    residual(NODE_TILES // 2 - 1, 0, False)
                    residual(NODE_TILES // 2 - 1, 1, False)

                @block.scalar
                def _(act):
                    def deviation(i, r):
                        act.wait_ge(s_var, i + 1)
                        nc.scalar.activation(std[:, r, :], mean_var[:, r, 1:2], ACT.Sqrt, bias=eps[:, :]).then_inc(s_std, 1)

                    def transposed(j, r):
                        act.wait_ge(s_t, j + 1)
                        nc.scalar.copy(x1t[:, r, :, :], ps_t[r][:, 0:2 * P].rearrange("p (a n) -> p a n", a=2)).then_inc(s_x1t, 1)

                    def products(t, r, first):
                        j = t * 2 + r
                        if not first:
                            act.wait_ge(s_st[r], t * 32)
                        act.wait_ge(s_f, j + 1)
                        nc.scalar.activation(f_out[:, r, :], ps_f[r][:, 0:D0], ACT.Copy, scale=vec[:, bass.ds(j, 1)]).then_inc(s_fo, 1)

                    deviation(0, 0)
                    deviation(1, 1)
                    transposed(0, 0)
                    deviation(2, 0)
                    transposed(1, 1)
                    products(0, 0, True)
                    deviation(3, 1)
                    transposed(2, 0)
                    products(0, 1, True)
                    with act.Fori(2, NODE_TILES // 2) as t:
                        deviation(t * 2, 0)
                        transposed(t * 2 - 1, 1)
                        products(t - 1, 0, False)
                        deviation(t * 2 + 1, 1)
                        transposed(t * 2, 0)
                        products(t - 1, 1, False)
                    transposed(NODE_TILES - 1, 1)
                    products(NODE_TILES // 2 - 1, 0, False)
                    products(NODE_TILES // 2 - 1, 1, False)

                @block.tensor
                def _(pe):
                    pe.wait_ge(s_w, WEIGHTS)
                    nc.tensor.matmul(ps_u[0][:, 0:D0], wm_ta[:, 0:P], wu1_a[:, :], start=True, stop=False)
                    nc.tensor.matmul(ps_u[0][:, 0:D0], wm_tb[:, 0:P], wu1_b[:, :], start=False, stop=True)
                    nc.tensor.matmul(ps_u[1][0:NV + 1, 0:D0], wm_ta[:, P:D0 + 1], wu1_a[:, :], start=True, stop=False)
                    nc.tensor.matmul(ps_u[1][0:NV + 1, 0:D0], wm_tb[:, P:D0 + 1], wu1_b[:, :], start=False, stop=True).then_inc(s_wc_ps, 1)
                    pe.wait_ge(s_wc, 2)
                    pe.wait_ge(s_scaled, 2)

                    def update(t, r, first):
                        i = t * 2 + r
                        if not first:
                            pe.wait_ge(s_y, i - 1)
                        pe.wait_ge(s_x[r], (t + 1) * 48)
                        pe.wait_ge(s_sum, i * 2 + 2)
                        nc.tensor.matmul(ps_u[r][:, 0:D0], xt_a[:, r, :], wu0_a[:, :], start=True, stop=False)
                        nc.tensor.matmul(ps_u[r][:, 0:D0], xt_b[:, r, :], wu0_b[:, :], start=False, stop=False)
                        nc.tensor.matmul(ps_u[r][:, 0:D0], sum_a[:, r, :], wc_a[:, :], start=False, stop=False)
                        nc.tensor.matmul(ps_u[r][:, 0:D0], sum_b[:, r, :], wc_b[:, :], start=False, stop=True).then_inc(s_u, 1)

                    def transposes(j, r, first):
                        if not first:
                            pe.wait_ge(s_x1t, j - 1)
                        pe.wait_ge(s_x1, j + 1)
                        nc.tensor.transpose(ps_t[r][:, 0:P], x1[:, r, 0:P], ident[:, :])
                        nc.tensor.transpose(ps_t[r][:, P:2 * P], x1[:, r, NV:D0], ident[:, :]).then_inc(s_t, 1)

                    def products(j, r, first):
                        if not first:
                            pe.wait_ge(s_fo, j - 1)
                            pe.wait_ge(s_bo, j - 1)
                        pe.wait_ge(s_x1t, j + 1)
                        for bank, c in ((ps_f[r], 0), (ps_s[r], D0)):
                            nc.tensor.matmul(bank[:, 0:D0], x1t[:, r, 0, :], wn_a[:, c:c + D0], start=True, stop=False)
                            last = nc.tensor.matmul(bank[:, 0:D0], x1t[:, r, 1, :], wn_b[:, c:c + D0], start=False, stop=True)
                        last.then_inc(s_f, 1)

                    update(0, 0, True)
                    update(0, 1, True)
                    transposes(0, 0, True)
                    update(1, 0, False)
                    transposes(1, 1, True)
                    products(0, 0, True)
                    update(1, 1, False)
                    transposes(2, 0, False)
                    products(1, 1, True)
                    with pe.Fori(2, NODE_TILES // 2) as t:
                        update(t, 0, False)
                        transposes(t * 2 - 1, 1, False)
                        products(t * 2 - 2, 0, False)
                        update(t, 1, False)
                        transposes(t * 2, 0, False)
                        products(t * 2 - 1, 1, False)
                    transposes(NODE_TILES - 1, 1, False)
                    products(NODE_TILES - 2, 0, False)
                    products(NODE_TILES - 1, 1, False)
        acc_ctx.close()

        W1_ = D0 + 1
        sums_tab = scratch["sums"]
        with ExitStack() as ctx:
            sb, ps, sem = sb_in(ctx, "e_"), ps_in(ctx, "e_"), sem_in(ctx, "e_")
            AHEAD = 4
            RING = AHEAD * GPB1
            PAIRS = BATCH1 // 2
            wfc1 = sb("wfc1", [P, PAIRS, P])
            wfc2 = sb("wfc2", [P, 2, 192])
            vis_start = sb("vis_start", [1, P * G1.cols], i32)
            first_node = sb("first_node", [P, G1.visits])
            same = sb("same", [P, G1.visits])
            rec = sb("rec", [P, AHEAD, BATCH1, REC1])
            fg = sb("fg", [P, RING, VG, D0])
            rel = sb("rel", [P, 2, BATCH1])
            onehot = sb("onehot", [P, AHEAD, BATCH1, 4, 32], bf16)
            onehot_sh = sb("onehot_sh", [P, AHEAD, BATCH1, 4, 32])
            scal = sb("scal", [P, BATCH1, 16])
            scal_t = sb("scal_t", [P, P])
            hidden = sb("hidden", [P, 2, PAIRS, P])
            prod = sb("prod", [P, 2, BATCH1, 2, D0])
            run = sb("run", [P, 2, BATCH1, W1_])
            ones = sb("ones", [P, 1], bf16)
            ps_t = ps("ps_t", [P, 512])
            ps_h = ps("ps_h", [P, PAIRS, P])
            ps_w = ps("ps_w", [P, GPB1, 2, 2, 256])
            ps_m = ps("ps_m", [P, 2, 512])
            s_zero, s_w, s_prep, s_dve = (sem(n) for n in ("zero", "w", "prep", "dve"))
            s_rec = [sem(f"rec{i}") for i in range(AHEAD)]
            s_fg = [sem(f"fg{i}") for i in range(AHEAD)]
            LOADED = 16 * BATCH1
            s_oh = sem("oh")
            s_scal, s_t, s_scal_t, s_h, s_hid = (sem(n) for n in ("scal", "t", "scal_t", "h", "hid"))
            s_wt = sem("wt")
            s_msg = sem("msg")
            s_m = sem("m")
            s_run = sem("run")
            s_st = [sem(f"st{r}") for r in range(2)]
            s_tab = sem("tab")
            tab = scratch["tables1"]
            STORED = 16 * GPB1

            SP_VISITS, ACT_VISITS = range(0, 6), range(6, BATCH1)

            def load_records(engine, visits, t, h, first):
                k = t * AHEAD + h
                if not first:
                    engine.wait_ge(s_msg, (k - AHEAD + 1) * GPB1)
                    engine.wait_ge(s_oh, k - AHEAD + 1)
                    engine.wait_ge(s_scal, k - AHEAD + 1)
                    engine.sem_inc(s_begun, 1)
                for v in visits:
                    row = engine.value_load(vis_start[0:1, bass.ds(k * BATCH1 + v, 1)], min_val=0, max_val=N_EDGES)
                    engine.dma_start(rec[:, h, v, :], rec1[bass.ds(row, P), :]).then_inc(s_rec[h], 16)

            with nc.Block() as block:
                @block.sync
                def _(sp):
                    rounds = rounds_of(sp, 1)
                    sp.wait_ge(s_zero, 2)
                    for v in range(BATCH1):
                        sp.dma_start(wfc1[16 * v:16 * v + 16, v // 2, (v % 2) * 64:(v % 2) * 64 + 64], A["Wfc1"]).then_inc(s_w, 16)
                    for v in range(2):
                        sp.dma_start(wfc2[64 * v:64 * v + 64, v, :], A["Wfc2"]).then_inc(s_w, 16)
                    sp.dma_start(vis_start[:, :], tab["start"].rearrange("(o v) -> o v", o=1)).then_inc(s_tab, 16)
                    sp.dma_start(first_node[:, :], tab["bucket"][0:G1.visits].rearrange("(o v) -> o v", o=1).broadcast_to([P, G1.visits])).then_inc(s_tab, 16)
                    sp.wait_ge(s_tab, 32)

                    for h in range(AHEAD):
                        load_records(sp, SP_VISITS, 0, h, True)
                    with sp.Fori(1, ROUNDS1) as t:
                        with sp.If(t < rounds):
                            for h in range(AHEAD):
                                load_records(sp, SP_VISITS, t, h, False)

                @block.gpsimd
                def _(pool):
                    rounds = rounds_of(pool, 1)
                    nc.gpsimd.memset(wfc1[:, :, :], 0.0).then_inc(s_zero, 1)
                    nc.gpsimd.memset(wfc2[:, :, :], 0.0).then_inc(s_zero, 1)

                    def group(t, i, first):
                        n = t * RING + i
                        if not first:
                            pool.wait_ge(s_msg, n - RING + 1)
                        pool.wait_ge(s_rec[i // GPB1], (t + 1) * LOADED)
                        pool.sem_inc(s_begun, 1)
                        for v in range(VG):
                            nc.gpsimd.indirect_dma_start(out=fg[:, i, v, :], out_offset=None, in_=f_tab,
                                                         in_offset=bass.IndirectOffsetOnAxis(ap=rec[:, i // GPB1, i % GPB1 * VG + v, REC1 - 2:REC1 - 1].bitcast(i32), axis=0)).then_inc(s_fg[i // GPB1], 16)

                    for i in range(RING):
                        group(0, i, True)
                    with pool.Fori(1, ROUNDS1) as t:
                        with pool.If(t < rounds):
                            for i in range(RING):
                                group(t, i, False)

                @block.vector
                def _(dve):
                    rounds = rounds_of(dve, 1)
                    nc.vector.memset(run[:, :, :, :], 0.0).then_inc(s_prep, 1)
                    nc.vector.memset(ones[:, :], 1.0).then_inc(s_prep, 1)
                    nc.vector.memset(onehot[:, :, :, :, :], 0.0).then_inc(s_prep, 1)
                    nc.vector.memset(same[:, 0:1], 0.0).then_inc(s_prep, 1)
                    dve.wait_ge(s_tab, 32)
                    nc.vector.tensor_tensor(same[:, 1:], first_node[:, 1:], first_node[:, :G1.visits - 1], ALU.is_equal).then_inc(s_prep, 1)
                    dve.wait_ge(s_prep, 5)
                    nc.vector.tensor_scalar(first_node[:, :], first_node[:, :], float(G1.width), None, ALU.mult).then_inc(s_prep, 1)
                    dve.wait_ge(s_prep, 6)

                    def onehots(t, h, first=False):
                        k = t * AHEAD + h
                        if not first:
                            dve.wait_ge(s_m, (k - AHEAD + 1) * PAIRS)
                        dve.wait_ge(s_rec[h], (t + 1) * LOADED)
                        rows = rec[:, h, :, :]
                        nc.vector.tensor_tensor(rel[:, h % 2, :], rows[:, :, REC1 - 1].bitcast(i32), first_node[:, bass.ds(k * BATCH1, BATCH1)], ALU.subtract).then_inc(s_dve, 1)
                        dve.wait_ge(s_dve, k * 2 + 1)
                        oh = onehot[:, h, :, 3, :]
                        nc.vector.tensor_tensor(oh, iota[:, 0:32].unsqueeze(1).broadcast_to([P, BATCH1, 32]),
                                                rel[:, h % 2, :].unsqueeze(2).broadcast_to([P, BATCH1, 32]), ALU.is_equal).then_inc(s_dve, 1)
                        dve.wait_ge(s_dve, k * 2 + 2)
                        nc.vector.tensor_tensor(onehot_sh[:, h, :, :, :], oh.unsqueeze(2).broadcast_to([P, BATCH1, 4, 32]),
                                                rows[:, :, 16:20].unsqueeze(3).broadcast_to([P, BATCH1, 4, 32]), ALU.mult).then_inc(s_oh, 1)

                    def message(t, h, g, step, first):
                        i, k = h * GPB1 + g, t * AHEAD + h
                        if step == 0:
                            if g == 0 and not first:
                                dve.wait_ge(s_m, (k - 1) * PAIRS)
                            dve.wait_ge(s_fg[h], (t + 1) * LOADED)
                            dve.wait_ge(s_wt, k * GPB1 + g + 1)
                        w = ps_w[:, g, :, :, :].rearrange("p b v w -> p (b v) w")
                        part, c = step % 2, (0, 64, 128, 160)[step]
                        to = prod[:, h % 2, g * VG:(g + 1) * VG, part, :]
                        if step < 2:
                            nc.vector.tensor_tensor(to[:, :, 0:NS], w[:, :, c:c + NS], fg[:, i, :, 0:NS], ALU.mult)
                        else:
                            last = nc.vector.tensor_tensor(to[:, :, NS:D0].rearrange("p v (i u) -> p v i u", u=NV),
                                                           w[:, :, c:c + NV].unsqueeze(2).broadcast_to([P, VG, 3, NV]),
                                                           fg[:, i, :, NS:D0].rearrange("p v (i u) -> p v i u", u=NV), ALU.mult)
                            if step == 3:
                                last.then_inc(s_msg, 1)

                    def running(k, par, at, first=False):
                        if at == 0 and not first:
                            dve.wait_ge(s_st[par], (k - par) * (STORED // 2))
                        if at % 2 == 0:
                            dve.wait_ge(s_m, k * PAIRS + at // 2 + 1)
                        no = k * BATCH1 + at
                        before = run[:, par, at - 1, :] if at else run[:, 1 - par, BATCH1 - 1, :]
                        if not (first and k == 0 and at == 0):
                            dve.wait_ge(s_run, no)
                        v = at % 2
                        nc.vector.scalar_tensor_tensor(run[:, par, at, :], before, same[:, bass.ds(no, 1)],
                                                       ps_m[:, at // 2 % 2, v * W1_:(v + 1) * W1_], ALU.mult, ALU.add).then_inc(s_run, 1)

                    def batch(t, h, first=0, last=False, begin=False):
                        k = t * AHEAD + h
                        par = h % 2
                        for step in range(4):
                            message(t, h, 0, step, first >= 2)
                            if first < 2:
                                running(k - 2, par, VG + step, first >= 1)
                        for step in range(4):
                            message(t, h, 1, step, first >= 2)
                            if first < 3:
                                running(k - 1, 1 - par, step, first >= 1)
                        if not last:
                            onehots(t + (h + 1) // AHEAD, (h + 1) % AHEAD, begin and h < AHEAD - 1)

                    onehots(0, 0, True)
                    for h in range(AHEAD):
                        batch(0, h, first=max(0, 3 - h), begin=True)
                    with dve.Fori(1, ROUNDS1 - 1) as t:
                        with dve.If(t < rounds - 1):
                            for h in range(AHEAD):
                                batch(t, h)
                        with dve.If(t == rounds - 2):
                            for h in range(AHEAD):
                                batch(t + 1, h, last=(h == AHEAD - 1))
                            for at in range(VG, BATCH1):
                                running(t * AHEAD + 2 * AHEAD - 2, 0, at)
                            for at in range(BATCH1):
                                running(t * AHEAD + 2 * AHEAD - 1, 1, at)

                @block.scalar
                def _(act):
                    rounds = rounds_of(act, 1)
                    def copy_scalars(t, h, first=False):
                        act.wait_ge(s_rec[h], (t + 1) * LOADED)
                        if not first:
                            act.wait_ge(s_t, t * AHEAD + h)
                        nc.scalar.copy(scal[:, :, :], rec[:, h, :, 0:16]).then_inc(s_scal, 1)

                    def copy_transposed(k, first=False):
                        if not first:
                            act.wait_ge(s_h, k)
                        act.wait_ge(s_t, k + 1)
                        nc.scalar.copy(scal_t[:, :], ps_t[:, 0:P]).then_inc(s_scal_t, 1)

                    def silu(k, par, first=False):
                        if not first:
                            act.wait_ge(s_wt, (k - 1) * GPB1)
                        act.wait_ge(s_h, k + 1)
                        nc.scalar.activation(hidden[:, par, :, :], ps_h[:, :, :], ACT.Silu, scale=0.25).then_inc(s_hid, 1)

                    def store(k, par):
                        act.wait_ge(s_run, (k + 1) * BATCH1)
                        for g in range(GPB1):
                            act.dma_start(sums_tab[bass.ds(k * BATCH1 + g * VG, VG), :, :].rearrange("v p w -> p v w"),
                                          run[:, par, g * VG:(g + 1) * VG, :]).then_inc(s_st[par], 16)

                    act.wait_ge(s_tab, 32)
                    for h in range(AHEAD):
                        load_records(act, ACT_VISITS, 0, h, True)
                    for h in range(AHEAD):
                        copy_scalars(0, h, h == 0)
                        if h:
                            silu(h - 1, (h - 1) % 2, h < 3)
                        copy_transposed(h, h == 0)
                    load_records(act, ACT_VISITS, 1, 0, False)

                    def batch(t, h, last=False):
                        k = t * AHEAD + h
                        copy_scalars(t, h)
                        silu(k - 1, (h + 1) % 2)
                        copy_transposed(k)
                        store(k - AHEAD, h % 2)
                        if not last:
                            load_records(act, ACT_VISITS, t + (h + 1) // AHEAD, (h + 1) % AHEAD, False)

                    with act.Fori(1, ROUNDS1 - 1) as t:
                        with act.If(t < rounds - 1):
                            for h in range(AHEAD):
                                batch(t, h)
                        with act.If(t == rounds - 2):
                            for h in range(AHEAD):
                                batch(t + 1, h, h == AHEAD - 1)
                            silu(t * AHEAD + 2 * AHEAD - 1, 1)
                            for h in range(AHEAD):
                                store((t + 1) * AHEAD + h, h % 2)
                            for par in range(2):
                                act.wait_ge(s_st[par], (t + 2) * (STORED * AHEAD // 2))
                            act.sem_inc(s_begun, 1)

                @block.tensor
                def _(pe):
                    rounds = rounds_of(pe, 1)
                    pe.wait_ge(s_w, 160)
                    pe.wait_ge(s_prep, 6)

                    def transposed(k, first=False):
                        pe.wait_ge(s_scal, k + 1)
                        if not first:
                            pe.wait_ge(s_scal_t, k)
                        nc.tensor.transpose(ps_t[:, 0:P], scal[:, :, :].rearrange("p v a -> p (v a)"), ident[:, :]).then_inc(s_t, 1)

                    def hidden_layer(k, first=False):
                        if not first:
                            pe.wait_ge(s_hid, k)
                        pe.wait_ge(s_scal_t, k + 1)
                        for j in range(PAIRS):
                            last = nc.tensor.matmul(ps_h[:, j, :], wfc1[:, j, :], scal_t[:, :], start=(j == 0), stop=(j == PAIRS - 1))
                        last.then_inc(s_h, 1)

                    def edge_weights(k, par, g, first=False):
                        if g == 0:
                            pe.wait_ge(s_hid, k + 1)
                        if not first:
                            pe.wait_ge(s_msg, (k - 1) * GPB1 + g + 1)
                        for b in range(2):
                            last = nc.tensor.matmul(ps_w[:, g, b, :, 0:192], hidden[:, par, 2 * g + b, :], wfc2[:, :, :], start=True, stop=True)
                        last.then_inc(s_wt, 1)

                    def node_sums(k, h, j, first=False):
                        par = h % 2
                        if j == 0:
                            pe.wait_ge(s_oh, k + 1)
                        if j % 2 == 0:
                            pe.wait_ge(s_msg, k * GPB1 + j // 2 + 1)
                        if not first or j >= 2:
                            pe.wait_ge(s_run, (k * PAIRS + j - 1) * 2)
                        bank = ps_m[:, j % 2, :]
                        for v in range(2):
                            at = 2 * j + v
                            oh_sh = onehot_sh[:, h, at, :, :].rearrange("p c m -> p (c m)")
                            nc.tensor.matmul(bank[0:96, v * W1_:v * W1_ + D0], oh_sh[:, 0:96], prod[:, par, at, 1, :], start=(v == 0), stop=False)
                            nc.tensor.matmul(bank[96:128, v * W1_:v * W1_ + D0], oh_sh[:, 96:128], prod[:, par, at, 0, :], start=(v == 0), stop=False, tile_position=(0, 96))
                            last = nc.tensor.matmul(bank[:, v * W1_ + D0:(v + 1) * W1_], onehot[:, h, at, :, :].rearrange("p c m -> p (c m)"), ones[:, :],
                                                    start=False, stop=(v == 1))
                        last.then_inc(s_m, 1)

                    def batch(t, h, first=0, last=0):
                        k, before = t * AHEAD + h, (h - 1) % AHEAD
                        edge_weights(k, h % 2, 0, first == 2)
                        edge_weights(k, h % 2, 1, first == 2)
                        if first < 2:
                            node_sums(k - 1, before, 0, first == 1)
                            node_sums(k - 1, before, 1, first == 1)
                        if last < 2:
                            hidden_layer(k + 1)
                        if last < 1:
                            transposed(k + 2)
                        if first < 2:
                            node_sums(k - 1, before, 2)
                            node_sums(k - 1, before, 3)

                    transposed(0, True)
                    hidden_layer(0, True)
                    transposed(1)
                    for h in range(AHEAD):
                        batch(0, h, first=max(0, 2 - h))
                    with pe.Fori(1, ROUNDS1 - 1) as t:
                        with pe.If(t < rounds - 1):
                            for h in range(AHEAD):
                                batch(t, h)
                        with pe.If(t == rounds - 2):
                            for h in range(AHEAD):
                                batch(t + 1, h, last=max(0, h - 1))
                            for j in range(PAIRS):
                                node_sums(t * AHEAD + 2 * AHEAD - 1, AHEAD - 1, j)

        with ExitStack() as ctx:
            sb, ps, sem = sb_in(ctx, "f_"), ps_in(ctx, "f_"), sem_in(ctx, "f_")
            CX, CY, CZ, C0, CB0, CBZ = range(6)
            OUT = D0 + 2
            BUCKETS = NODE_TILES * P // G1.width
            wl2 = sb("wl2", [P, 6, OUT])
            first_visit = sb("first_visit", [1, BUCKETS + 1])
            last_visit = sb("last_visit", [1, BUCKETS])
            last_i = sb("last_i", [1, BUCKETS], i32)
            factor2 = sb("factor2", [P, 6])
            AHEAD = 4
            cur = sb("cur", [P, AHEAD, 4, W1_])
            ta = sb("ta", [P, 2, 4, 4, 32])
            tb = sb("tb", [P, 2, 4, 4, 32])
            base = sb("base", [P, 2, D0])
            count = sb("count", [P, 2, 4])
            y = sb("y", [P, 2, D0])
            stats = sb("stats", [P, 2, 6])
            mean_var = sb("mean_var", [P, 2, 2])
            std = sb("std", [P, 2, 1])
            rstd = sb("rstd", [P, 2, 1])
            x2 = sb("x2", [P, 2, D0])
            ps_ta = [ps(f"ps_ta{r}", [P, 512]) for r in range(2)]
            ps_tb = [ps(f"ps_tb{r}", [P, 512]) for r in range(2)]
            ps_o = [ps(f"ps_o{r}", [P, 512]) for r in range(2)]
            WEIGHTS = 16 * 16
            s_zero, s_scaled, s_first, s_t, s_ta, s_o = (sem(n) for n in ("zero", "scaled", "first", "t", "ta", "o"))
            s_cur = [[sem(f"cur{h}_{r}") for r in range(AHEAD)] for h in range(2)]
            s_last = sem("last")
            s_y, s_bn, s_var, s_std, s_rstd, s_x2 = (sem(n) for n in ("y", "bn", "var", "std", "rstd", "x2"))
            s_gate = sem("gate")
            s_base = [sem(f"base{r}") for r in range(2)]
            s_out = [sem(f"out{r}") for r in range(2)]
            s_w = sem("w")
            MORE = P - NV - 1

            def load_sums(engine, half):
                def load(t, h, first):
                    i = t * AHEAD + h
                    if not first:
                        engine.wait_ge(s_t, i - AHEAD + 1)
                    engine.wait_ge(s_last, 2)
                    for b in (2 * half, 2 * half + 1):
                        row = engine.value_load(last_i[0:1, bass.ds(i * 4 + b, 1)], min_val=0, max_val=G1.visits - 1)
                        engine.dma_start(cur[:, h, b, :], sums_tab[bass.ds(row, 1), :, :].rearrange("o p w -> p (o w)")).then_inc(s_cur[half][h], 16)

                for h in range(AHEAD):
                    load(0, h, True)
                with engine.Fori(1, NODE_TILES // AHEAD) as t:
                    for h in range(AHEAD):
                        load(t, h, False)
                for h in range(NODE_TILES % AHEAD):
                    load(NODE_TILES // AHEAD, h, False)

            with nc.Block() as block:
                @block.sync
                def _(sp):
                    sp.dma_start(first_visit[:, :], scratch["tables1"]["vb"][0:BUCKETS + 1].rearrange("(o b) -> o b", o=1)).then_inc(s_first, 16)
                    sp.wait_ge(s_zero, 1)
                    S_, V_, A_ = A["Wl2_s"], A["Wl2_v"], A["Wa"]
                    al = D0
                    pieces = [(wl2[0:64, C0, 0:64], S_[0:64, :]), (wl2[0:64, C0, al:al + 1], A_[0:64, :]),
                              (wl2[64:96, C0, 64:96], V_[64:96, :]), (wl2[96:128, C0, 96:128], V_[64:96, :]),
                              (wl2[0:64, CX, 64:96], V_[0:64, :]), (wl2[64:96, CX, 0:64], S_[64:96, :]), (wl2[64:96, CX, al:al + 1], A_[64:96, :]),
                              (wl2[0:64, CY, 96:128], V_[0:64, :]), (wl2[96:128, CY, 0:64], S_[64:96, :]), (wl2[96:128, CY, al:al + 1], A_[64:96, :]),
                              (wl2[0:64, CZ, 128:160], V_[0:64, :]),
                              (wl2[MORE:MORE + NV, CB0, 128:160], V_[64:96, :]), (wl2[P - 1:P, CB0, al + 1:al + 2], A["ident"][0:1, 0:1]),
                              (wl2[MORE:MORE + NV, CBZ, 0:64], S_[64:96, :]), (wl2[MORE:MORE + NV, CBZ, al:al + 1], A_[64:96, :]),
                              (factor2[:, :], A["factor2"])]
                    for tile, dram in pieces:
                        sp.dma_start(tile, dram).then_inc(s_w, 16)

                    load_sums(sp, 0)

                @block.gpsimd
                def _(pool):
                    nc.gpsimd.memset(wl2[:, :, :], 0.0).then_inc(s_zero, 1)

                    load_sums(pool, 1)

                @block.vector
                def _(dve):
                    dve.wait_ge(s_first, 16)
                    nc.vector.tensor_scalar(last_visit[:, :], first_visit[:, 1:], first_visit[:, G1.buckets:G1.buckets + 1], -1.0, ALU.min, ALU.add).then_inc(s_last, 1)
                    dve.wait_ge(s_last, 1)
                    nc.vector.tensor_copy(last_i[:, :], last_visit[:, :]).then_inc(s_last, 1)
                    dve.wait_ge(s_w, WEIGHTS)
                    nc.vector.tensor_tensor(wl2[:, :, :], wl2[:, :, :], factor2[:, :].unsqueeze(2).broadcast_to([P, 6, OUT]), ALU.mult).then_inc(s_scaled, 1)

                    def finish(t, r, first):
                        i = t * 2 + r
                        dve.wait_ge(s_o, i + 1)
                        c = count[:, r, :]
                        nc.vector.tensor_scalar(c[:, 0:1], ps_o[r][:, D0 + 1:D0 + 2], 1.0, None, ALU.max).then_inc(s_gate, 1)
                        dve.wait_ge(s_gate, i * 4 + 1)
                        nc.vector.reciprocal(c[:, 1:2], c[:, 0:1]).then_inc(s_gate, 1)
                        dve.wait_ge(s_gate, i * 4 + 2)
                        nc.vector.tensor_scalar(c[:, 2:3], c[:, 1:2], vec[:, bass.ds(i, 1)], None, ALU.mult).then_inc(s_gate, 1)
                        dve.wait_ge(s_gate, i * 4 + 3)
                        nc.vector.tensor_scalar(c[:, 3:4], ps_o[r][:, D0:D0 + 1], c[:, 2:3], c[:, 2:3], ALU.mult, ALU.mult).then_inc(s_gate, 1)
                        dve.wait_ge(s_gate, i * 4 + 4)
                        dve.wait_ge(s_base[r], (t + 1) * 16)
                        nc.vector.scalar_tensor_tensor(y[:, r, :], ps_o[r][:, 0:D0], c[:, 3:4], base[:, r, :], ALU.mult, ALU.add).then_inc(s_y, 1)
                        dve.wait_ge(s_y, i + 1)
                        nc.vector.bn_stats(stats[:, r, :], y[:, r, :]).then_inc(s_bn, 1)
                        dve.wait_ge(s_w, WEIGHTS)
                        dve.wait_ge(s_bn, i + 1)
                        nc.vector.bn_aggr(mean_var[:, r, :], stats[:, r, :]).then_inc(s_var, 1)

                    def normalise(t, r, first):
                        j = t * 2 + r
                        dve.wait_ge(s_std, j + 1)
                        nc.vector.reciprocal(rstd[:, r, :], std[:, r, :]).then_inc(s_rstd, 1)
                        if not first:
                            dve.wait_ge(s_out[r], t * 16)
                        dve.wait_ge(s_rstd, j + 1)
                        nc.vector.tensor_scalar(x2[:, r, :], y[:, r, :], mean_var[:, r, 0:1], rstd[:, r, :], ALU.subtract, ALU.mult).then_inc(s_x2, 1)

                    finish(0, 0, True)
                    finish(0, 1, True)
                    normalise(0, 0, True)
                    finish(1, 0, False)
                    normalise(0, 1, True)
                    finish(1, 1, False)
                    with dve.Fori(2, NODE_TILES // 2) as t:
                        for r in range(2):
                            normalise(t - 1, r, False)
                            finish(t, r, False)
                    for r in range(2):
                        normalise(NODE_TILES // 2 - 1, r, False)

                @block.scalar
                def _(act):
                    def features(i, r, first):
                        if not first:
                            act.wait_ge(s_o, i - 1)
                        act.wait_ge(s_t, i + 1)
                        for dst_t, src_t in ((ta, ps_ta), (tb, ps_tb)):
                            nc.scalar.copy(dst_t[:, r, :, :, :], src_t[r][:, :].rearrange("p (q c n) -> p c q n", q=4, c=4)).then_inc(s_ta, 1)

                    def deviation(j, r):
                        act.wait_ge(s_var, j + 1)
                        nc.scalar.activation(std[:, r, :], mean_var[:, r, 1:2], ACT.Sqrt, bias=eps[:, :]).then_inc(s_std, 1)

                    def load_base(i, r, first=False):
                        if not first:
                            act.wait_ge(s_y, i - 1)
                        act.dma_start(base[:, r, :], base_tab[bass.ds(i * P, P), :]).then_inc(s_base[r], 16)

                    def store(i, r):
                        act.wait_ge(s_x2, i + 1)
                        act.dma_start(out[bass.ds(i * P, P), :], x2[:, r, :]).then_inc(s_out[r], 16)

                    for r in range(2):
                        load_base(r, r, True)
                    features(0, 0, True)
                    features(1, 1, True)
                    deviation(0, 0)
                    with act.Fori(1, NODE_TILES // 2) as t:
                        load_base(t * 2, 0)
                        features(t * 2, 0, False)
                        deviation(t * 2 - 1, 1)
                        store(t * 2 - 2, 0)
                        load_base(t * 2 + 1, 1)
                        features(t * 2 + 1, 1, False)
                        deviation(t * 2, 0)
                        store(t * 2 - 1, 1)
                    deviation(NODE_TILES - 1, 1)
                    for r in range(2):
                        store(NODE_TILES - 2 + r, r)
                    for r in range(2):
                        act.wait_ge(s_out[r], 16 * (NODE_TILES // 2))

                @block.tensor
                def _(pe):
                    pe.wait_ge(s_scaled, 1)

                    def transposes(t, h, first=False):
                        i, r = t * AHEAD + h, h % 2
                        if not first:
                            pe.wait_ge(s_ta, i * 2 - 2)
                        for half in range(2):
                            pe.wait_ge(s_cur[half][h], (t + 1) * 32)
                        for q in range(4):
                            nc.tensor.transpose(ps_ta[r][:, q * P:(q + 1) * P], cur[:, h, q, 0:P], ident[:, :])
                            last = nc.tensor.transpose(ps_tb[r][:, q * P:(q + 1) * P], cur[:, h, q, W1_ - P:W1_], ident[:, :])
                        last.then_inc(s_t, 1)

                    def products(i, r, first):
                        if not first:
                            pe.wait_ge(s_y, i - 1)
                        pe.wait_ge(s_ta, i * 2 + 2)
                        for c in range(4):
                            nc.tensor.matmul(ps_o[r][:, 0:OUT], ta[:, r, c, :, :].rearrange("p q n -> p (q n)"), wl2[:, c, :], start=(c == 0), stop=False)
                        nc.tensor.matmul(ps_o[r][:, 0:OUT], tb[:, r, C0, :, :].rearrange("p q n -> p (q n)"), wl2[:, CB0, :], start=False, stop=False)
                        nc.tensor.matmul(ps_o[r][:, 0:OUT], tb[:, r, CZ, :, :].rearrange("p q n -> p (q n)"), wl2[:, CBZ, :], start=False, stop=True).then_inc(s_o, 1)

                    for h in range(2):
                        transposes(0, h, True)
                    for h in range(2):
                        products(h, h, True)
                        transposes(0, 2 + h)
                    with pe.Fori(1, NODE_TILES // AHEAD) as t:
                        for h in range(AHEAD):
                            products(t * AHEAD + h - 2, h % 2, False)
                            transposes(t, h)
                    for h in range(NODE_TILES % AHEAD):
                        products(NODE_TILES - 4 + h, h, False)
                        transposes(NODE_TILES // AHEAD, h)
                    for r in range(2):
                        products(NODE_TILES - 2 + r, r, False)



def _vectors_by_component(n):
    import numpy as np
    return np.concatenate([np.arange(64), 64 + 3 * np.arange(n)[None, :].repeat(3, 0).reshape(3, n).ravel() + np.repeat(np.arange(3), n)])


def kernel(**inputs):
    import numpy as np
    import concourse.bacc as bacc
    from concourse import mybir as my
    from concourse.bass_utils import run_bass_kernel_spmd

    G0, G1 = Grouping("src", 2, True), Grouping("dst", 5, False)
    a = {k: np.asarray(v) for k, v in inputs.items()}
    cols = _vectors_by_component(32)

    def pad(v, rows, value=0):
        return np.concatenate([v, np.full((rows - v.shape[0],) + v.shape[1:], value, v.dtype)])

    x = np.ascontiguousarray(pad(a["x"][:, cols], NODE_ROWS))
    z_cols, x_cols, y_cols = (8 + 3 * np.arange(8) + c for c in (2, 0, 1))
    edge_cols = np.concatenate([z_cols, np.arange(8), x_cols, y_cols])
    Wu = a["L0_gnn_Wu"]
    arrays = {
        "src": pad(a["src"], SLOTS, PAD_NODE).reshape(P, TILES),
        "dst": pad(a["dst"], SLOTS, PAD_NODE).reshape(P, TILES),
        "next_dst": pad(a["dst"], SLOTS + 1, PAD_NODE)[1:].reshape(P, TILES),
        "edge_attr_32": pad(a["edge_attr_32"][:, edge_cols], SLOTS).reshape(P, TILES, 32),
        "edge_attr_16": pad(a["edge_attr_16"], SLOTS).reshape(P, TILES, 16),
        "edge_attr_4": pad(a["edge_attr_4"][:, [1, 2, 3, 0]], SLOTS).reshape(P, TILES, 4),
        "x": x,
        "xT": np.ascontiguousarray(x.T),
        "node_vec1": np.ascontiguousarray(pad(a["node_vec1"][:, 0], NODE_ROWS).reshape(NODE_TILES, P).T),
        "WmT": np.ascontiguousarray(np.concatenate([a["L0_gnn_Wm"][cols[np.r_[64:96, 0:64, 96:160]]], a["L0_gnn_bm"][None]]).T),
        "Wu": np.ascontiguousarray(np.concatenate([Wu[:160][cols], Wu[160:]])[:, cols]),
        "bu": a["L0_gnn_bu"][cols],
        **{n: a["L0_gnn_" + n] for n in ("W1", "W2", "W3", "W4")},
        **{n: a["L1_gnn_" + n] for n in ("Wfc1", "Wfc2", "Wsc0", "Wsc1", "Wl1_0", "Wl1_1", "Wl2_s", "Wl2_v", "Wa")},
    }
    arrays.update(rank_constants([G0, G1]))
    k = np.arange(P)
    half = 2.0 ** -0.5
    f0 = np.zeros((P, 4))
    f0[:, 0] = np.where(k < 64, 512 ** -0.5, 256 ** -0.5) * half
    f0[:, 1] = np.where(k < 64, 512 ** -0.5, 768 ** -0.5) * half
    f0[:, 2] = 512 ** -0.5 * half
    f0[:, 3] = np.where(k < 64, 768 ** -0.5, 256 ** -0.5) * half
    arrays["factor0"] = f0.astype(np.float32)
    arrays["spread0"] = ((k[:, None] // 8 == np.arange(16)).astype(np.float32) - (np.arange(16) == 0)).astype(np.float32)
    arrays["in_bucket0"] = (k % 8).astype(np.float32).reshape(P, 1)
    arrays["factor1"] = np.stack([np.where(k < 64, 64 ** -0.5, 32 ** -0.5), np.full(P, 32 ** -0.5)], 1).astype(np.float32)
    f2 = np.full((P, 6), 96 ** -0.5 / 8)
    f2[64:, 0] *= 3 ** -0.5
    f2[64:, 1] *= 3 ** -0.5
    f2[:, 5] *= 3 ** -0.5
    f2[P - 1, 4] = 1.0
    arrays["factor2"] = f2.astype(np.float32)

    nc = bacc.Bacc("TRN2", target_bir_lowering=False, num_devices=1)
    f32, int32 = my.dt.float32, my.dt.int32
    A, given = {"groupings": (G0, G1)}, {}
    for n, v in arrays.items():
        v = np.ascontiguousarray(v)
        given["in_" + n] = v
        A[n] = nc.dram_tensor("in_" + n, v.shape, my.dt.from_np(v.dtype), kind="ExternalInput").ap()

    def scratch(n, shape, dt=f32):
        return nc.dram_tensor(n, shape, dt, kind="Internal").ap()

    def tables(g):
        return {"vb": scratch(f"{g.name}_vb", (HI * LO,)), "s": scratch(f"{g.name}_s", (HI * LO,)),
                "bucket": scratch(f"{g.name}_bucket", (P * g.cols,)), "start": scratch(f"{g.name}_start", (P * g.cols,), int32)}

    S = {"rec0": scratch("rec0", (SLOTS, 34)), "rec1": scratch("rec1", (SLOTS, 22)), "f": scratch("f", (NODE_ROWS, 160)),
         "base": scratch("base", (NODE_ROWS, 160)), "sums": scratch("sums", (G1.visits, P, 161)), "tables0": tables(G0), "tables1": tables(G1)}
    out = nc.dram_tensor("out", (NODE_ROWS, 160), f32, kind="ExternalOutput").ap()
    gnn_kernel(nc, A, out, S)
    r = run_bass_kernel_spmd(nc, [given], core_ids=[0])
    got = r.results[0]["out"]
    back = np.empty(160, np.int64)
    back[cols] = np.arange(160)
    return np.ascontiguousarray(got[:N_NODES][:, back])
```
